# Optimizing a Trainium2 kernel written in Bass

```python
import numpy as np
import jax
import jax.numpy as jnp

def _softmax(x, axis=-1):
    return jax.nn.softmax(x, axis=axis)

def _gelu(x):
    return jax.nn.gelu(x, approximate=True)

def _silu(x):
    return jax.nn.silu(x)

def _sigmoid(x):
    return jax.nn.sigmoid(x)

def _layernorm(x, axis=-1, eps=1e-05):
    m = jnp.mean(x, axis=axis, keepdims=True)
    v = jnp.var(x, axis=axis, keepdims=True)
    return (x - m) / jnp.sqrt(v + eps)

def _scatter_add(tgt, idx, src, axis=0):
    return tgt.at[idx].add(src)

def _segment_sum(src, seg, n):
    return jax.ops.segment_sum(src, seg, n)
kernel_name = 'mk_lm_tower_d1_tok_ids512_r4_c87c1f'

def setup_inputs(seed: int=0):
    np.random.seed(seed)
    _w = jnp.asarray

    def _rec_inputs():
        import jax
        import jax.numpy as jnp
        _rk = jax.random.key(seed)
        x = jax.random.randint(jax.random.fold_in(_rk, 1), (2, 2048), 0, 50257, jnp.int32)
        return x
    x = _rec_inputs()

    def _L0_tok_setup():
        import jax, jax.numpy as jnp
        import numpy as np
        D_MODEL = 128
        VOCAB = 50257
        BATCH = 8
        SEQ = 512

        def _positional_encoding(seq_len, d_model, dtype):
            pos = jnp.arange(1, seq_len + 1, dtype=jnp.float32)[:, None]
            i = jnp.arange(d_model)
            exponent = jnp.where(i % 2 == 0, i, i + 1).astype(jnp.float32) / d_model
            angle = pos / 10000.0 ** exponent
            pe = jnp.where(i % 2 == 0, jnp.cos(angle), jnp.sin(angle))
            return pe.astype(dtype)
        key = jax.random.key(seed)
        k1, k2, k3 = jax.random.split(key, 3)
        x = jax.random.randint(k1, (BATCH, SEQ), 0, VOCAB)
        W = jax.random.normal(k2, (D_MODEL, VOCAB), dtype=jnp.float32) * 0.02
        b = jax.random.normal(k3, (D_MODEL,), dtype=jnp.float32) * 0.02
        return {'x': x, 'W': W, 'b': b}
    _L0_tok_all = _L0_tok_setup()
    _L0_tok_in = {k: v for k, v in _L0_tok_all.items() if k in ('W', 'b')}
    del _L0_tok_all

    def _L0_attn_setup():
        import jax, jax.numpy as jnp
        import numpy as np
        EPS = 1e-08

        def _cum_mean(t):
            n = t.shape[-1]
            denom = jnp.arange(1, n + 1, dtype=t.dtype)
            return jnp.cumsum(t, axis=-1) / denom
        key = jax.random.key(seed)
        ks = jax.random.split(key, 4)
        b, n, dim, h = (2, 512, 128, 8)
        x = jax.random.normal(ks[0], (b, n, dim), dtype=jnp.float32)
        w_qkv = jax.random.normal(ks[1], (dim, 3 * dim), dtype=jnp.float32) * dim ** (-0.5)
        w_out = jax.random.normal(ks[2], (dim, dim), dtype=jnp.float32) * dim ** (-0.5)
        b_out = jnp.zeros((dim,), dtype=jnp.float32)
        norm_g = jnp.ones((1, h, 1, 1), dtype=jnp.float32)
        norm_b = jnp.zeros((1, h, 1, 1), dtype=jnp.float32)
        return {'x': x, 'w_qkv': w_qkv, 'w_out': w_out, 'b_out': b_out, 'norm_g': norm_g, 'norm_b': norm_b}
    _L0_attn_all = _L0_attn_setup()
    _L0_attn_in = {k: v for k, v in _L0_attn_all.items() if k in ('w_qkv', 'w_out', 'b_out', 'norm_g', 'norm_b')}
    del _L0_attn_all

    def _L0_ffn_setup():
        import jax, jax.numpy as jnp
        import numpy as np
        B, N, DIM = (1, 512, 128)
        DH, H = (64, 8)
        E, FF = (8, 512)

        def _layernorm(x, g, b, eps=1e-05):
            mu = jnp.mean(x, axis=-1, keepdims=True)
            var = jnp.mean(jnp.square(x - mu), axis=-1, keepdims=True)
            return (x - mu) * jax.lax.rsqrt(var + eps) * g + b

        def _l2norm(x, eps=1e-12):
            return x / jnp.sqrt(jnp.sum(jnp.square(x), axis=-1, keepdims=True) + eps)
        key = jax.random.key(seed)
        ks = jax.random.split(key, 12)
        g = lambda k, shape: jax.random.normal(k, shape, jnp.float32) * 0.02
        return {'x': jax.random.normal(ks[0], (B, N, DIM), jnp.float32), 'ln_g': jnp.ones((DIM,), jnp.float32), 'ln_b': jnp.zeros((DIM,), jnp.float32), 'Wq': g(ks[1], (DIM, DIM)), 'Wk': g(ks[2], (DIM, DIM)), 'Wv': g(ks[3], (DIM, DIM)), 'Wo': g(ks[4], (DIM, DIM)), 'qn_g': jnp.ones((DH,), jnp.float32), 'kn_g': jnp.ones((DH,), jnp.float32), 'gate_W': g(ks[5], (DIM, E)), 'gate_b': jnp.zeros((E,), jnp.float32), 'W1': g(ks[6], (E, DIM, FF)), 'b1': jnp.zeros((E, FF), jnp.float32), 'W2': g(ks[7], (E, FF, DIM)), 'b2': jnp.zeros((E, DIM), jnp.float32)}
    _L0_ffn_all = _L0_ffn_setup()
    _L0_ffn_in = {k: v for k, v in _L0_ffn_all.items() if k in ('ln_g', 'ln_b', 'Wq', 'Wk', 'Wv', 'Wo', 'qn_g', 'kn_g', 'gate_W', 'gate_b', 'W1', 'b1', 'W2', 'b2')}
    del _L0_ffn_all
    return {'x': x, 'L0_tok_W': _L0_tok_in['W'], 'L0_tok_b': _L0_tok_in['b'], 'L0_attn_w_qkv': _L0_attn_in['w_qkv'], 'L0_attn_w_out': _L0_attn_in['w_out'], 'L0_attn_b_out': _L0_attn_in['b_out'], 'L0_attn_norm_g': _L0_attn_in['norm_g'], 'L0_attn_norm_b': _L0_attn_in['norm_b'], 'L0_ffn_ln_g': _L0_ffn_in['ln_g'], 'L0_ffn_ln_b': _L0_ffn_in['ln_b'], 'L0_ffn_Wq': _L0_ffn_in['Wq'], 'L0_ffn_Wk': _L0_ffn_in['Wk'], 'L0_ffn_Wv': _L0_ffn_in['Wv'], 'L0_ffn_Wo': _L0_ffn_in['Wo'], 'L0_ffn_qn_g': _L0_ffn_in['qn_g'], 'L0_ffn_kn_g': _L0_ffn_in['kn_g'], 'L0_ffn_gate_W': _L0_ffn_in['gate_W'], 'L0_ffn_gate_b': _L0_ffn_in['gate_b'], 'L0_ffn_W1': _L0_ffn_in['W1'], 'L0_ffn_b1': _L0_ffn_in['b1'], 'L0_ffn_W2': _L0_ffn_in['W2'], 'L0_ffn_b2': _L0_ffn_in['b2']}

def reference(x, L0_tok_W, L0_tok_b, L0_attn_w_qkv, L0_attn_w_out, L0_attn_b_out, L0_attn_norm_g, L0_attn_norm_b, L0_ffn_ln_g, L0_ffn_ln_b, L0_ffn_Wq, L0_ffn_Wk, L0_ffn_Wv, L0_ffn_Wo, L0_ffn_qn_g, L0_ffn_kn_g, L0_ffn_gate_W, L0_ffn_gate_b, L0_ffn_W1, L0_ffn_b1, L0_ffn_W2, L0_ffn_b2):
    import jax
    import jax.numpy as jnp

    def _L0_tok_ref(x, W, b):
        import jax, jax.numpy as jnp
        import numpy as np
        D_MODEL = 128
        VOCAB = 50257
        BATCH = 8
        SEQ = 512

        def _positional_encoding(seq_len, d_model, dtype):
            pos = jnp.arange(1, seq_len + 1, dtype=jnp.float32)[:, None]
            i = jnp.arange(d_model)
            exponent = jnp.where(i % 2 == 0, i, i + 1).astype(jnp.float32) / d_model
            angle = pos / 10000.0 ** exponent
            pe = jnp.where(i % 2 == 0, jnp.cos(angle), jnp.sin(angle))
            return pe.astype(dtype)
        emb = jnp.take(W.T, x, axis=0) + b
        pe = _positional_encoding(x.shape[1], W.shape[0], emb.dtype)
        return emb + pe[None, :, :]

    def _L0_attn_ref(x, w_qkv, w_out, b_out, norm_g, norm_b):
        import jax, jax.numpy as jnp
        import numpy as np
        EPS = 1e-08

        def _cum_mean(t):
            n = t.shape[-1]
            denom = jnp.arange(1, n + 1, dtype=t.dtype)
            return jnp.cumsum(t, axis=-1) / denom
        b, n, dim = x.shape
        h = norm_g.shape[1]
        d = dim // h
        scale = dim ** (-0.5)
        qkv = (x @ w_qkv).reshape(b, n, 3, h, d).transpose(2, 0, 3, 1, 4)
        q, k, v = (qkv[0], qkv[1], qkv[2])
        dots = jnp.einsum('bhid,bhjd->bhij', q, k) * scale
        causal_mask = jnp.triu(jnp.ones((n, n), dtype=bool), k=1)
        dots = jnp.where(causal_mask, 0.0, dots)
        mu = jnp.diagonal(_cum_mean(dots), axis1=-2, axis2=-1)[..., None]
        t = dots - mu
        s = jnp.diagonal(_cum_mean(t * t), axis1=-2, axis2=-1)[..., None]
        normed = t * jax.lax.rsqrt(s + EPS)
        attn = normed * norm_g + norm_b
        attn = jnp.where(causal_mask, 0.0, attn)
        out = jnp.einsum('bhij,bhjd->bhid', attn, v)
        out = out.transpose(0, 2, 1, 3).reshape(b, n, dim)
        return out @ w_out + b_out

    def _L0_ffn_ref(x, ln_g, ln_b, Wq, Wk, Wv, Wo, qn_g, kn_g, gate_W, gate_b, W1, b1, W2, b2):
        import jax, jax.numpy as jnp
        import numpy as np
        B, N, DIM = (1, 512, 128)
        DH, H = (64, 8)
        E, FF = (8, 512)

        def _layernorm(x, g, b, eps=1e-05):
            mu = jnp.mean(x, axis=-1, keepdims=True)
            var = jnp.mean(jnp.square(x - mu), axis=-1, keepdims=True)
            return (x - mu) * jax.lax.rsqrt(var + eps) * g + b

        def _l2norm(x, eps=1e-12):
            return x / jnp.sqrt(jnp.sum(jnp.square(x), axis=-1, keepdims=True) + eps)
        b, n, d = x.shape
        dh = qn_g.shape[0]
        h = d // dh
        hx = _layernorm(x, ln_g, ln_b)
        q = (hx @ Wq).reshape(b, n, h, dh).transpose(0, 2, 1, 3)
        k = (hx @ Wk).reshape(b, n, h, dh).transpose(0, 2, 1, 3)
        v = (hx @ Wv).reshape(b, n, h, dh).transpose(0, 2, 1, 3)
        scale = jnp.sqrt(jnp.float32(dh))
        q = _l2norm(q) * scale * qn_g
        k = _l2norm(k) * scale * kn_g
        scores = jnp.einsum('bhqd,bhkd->bhqk', q, k) * dh ** (-0.5)
        causal = jnp.tril(jnp.ones((n, n), bool))
        scores = jnp.where(causal, scores, jnp.finfo(scores.dtype).min)
        attn = jax.nn.softmax(scores, axis=-1)
        o = jnp.einsum('bhqk,bhkd->bhqd', attn, v)
        y = o.transpose(0, 2, 1, 3).reshape(b, n, d) @ Wo
        gate = jax.nn.softmax(y @ gate_W + gate_b, axis=-1)
        hid = jax.nn.gelu(jnp.einsum('bnd,edf->bnef', y, W1) + b1)
        eo = jnp.einsum('bnef,efd->bned', hid, W2) + b2
        out = jnp.einsum('bned,bne->bnd', eo, gate)
        return out
    h = _L0_tok_ref(x, L0_tok_W, L0_tok_b)
    h = h + _L0_attn_ref(_layernorm(h, axis=-1), L0_attn_w_qkv, L0_attn_w_out, L0_attn_b_out, L0_attn_norm_g, L0_attn_norm_b)
    h = h + _L0_ffn_ref(_layernorm(h, axis=-1), L0_ffn_ln_g, L0_ffn_ln_b, L0_ffn_Wq, L0_ffn_Wk, L0_ffn_Wv, L0_ffn_Wo, L0_ffn_qn_g, L0_ffn_kn_g, L0_ffn_gate_W, L0_ffn_gate_b, L0_ffn_W1, L0_ffn_b1, L0_ffn_W2, L0_ffn_b2)
    return h

_drawn_inputs = setup_inputs


def setup_inputs(seed=0):
    import zlib

    import numpy as np

    out = dict(_drawn_inputs(seed))
    spreads = {'L0_attn_b_out': (0.0, 2.0),
     'L0_attn_norm_g': (1.0, 0.2),
     'L0_attn_norm_b': (0.0, 0.1),
     'L0_ffn_ln_g': (1.0, 0.6),
     'L0_ffn_ln_b': (0.0, 0.8),
     'L0_ffn_qn_g': (1.0, 0.6),
     'L0_ffn_kn_g': (1.0, 0.6),
     'L0_ffn_gate_b': (0.0, 2.0),
     'L0_ffn_b1': (0.0, 2.0),
     'L0_ffn_b2': (0.0, 2.0)}
    factors = {'L0_ffn_Wq': 8.0,
     'L0_ffn_Wk': 8.0,
     'L0_ffn_Wv': 8.0,
     'L0_ffn_Wo': 8.0,
     'L0_ffn_gate_W': 8.0,
     'L0_ffn_W1': 8.0,
     'L0_ffn_W2': 8.0}
    for name, (base, spread) in spreads.items():
        noise = np.random.default_rng([zlib.crc32(name.encode()), seed]).standard_normal(out[name].shape)
        drawn = base * np.exp(spread * noise) if base else spread * noise
        out[name] = jnp.asarray(drawn.astype(out[name].dtype))
    for name, factor in factors.items():
        out[name] = (out[name] * factor).astype(out[name].dtype)
    return out
```

```python
from contextlib import ExitStack

import numpy as np

import concourse.bass as bass
from concourse import mybir

F32 = mybir.dt.float32
F16 = mybir.dt.float16
I32 = mybir.dt.int32
ALU = mybir.AluOpType
ACT = mybir.ActivationFunctionType
AX = mybir.AxisListType.X

P = 128
B, N, D = 2, 2048, 128
NT = N // P
T = B * NT
HA, DA = 8, 16
HS, DS = 2, 64
E, FF = 8, 512
FT = FF // P
NQ = N // 512
CH = 512
LN_EPS = 1e-5
DOT_EPS = 1e-8 * D
L2_EPS = 1e-12
NEG = -60000.0
WS = 64.0
VW = 2 * DS + 1

C_ID, C_U, C_L, C_LAST, C_BLK, C_HEAD, C_INV, C_POS = 0, 128, 256, 384, 512, 640, 648, 664
C_END = C_POS + NT * D
R_TB, R_BO, R_GB, R_NG, R_NB = 0, 128, 256, 264, 272
R_END = 280
K_LG, K_LB, K_QG, K_KG, K_B1 = 0, 1, 2, 3, 4
K_END = K_B1 + E * FT


def tower(nc, ids, emb_rows, consts, consts16, rows, cols, w_qkv, w_out, w_sm, w_o, w_gate, w1, w2, b2, out):
    with ExitStack() as ctx:
        def sb(name, shape, dt=F32):
            return ctx.enter_context(nc.sbuf_tensor(name, shape, dt))

        def sem(name):
            return ctx.enter_context(nc.semaphore(name))

        cst = sb("cst", [P, C_END])
        c16 = sb("c16", [P, 3 * P], F16)
        row = sb("row", [P, R_END])
        col = sb("col", [P, K_END])
        idx = sb("idx", [P, T], I32)
        wqkv = sb("wqkv", [P, 3, D])
        wout = sb("wout", [P, D])
        wsm = sb("wsm", [P, 3 * D])
        wo = sb("wo", [P, D])
        wgate = sb("wgate", [P, E])
        b2s = sb("b2s", [E, D])
        ones = sb("ones", [P, 1])
        mhalf = sb("mhalf", [P, 16])
        qkg8 = sb("qkg8", [P, 1])
        eps = sb("eps", [P, 10])
        ln_eps, l2_eps = eps[:, 0:2], eps[:, 2:10]
        credit = sb("credit", [P, 16])
        h_all = sb("h_all", [P, T, D])
        khl = sb("khl", [P, HS, B * N], F16)
        kh1 = sb("kh1", [DS + 1, HS, B * N], F16)
        qhh = sb("qhh", [P, HS, B * N], F16)
        ql = sb("ql", [DS + 1, HS, B * N], F16)
        v16 = sb("v16", [P, T, HS, VW], F16)
        y2 = sb("y2", [P, B * N])
        yhi = y2[:, 0:B * N // 2].bitcast(F16)
        ylo = y2[:, B * N // 2:].bitcast(F16)
        arena = sb("arena", [P, 2 * E * FF])
        w1hi = arena[:, 0:E * FF // 2].bitcast(F16)
        w1lo = arena[:, E * FF // 2:E * FF].bitcast(F16)
        w2hl = arena[:, E * FF:].bitcast(F16).rearrange("p (w z d) -> p w z d", z=2, d=D)

        ident = cst[:, C_ID:C_ID + P]
        upper = cst[:, C_U:C_U + P]
        lower = cst[:, C_L:C_L + P]
        last_row = cst[:, C_LAST:C_LAST + P]
        blk = cst[:, C_BLK:C_BLK + P]
        head = cst[:, C_HEAD:C_HEAD + HA]
        pos = cst[:, C_POS:C_END].rearrange("p (c d) -> p c d", d=D)
        ident16 = c16[:, 0:P]
        neg_qk = c16[:, P:2 * P]
        neg_kq = c16[:, 2 * P:3 * P]

        taken = [0]

        def early(*dims):
            n = int(np.prod(dims))
            piece = arena[:, taken[0]:taken[0] + n]
            taken[0] += n
            assert taken[0] <= 2 * E * FF
            names_ = "abcd"[:len(dims)]
            return piece if len(dims) == 1 else piece.rearrange(
                f"p ({' '.join(names_)}) -> p {' '.join(names_)}", **dict(zip(names_[1:], dims[1:])))

        xn = [early(B, D) for i in range(2)]
        xnT = [early(B, P) for i in range(2)]
        xsT = [early(B, P) for i in range(2)]
        qkT = [early(2, B, P) for i in range(2)]
        qkv = [early(B, 3, D) for i in range(2)]
        hb = [early(B, D) for i in range(2)]
        prod = early(B, 2, D)
        ao = early(B, D)
        ao2 = early(B, D)
        aoT = early(B, P)
        st6 = sb("st6", [P, B, 6])
        mv = [sb(f"mv{i}", [P, B, 2]) for i in range(2)]
        rs = [sb(f"rs{i}", [P, B]) for i in range(2)]
        x0 = sb("x0", [P, B])
        sg = sb("sg", [P, B, 2, D])
        cum = sb("cum", [P, B, 2, D])
        ab = sb("ab", [P, B, 2, HA])
        sm = sb("sm", [P, 8, B, HA])
        blkbuf = y2[:, 0:B * HA * P].rearrange("p (b h j) -> p b h j", b=B, h=HA)
        dtm = y2[:, B * HA * P:].rearrange("p (b h j) -> p b h j", b=B, h=HA)
        sq = sb("sq", [P, B, HA, P])
        st2 = sb("st2", [P, B, 6])
        mv2 = [sb(f"mv2{i}", [P, B, 2]) for i in range(2)]
        rr = [sb(f"rr{i}", [P, 4, B]) for i in range(2)]
        x2 = [sb(f"x2{i}", [P, B, D]) for i in range(2)]
        hxT = [sb(f"hxT{i}", [P, B, P]) for i in range(2)]
        qk2 = sb("qk2", [P, B, 4 * DS])
        ss = sb("ss", [P, 3, B * 4])
        qkn = sb("qkn", [P, B, 4, 2, DS])
        mx = sb("mx", [P, 4, NQ])
        mpad = sb("mpad", [P, HS, 4, DS + 1], F16)
        p32 = sb("p32", [P, 2, CH])
        phi = sb("phi", [P, 2, CH], F16)
        plo = sb("plo", [P, 2, CH], F16)
        rl = sb("rl", [P, 4])
        ot = sb("ot", [P, 2, 4, DS])
        och = sb("och", [P, 4, D])
        gt = sb("gt", [P, 4, 4, E])
        gl = sb("gl", [P, 4, 4])
        gT = sb("gT", [E, CH])
        sqf = sq[:].rearrange("p b h j -> p (b h j)")
        stage, oT, y32 = sqf[:, 0:1024], sqf[:, 1024:1536], sqf[:, 1536:2048]
        blkf = cst[:, C_POS:C_END]
        hid = blkf[:, 0:2 * CH].rearrange("p (u t) -> p u t", u=2)
        hhi = blkf[:, 2 * CH:3 * CH].bitcast(F16).rearrange("p (u t) -> p u t", u=2)
        hlo = blkf[:, 3 * CH:4 * CH].bitcast(F16).rearrange("p (u t) -> p u t", u=2)
        gs = sb("gs", [P, B * NQ, 4, E])

        ps = ctx.enter_context(nc.psum_tensor("ps", [P, 8, 512], F32))

        names = """load_c load_w load_s load_stage split_done gathered0 gathered setup
            stats veps rstd hb_ready xn_ready xnT_ps xnT_sb x0_link xsT_sb qkT_ps qkT_sb qkv_ps qkv_sb
            blk_ready dt_ps dt_sb sq_ready state_ps sg_ready x_ps cum_sb var_ready r_ready gr_ready grmu_ready
            coef ao_ready aoT_ps aoT_sb pr_ps h1_ready attn0 attnT0_ps attnT0_sb front_link core_link direct_link
            pos_ready stats2 st2_link rr_link rr_ready x2_ready x2T_ps hxT_sb qkv2_ps sqqk ss_ready rn_link rn_ready
            qkn_ready vhi_ready vlo_ready qkd_ps hi_ready lo_ready kh1_ready
            sm_ps sm_used max_link mneg mrow_ps mrow_sb s_ps p_ready plo_ready pv_done o_link o_used och_ready
            oT_ps oT_sb y_ps yhi_ready ylo_ready lg_ps lg_link lg_ready eg_ready gate_ready gT_ps gT_sb b2_ps h2_ready
            split_link hid_ps hid_ready hhi_ready hlo_ready w2_done eo_used stored"""
        S = {name: sem(name) for name in names.split()}
        NPIECE = (E * FF) // 1024
        CR = 2
        NEXP = B * NQ * E
        ds = bass.ds

        block = ctx.enter_context(nc.Block())

        @block.sync
        def _(sp):
            sp.dma_start(idx[:], ids).then_inc(S["load_c"], 16)
            sp.dma_start(row[:], rows).then_inc(S["load_w"], 16)
            sp.dma_start(cst[:], consts).then_inc(S["load_w"], 16)
            sp.dma_start(wqkv[:].rearrange("p a d -> p (a d)"), w_qkv).then_inc(S["load_w"], 16)
            sp.dma_start(col[:], cols).then_inc(S["load_w"], 16)
            sp.dma_start(wout[:], w_out).then_inc(S["load_w"], 16)
            sp.dma_start(wsm[:], w_sm).then_inc(S["load_s"], 16)
            sp.dma_start(c16[:], consts16).then_inc(S["load_s"], 16)
            sp.dma_start(wo[:], w_o).then_inc(S["load_s"], 16)
            sp.dma_start(wgate[:], w_gate).then_inc(S["load_s"], 16)
            sp.dma_start(b2s[:], b2).then_inc(S["load_s"], 16)
            sp.wait_ge(S["h1_ready"], NT)
            for n in range(2 * NPIECE):
                if n >= 1:
                    sp.wait_ge(S["split_done"], n)
                src = (w1 if n < NPIECE else w2)[:, (n % NPIECE) * 1024:(n % NPIECE) * 1024 + 1024]
                sp.dma_start(stage, src).then_inc(S["load_stage"], 16)
            for c in range(NQ):
                with sp.Fori(0, B) as b:
                    sp.wait_ge(S["eo_used"], (2 * c + b + 1) * E * 4 + 8)
                    for r in range(4):
                        sp.dma_start(out[ds(b * N + c * CH + r * P, P), :],
                                     h_all[:, ds(8 * c + 2 * r + b, 1), :].rearrange("p a d -> p (a d)")
                                     ).then_inc(S["stored"], 16)
            sp.wait_ge(S["stored"], 16 * 4 * B * NQ)

        @block.gpsimd
        def _(pool):
            g = nc.gpsimd
            pool.wait_ge(S["load_c"], 16)
            for t in range(T):
                g.indirect_dma_start(out=h_all[:, t, :], out_offset=None, in_=emb_rows,
                                     in_offset=bass.IndirectOffsetOnAxis(ap=idx[:, t:t + 1], axis=0)
                                     ).then_inc(S["gathered0" if t < B else "gathered"], 16)
            g.memset(mhalf[:], -0.5).then_inc(S["setup"], 1)
            g.memset(ln_eps, LN_EPS).then_inc(S["setup"], 1)
            g.memset(l2_eps, L2_EPS).then_inc(S["setup"], 1)
            g.memset(v16[:, :, :, DS:DS + 1], 1.0).then_inc(S["setup"], 1)
            g.memset(mpad[:], 0.0).then_inc(S["setup"], 1)
            g.memset(ones[:], 1.0).then_inc(S["setup"], 1)
            pool.wait_ge(S["setup"], 6)
            pool.wait_ge(S["load_w"], 80)

            def front(c, par, first=False):
                pool.wait_ge(S["stats"], c + 1)
                g.tensor_tensor(rs[par][:], mv[par][:, :, 1], ln_eps, ALU.add).then_inc(S["veps"], 1)
                pool.wait_ge(S["veps"], c + 1)
                g.tensor_tensor(rs[par][:], rs[par][:], mhalf[:, 0:B], ALU.pow).then_inc(S["rstd"], 1)
                if not first:
                    pool.wait_ge(S["h1_ready"], c - 1)
                g.tensor_tensor(hb[par], h_all[:, ds(2 * c, 2), :],
                                row[:, R_BO:R_BO + D].unsqueeze(1).to_broadcast([P, B, D]),
                                ALU.add).then_inc(S["hb_ready"], 1)

            def shifted(c, par):
                pool.wait_ge(S["xnT_sb"], c + 1)
                g.tensor_tensor(xsT[par], xnT[par], x0[:].unsqueeze(2).to_broadcast([P, B, P]), ALU.subtract
                                ).then_inc(S["xsT_sb"], 1)

            def q_blocks(c, par, first=False):
                pool.wait_ge(S["qkT_sb"], c + 1)
                for b in range(B):
                    if not first:
                        pool.wait_ge(S["dt_ps"], 2 * c + b - 1)
                    g.tensor_tensor(blkbuf[:, b],
                                    qkT[par][:, 1 if first else 0, b, :].unsqueeze(1).to_broadcast([P, HA, P]),
                                    head.unsqueeze(2).to_broadcast([P, HA, P]), ALU.mult
                                    ).then_inc(S["blk_ready"], 1)

            def coefs(c):
                pool.wait_ge(S["var_ready"], c + 1)
                g.tensor_tensor(sm[:, 4], sm[:, 3], mhalf[:].rearrange("p (b h) -> p b h", b=B),
                                ALU.pow).then_inc(S["r_ready"], 1)
                pool.wait_ge(S["r_ready"], c + 1)
                g.tensor_tensor(sm[:, 5], sm[:, 4], row[:, R_NG:R_NG + HA].unsqueeze(1).to_broadcast([P, B, HA]),
                                ALU.mult).then_inc(S["gr_ready"], 1)
                pool.wait_ge(S["gr_ready"], c + 1)
                g.tensor_tensor(sm[:, 6], sm[:, 5], sm[:, 0], ALU.mult).then_inc(S["grmu_ready"], 1)
                pool.wait_ge(S["grmu_ready"], c + 1)
                g.tensor_tensor(sm[:, 7], row[:, R_NB:R_NB + HA].unsqueeze(1).to_broadcast([P, B, HA]), sm[:, 6],
                                ALU.subtract).then_inc(S["coef"], 1)

            front(0, 0, first=True)
            pool.wait_ge(S["x0_link"], 2)
            shifted(0, 0)
            q_blocks(0, 0, first=True)
            coefs(0)
            front(1, 1, first=True)
            shifted(1, 1)
            q_blocks(1, 1)
            with pool.Fori(1, NT - 2, 2) as c:
                for u in range(2):
                    front(c + u + 1, u)
                    shifted(c + u + 1, u)
                    coefs(c + u)
                    q_blocks(c + u + 1, u)
            coefs(NT - 1)

            def both_norms(c, par):
                pool.wait_ge(S["stats2"], c + 1)
                k = 5 * c
                var = mv2[par][:, :, 1]
                a, b_, c_ = rr[par][:, 0], rr[par][:, 1], rr[par][:, 2]
                g.tensor_tensor(a, var, ln_eps, ALU.add).then_inc(S["rr_link"], 1)
                pool.wait_ge(S["rr_link"], k + 1)
                g.tensor_tensor(b_, a, mhalf[:, 0:B], ALU.pow).then_inc(S["rr_link"], 1)
                pool.wait_ge(S["rr_link"], k + 2)
                g.tensor_tensor(a, var, b_, ALU.mult).then_inc(S["rr_link"], 1)
                pool.wait_ge(S["rr_link"], k + 3)
                g.tensor_tensor(c_, a, b_, ALU.mult).then_inc(S["rr_link"], 1)
                pool.wait_ge(S["rr_link"], k + 4)
                g.tensor_tensor(c_, c_, ln_eps, ALU.add).then_inc(S["rr_link"], 1)
                pool.wait_ge(S["rr_link"], k + 5)
                g.tensor_tensor(a, c_, mhalf[:, 0:B], ALU.pow).then_inc(S["rn_link"], 1)
                pool.wait_ge(S["rn_link"], 2 * c + 1)
                g.tensor_tensor(rr[par][:, 3], a, b_, ALU.mult).then_inc(S["rr_ready"], 1)

            def l2_factors(c):
                pool.wait_ge(S["ss_ready"], c + 1)
                g.tensor_tensor(ss[:, 1], ss[:, 0], l2_eps, ALU.add).then_inc(S["rn_link"], 1)
                pool.wait_ge(S["rn_link"], 2 * c + 2)
                g.tensor_tensor(ss[:, 2], ss[:, 1], mhalf[:, 0:8], ALU.pow).then_inc(S["rn_ready"], 1)

            def keys_high(c, par):
                for b in range(B):
                    pool.wait_ge(S["hi_ready"], 2 * c + b + 1)
                    g.tensor_copy(kh1[0:DS, :, ds(b * N + c * P, P)],
                                  khl[0:DS, :, ds(b * N + c * P, P)]).then_inc(S["kh1_ready"], 1)

            with pool.Fori(0, NT - 1, 2) as c:
                for u in range(2):
                    both_norms(c + u, u)
                    l2_factors(c + u)
                    keys_high(c + u, u)

            for n in range(2 * NPIECE):
                o = (n % NPIECE) * 1024
                if n < NPIECE:
                    st_, hi, lo = stage, w1hi[:, o:o + 1024], w1lo[:, o:o + 1024]
                else:
                    st_ = stage.rearrange("p (a d) -> p a d", d=D)
                    hi, lo = (w2hl[:, o // D:o // D + 8, part, :] for part in range(2))
                pool.wait_ge(S["load_stage"], 16 * (n + 1))
                g.tensor_scalar(st_, st_, WS, None, ALU.mult).then_inc(S["split_link"], 1)
                pool.wait_ge(S["split_link"], 2 * n + 1)
                g.tensor_copy(hi, st_).then_inc(S["split_link"], 1)
                pool.wait_ge(S["split_link"], 2 * n + 2)
                g.tensor_tensor(lo, st_, hi, ALU.subtract).then_inc(S["split_done"], 1)

            with pool.Fori(0, NEXP * FT - 1, 2) as s:
                for u in range(2):
                    pool.wait_ge(S["hhi_ready"], s + u + 1)
                    pool.wait_ge(S["w2_done"], s + u + 1)
                    g.tensor_tensor(hlo[:, u], hid[:, u], hhi[:, u], ALU.subtract).then_inc(S["hlo_ready"], 1)

        @block.scalar
        def _(act):
            a = nc.scalar

            def front(c, par):
                act.wait_ge(S["xnT_ps"], c + 1)
                a.copy(xnT[par].rearrange("p b t -> p (b t)"), ps[:, 0, 0:B * P]).then_inc(S["xnT_sb"], 1)
                act.wait_ge(S["qkT_ps"], c + 1)
                a.copy(qkT[par].rearrange("p a b t -> p (a b t)"), ps[:, 1, :]).then_inc(S["qkT_sb"], 1)

            def cum_out(c):
                act.wait_ge(S["x_ps"], 2 * c + 2)
                a.copy(cum[:].rearrange("p b a d -> p b (a d)"), ps[:, 5:7, 0:2 * D]).then_inc(S["cum_sb"], 1)

            def ao_out(c):
                act.wait_ge(S["aoT_ps"], c + 1)
                a.copy(aoT.rearrange("p b t -> p (b t)"), ps[:, 0, B * P:]).then_inc(S["aoT_sb"], 1)

            front(0, 0)
            for b in range(B):
                act.wait_ge(S["attnT0_ps"], b + 1)
                a.copy(dtm[:, b].rearrange("p (z h) j -> p z (h j)", z=2), ps[:, 3:5, :]).then_inc(S["attnT0_sb"], 1)
            cum_out(0)
            ao_out(0)
            front(1, 1)

            def core(c, par, nxt):
                if nxt:
                    act.wait_ge(S["xnT_ps"], c + 2)
                    a.copy(xnT[par].rearrange("p b t -> p (b t)"), ps[:, 0, 0:B * P]).then_inc(S["xnT_sb"], 1)
                for b in range(B):
                    act.wait_ge(S["dt_sb"], 2 * c + b + 1)
                    a.activation(sq[:, b], dtm[:, b], ACT.Square).then_inc(S["sq_ready"], 1)
                if nxt:
                    act.wait_ge(S["qkT_ps"], c + 2)
                    a.copy(qkT[par].rearrange("p a b t -> p (a b t)"), ps[:, 1, :]).then_inc(S["qkT_sb"], 1)
                cum_out(c)
                ao_out(c)

            with act.Fori(1, NT - 2, 2) as c:
                for u in range(2):
                    core(c + u, u, True)
            core(NT - 1, 0, False)

            def a2(c, par):
                act.wait_ge(S["x2T_ps"], c + 1)
                a.activation(hxT[par][:].rearrange("p b t -> p (b t)"), ps[:, 0, B * P * par:B * P * (par + 1)],
                             ACT.Identity, bias=col[:, K_LB:K_LB + 1], scale=col[:, K_LG:K_LG + 1]
                             ).then_inc(S["hxT_sb"], 1)
                act.wait_ge(S["qkv2_ps"], c + 1)
                a.activation(qk2[:], ps[:, 1:3, 0:2 * D], ACT.Square).then_inc(S["sqqk"], 1)
                a.copy(v16[:, ds(2 * c, B), :, 0:DS],
                       ps[:, 1:3, 2 * D:3 * D].rearrange("p b (h d) -> p b h d", h=HS)).then_inc(S["vhi_ready"], 1)
                for b in range(B):
                    act.wait_ge(S["qkd_ps"], 2 * c + b + 1)
                    at = ds(b * N + c * P, P)
                    a.activation(qhh[:, :, at], ps[:, 3 + b, 0:2 * P].rearrange("p (h t) -> p h t", h=HS),
                                 ACT.Copy, scale=qkg8[:])
                    a.activation(khl[:, :, at], ps[:, 3 + b, 2 * P:4 * P].rearrange("p (h t) -> p h t", h=HS),
                                 ACT.Copy, scale=col[:, K_KG:K_KG + 1]).then_inc(S["hi_ready"], 1)

            with act.Fori(0, NT - 1, 2) as c:
                for u in range(2):
                    a2(c + u, u)

            def probs(s0, u, lo=0):
                act.wait_ge(S["s_ps"], s0 + 1)
                act.wait_ge(S["plo_ready"], s0 + 1)
                act.wait_ge(S["pv_done"], s0 + 1)
                a.activation(p32[:, u, lo:], ps[:, u, lo:], ACT.Exp)
                a.activation(phi[:, u, lo:], ps[:, u, lo:], ACT.Exp).then_inc(S["p_ready"], 1)

            base = 0
            for c in range(NQ):
                steps = 4 * c + 4
                with act.Fori(0, B) as b:
                    for h in range(HS):
                        it = 4 * c + 2 * b + h
                        act.wait_ge(S["mrow_ps"], it + 1)
                        a.copy(ql[DS:DS + 1, h, ds(b * N + c * CH, CH)], ps[DS:DS + 1, 4, :]).then_inc(S["mrow_sb"], 1)
                        s0 = base + (2 * b + h) * steps
                        for d in range(4):
                            probs(s0 + d, d % 2, d * P)
                        if c:
                            with act.Fori(0, c) as kb:
                                for i in range(4):
                                    probs(s0 + 4 + 4 * kb + i, i % 2)
                    m = 2 * c + b
                    act.wait_ge(S["oT_ps"], 1 + m + 1)
                    a.copy(oT, ps[:, 4, :]).then_inc(S["oT_sb"], 1)
                    act.wait_ge(S["y_ps"], m + 1)
                    a.copy(y32, ps[:, 5, :])
                    a.copy(yhi[:, ds(m * CH, CH)], ps[:, 5, :]).then_inc(S["yhi_ready"], 1)
                    act.wait_ge(S["lg_ready"], m + 1)
                    a.activation(gt[:, 1], gt[:, 0], ACT.Exp).then_inc(S["eg_ready"], 1)
                    act.wait_ge(S["gT_ps"], m + 1)
                    a.copy(gT[:], ps[0:E, 4, :]).then_inc(S["gT_sb"], 1)
                base += 4 * steps

            with act.Fori(0, NEXP) as n:
                for f in range(FT):
                    s = n * FT + f
                    act.wait_ge(S["hid_ps"], s + 1)
                    act.wait_ge(S["hlo_ready"], s + 1)
                    a.activation(hid[:, f % 2], ps[:, f % 2, :], ACT.Gelu_apprx_tanh,
                                 bias=col[:, ds(K_B1 + (n % E) * FT + f, 1)], scale=1.0 / WS
                                 ).then_inc(S["hid_ready"], 1)

        @block.vector
        def _(dve):
            v = nc.vector

            for i, name in enumerate(["sm_used", "p_ready", "plo_ready", "pv_done", "hid_ready", "hlo_ready", "w2_done"]):
                v.memset(credit[:, i:i + 1], 0.0).then_inc(S[name], CR)
            v.memset(credit[:, 14:15], 0.0).then_inc(S["eo_used"], 8)
            for i, name in enumerate(["oT_ps", "mrow_sb", "gT_sb", "o_used", "h2_ready", "qkn_ready", "lo_ready"]):
                v.memset(credit[:, 7 + i:8 + i], 0.0).then_inc(S[name], 1)
            v.memset(kh1[DS:DS + 1, :, :], 1.0).then_inc(S["pos_ready"], 1)
            dve.wait_ge(S["load_w"], 80)
            v.tensor_scalar(qkg8[:], col[:, K_QG:K_QG + 1], float(DS) ** 0.5, None, ALU.mult).then_inc(S["pos_ready"], 1)
            v.tensor_tensor(pos, pos, row[:, R_TB:R_TB + D].unsqueeze(1).to_broadcast([P, NT, D]),
                            ALU.add).then_inc(S["pos_ready"], 1)
            dve.wait_ge(S["pos_ready"], 3)

            def embed(c, par):
                h = h_all[:, ds(2 * c, 2), :]
                v.tensor_tensor(h, h, cst[:, ds(C_POS + c * D, D)].unsqueeze(1).to_broadcast([P, B, D]),
                                ALU.add).then_inc(S["front_link"], 1)
                dve.wait_ge(S["front_link"], 2 * c + 1)
                v.memset(credit[:, 13:14], 0.0)
                for b in range(B):
                    last = v.bn_stats(st6[:, b], h_all[:, ds(2 * c + b, 1), :].rearrange("p a d -> p (a d)"))
                last.then_inc(S["front_link"], 1)
                dve.wait_ge(S["front_link"], 2 * c + 2)
                v.memset(credit[:, 13:14], 0.0)
                for b in range(B):
                    last = v.bn_aggr(mv[par][:, b], st6[:, b])
                last.then_inc(S["stats"], 1)

            def normed(c, par):
                dve.wait_ge(S["rstd"], c + 1)
                dve.wait_ge(S["stats"], c + 1)
                for b in range(B):
                    last = v.tensor_scalar(xn[par][:, b], h_all[:, ds(2 * c + b, 1), :].rearrange("p a d -> p (a d)"),
                                           mv[par][:, b, 0:1], rs[par][:, b:b + 1], ALU.subtract, ALU.mult)
                last.then_inc(S["xn_ready"], 1)

            def rows_out(c, par):
                for b in range(B):
                    dve.wait_ge(S["qkv_ps"], 2 * c + b + 1)
                    v.tensor_copy(qkv[par][:, b], ps[:, 2, 0:3 * D].rearrange("p (a d) -> p a d", d=D)
                                  ).then_inc(S["qkv_sb"], 1)

            def state_out(c):
                dve.wait_ge(S["state_ps"], 2 * c + B)
                for b in range(B):
                    v.tensor_tensor(sg[:, b], ps[:, 7, b * 2 * D:(b + 1) * 2 * D].rearrange("p (a d) -> p a d", d=D),
                                    blk.unsqueeze(1).to_broadcast([P, 2, D]), ALU.mult).then_inc(S["sg_ready"], 1)

            def h1_out(c, par):
                dve.wait_ge(S["pr_ps"], c + 1)
                dve.wait_ge(S["hb_ready"], c + 1)
                v.tensor_tensor(h_all[:, ds(2 * c, 2), :], ps[:, 0, B * P:].rearrange("p (b d) -> p b d", b=B),
                                hb[par], ALU.add).then_inc(S["h1_ready"], 1)

            dve.wait_ge(S["gathered0"], 16 * B)
            embed(0, 0)
            normed(0, 0)
            dve.wait_ge(S["xnT_sb"], 1)
            v.tensor_reduce(x0[:], xnT[0], AX, ALU.add
                            ).then_inc(S["x0_link"], 1)
            dve.wait_ge(S["x0_link"], 1)
            v.tensor_scalar(x0[:], x0[:], 1.0 / P, None, ALU.mult).then_inc(S["x0_link"], 1)
            dve.wait_ge(S["x0_link"], 2)
            rows_out(0, 0)
            links = 0

            def link(ins):
                nonlocal links
                links += 1
                ins.then_inc(S["direct_link"], 1)
                dve.wait_ge(S["direct_link"], links)

            low_h = lower.unsqueeze(1).to_broadcast([P, HA, P])
            inv0 = cst[:, C_INV:C_INV + 1]
            for b in range(B):
                dve.wait_ge(S["dt_ps"], b + 1)
                dots = ps[:, 3:5, :].rearrange("p z (h j) -> p (z h) j", j=P)
                v.tensor_tensor(dtm[:, b], dots, low_h, ALU.mult).then_inc(S["dt_sb"], 1)
                dve.wait_ge(S["dt_sb"], b + 1)
                link(v.tensor_reduce(sm[:, 1, b], dtm[:, b], AX, ALU.add))
                link(v.tensor_scalar(sm[:, 0, b], sm[:, 1, b], inv0, None, ALU.mult))
                link(v.tensor_tensor(sq[:, b], dtm[:, b], sm[:, 0, b].unsqueeze(2).to_broadcast([P, HA, P]), ALU.subtract))
                link(v.tensor_tensor(dtm[:, b], sq[:, b], low_h, ALU.mult))
                link(v.tensor_tensor(sq[:, b], dtm[:, b], dtm[:, b], ALU.mult))
                link(v.tensor_reduce(sm[:, 1, b], sq[:, b], AX, ALU.add))
            v.tensor_scalar(sm[:, 3], sm[:, 1], inv0, DOT_EPS, ALU.mult, ALU.add).then_inc(S["var_ready"], 1)
            state_out(0)
            dve.wait_ge(S["coef"], 1)
            for b in range(B):
                link(v.tensor_tensor(sq[:, b], dtm[:, b], sm[:, 5, b].unsqueeze(2).to_broadcast([P, HA, P]), ALU.mult))
                link(v.tensor_tensor(dtm[:, b], low_h,
                                     row[:, R_NB:R_NB + HA].unsqueeze(2).to_broadcast([P, HA, P]), ALU.mult))
                v.tensor_tensor(sq[:, b], sq[:, b], dtm[:, b], ALU.add).then_inc(S["attn0"], 1)
            dve.wait_ge(S["x_ps"], B)
            dve.wait_ge(S["cum_sb"], 1)
            v.tensor_copy(ao, ps[:, 5:7, 3 * D:4 * D]).then_inc(S["ao_ready"], 1)
            h1_out(0, 0)
            dve.wait_ge(S["gathered"], 16 * (T - B))
            embed(1, 1)
            normed(1, 1)
            rows_out(1, 1)

            def core(c, par, nxt):
                if nxt:
                    embed(c + 1, par)
                for b in range(B):
                    if nxt and b == 1:
                        normed(c + 1, par)
                    dve.wait_ge(S["dt_ps"], 2 * c + b + 1)
                    dve.wait_ge(S["x_ps"], 2 * c + b - 1)
                    v.tensor_tensor(dtm[:, b], ps[:, 3:5, :].rearrange("p z (h j) -> p (z h) j", j=P),
                                    upper.unsqueeze(1).to_broadcast([P, HA, P]), ALU.mult).then_inc(S["dt_sb"], 1)
                state_out(c)
                q = qkv[1 - par][:, :, 0, :]
                k = 6 * (c - 1)
                dve.wait_ge(S["x_ps"], 2 * c + 2)
                dve.wait_ge(S["cum_sb"], c + 1)
                v.tensor_tensor(prod, ps[:, 5:7, :].rearrange("p b (a z d) -> p b a z d", z=2, d=D)[:, :, :, 0, :],
                                q.unsqueeze(2).to_broadcast([P, B, 2, D]), ALU.mult).then_inc(S["core_link"], 1)
                dve.wait_ge(S["core_link"], k + 1)
                v.tensor_reduce(ab[:].rearrange("p b a h -> p (b a h)"),
                                prod.rearrange("p b a (h e) -> p (b a h) e", e=DA), AX, ALU.add
                                ).then_inc(S["core_link"], 1)
                dve.wait_ge(S["core_link"], k + 2)
                inv = cst[:, ds(C_INV + c, 1)]
                v.tensor_scalar(sm[:, 0], ab[:, :, 0], inv, None, ALU.mult).then_inc(S["core_link"], 1)
                v.tensor_tensor(sm[:, 1], ps[:, 2, 3 * D:3 * D + 16].rearrange("p (b h) -> p b h", b=B), ab[:, :, 1],
                                ALU.add)
                dve.wait_ge(S["core_link"], k + 3)
                v.tensor_tensor(sm[:, 2], sm[:, 0], sm[:, 0], ALU.mult).then_inc(S["core_link"], 1)
                dve.wait_ge(S["core_link"], k + 4)
                v.scalar_tensor_tensor(sm[:, 4], sm[:, 1], inv, sm[:, 2], ALU.mult, ALU.subtract
                                       ).then_inc(S["core_link"], 1)
                dve.wait_ge(S["core_link"], k + 5)
                v.tensor_scalar(sm[:, 3], sm[:, 4], 0.0, DOT_EPS, ALU.max, ALU.add).then_inc(S["var_ready"], 1)
                if nxt:
                    rows_out(c + 1, par)
                dve.wait_ge(S["coef"], c + 1)
                v.tensor_tensor(ao.rearrange("p b (h e) -> p b h e", e=DA),
                                ps[:, 5:7, 3 * D:4 * D].rearrange("p b (h e) -> p b h e", e=DA),
                                sm[:, 5].unsqueeze(3).to_broadcast([P, B, HA, DA]), ALU.mult)
                v.tensor_tensor(ao2.rearrange("p b (h e) -> p b h e", e=DA),
                                ps[:, 5:7, D:2 * D].rearrange("p b (h e) -> p b h e", e=DA),
                                sm[:, 7].unsqueeze(3).to_broadcast([P, B, HA, DA]), ALU.mult
                                ).then_inc(S["core_link"], 1)
                dve.wait_ge(S["core_link"], k + 6)
                v.tensor_tensor(ao, ao, ao2, ALU.add).then_inc(S["ao_ready"], 1)
                h1_out(c, 1 - par)

            with dve.Fori(1, NT - 2, 2) as c:
                for u in range(2):
                    core(c + u, u, True)
            core(NT - 1, 0, False)

            def a2(c, par):
                dve.wait_ge(S["h1_ready"], c + 1)
                v.memset(credit[:, 13:14], 0.0)
                for b in range(B):
                    last = v.bn_stats(st2[:, b], h_all[:, ds(2 * c + b, 1), :].rearrange("p a d -> p (a d)"))
                last.then_inc(S["st2_link"], 1)
                dve.wait_ge(S["st2_link"], c + 1)
                v.memset(credit[:, 13:14], 0.0)
                for b in range(B):
                    last = v.bn_aggr(mv2[par][:, b], st2[:, b])
                last.then_inc(S["stats2"], 1)
                dve.wait_ge(S["stats2"], c + 1)
                dve.wait_ge(S["rr_ready"], c + 1)
                for b in range(B):
                    last = v.tensor_scalar(x2[par][:, b], h_all[:, ds(2 * c + b, 1), :].rearrange("p a d -> p (a d)"),
                                           mv2[par][:, b, 0:1], rr[par][:, 3, b:b + 1], ALU.subtract, ALU.mult)
                last.then_inc(S["x2_ready"], 1)
                dve.wait_ge(S["sqqk"], c + 1)
                v.tensor_reduce(ss[:, 0], qk2[:].rearrange("p b (g e) -> p (b g) e", e=DS), AX, ALU.add
                                ).then_inc(S["ss_ready"], 1)
                dve.wait_ge(S["vhi_ready"], c + 1)
                v.tensor_tensor(v16[:, ds(2 * c, B), :, DS + 1:],
                                ps[:, 1:3, 2 * D:3 * D].rearrange("p b (h e) -> p b h e", h=HS),
                                v16[:, ds(2 * c, B), :, 0:DS], ALU.subtract).then_inc(S["vlo_ready"], 1)
                dve.wait_ge(S["rn_ready"], c + 1)
                for b in range(B):
                    v.tensor_tensor(qkn[:, b], ps[:, 1 + b, 0:2 * D].rearrange("p (g e) -> p g e", e=DS)
                                    .unsqueeze(2).to_broadcast([P, 4, 2, DS]),
                                    ss[:, 2, 4 * b:4 * b + 4].unsqueeze(2).unsqueeze(3).to_broadcast([P, 4, 2, DS]),
                                    ALU.mult).then_inc(S["qkn_ready"], 1)
                for b in range(B):
                    at = ds(b * N + c * P, P)
                    dve.wait_ge(S["hi_ready"], 2 * c + b + 1)
                    v.scalar_tensor_tensor(ql[0:DS, :, at], ps[0:DS, 3 + b, 0:2 * P].rearrange("p (h t) -> p h t", h=HS),
                                           qkg8[0:DS], qhh[0:DS, :, at], ALU.mult, ALU.subtract)
                    v.scalar_tensor_tensor(khl[DS:, :, at], ps[DS:, 3 + b, 2 * P:].rearrange("p (h t) -> p h t", h=HS),
                                           col[DS:, K_KG:K_KG + 1], khl[DS:, :, at], ALU.mult, ALU.subtract
                                           ).then_inc(S["lo_ready"], 1)

            with dve.Fori(0, NT - 1, 2) as c:
                for u in range(2):
                    a2(c + u, u)

            def low_parts(s, u, lo=0):
                dve.wait_ge(S["p_ready"], s + 1 + CR)
                dve.wait_ge(S["pv_done"], s + 1)
                v.tensor_tensor(plo[:, u, lo:], p32[:, u, lo:], phi[:, u, lo:], ALU.subtract
                                ).then_inc(S["plo_ready"], 1)

            base, mbase = 0, 0
            for c in range(NQ):
                steps = 4 * c + 4
                with dve.Fori(0, B) as b:
                    it0 = 4 * c + 2 * b
                    m = 2 * c + b
                    for h in range(HS):
                        for r in range(4):
                            for kb in range(c + 1):
                                k = mbase + (2 * b + h) * steps + r * (c + 1) + kb
                                w = CH if kb < c else (r + 1) * P
                                dve.wait_ge(S["sm_ps"], k + 1)
                                v.tensor_reduce(mx[:, r, kb:kb + 1], ps[:, 2 + (r * (c + 1) + kb) % 2, 0:w], AX, ALU.max
                                                ).then_inc(S["sm_used"], 1)
                        dve.wait_ge(S["sm_used"], k + 1 + CR)
                        v.tensor_reduce(rl[:], mx[:, :, 0:c + 1], AX, ALU.max).then_inc(S["max_link"], 1)
                        dve.wait_ge(S["max_link"], it0 + h + 1)
                        v.tensor_scalar(mpad[:, h, :, DS], rl[:], -1.0, None, ALU.mult).then_inc(S["mneg"], 1)
                    for h in range(HS):
                        s0 = base + (2 * b + h) * steps
                        for d in range(4):
                            low_parts(s0 + d, d % 2, d * P)
                        if c:
                            with dve.Fori(0, c) as kb:
                                for i in range(4):
                                    low_parts(s0 + 4 + 4 * kb + i, i % 2)
                        it = it0 + h
                        dve.wait_ge(S["pv_done"], s0 + steps + CR)
                        if h == 0:
                            dve.wait_ge(S["oT_ps"], 1 + m)
                        o = ps[:, 6:8, 0:2 * VW].rearrange("p a (z e) -> p a z e", e=VW)
                        rlv = rl[:].rearrange("p (a z) -> p a z", a=2)
                        v.reciprocal(rlv, o[:, :, :, DS]).then_inc(S["o_link"], 1)
                        dve.wait_ge(S["o_link"], 2 * it + 1)
                        rlb = rlv.unsqueeze(3).to_broadcast([P, 2, 2, DS])
                        v.tensor_tensor(ot[:, 0].rearrange("p (a z) e -> p a z e", a=2), o[:, :, :, DS + 1:], rlb, ALU.mult)
                        v.tensor_tensor(ot[:, 1].rearrange("p (a z) e -> p a z e", a=2), o[:, :, :, 0:DS], rlb,
                                        ALU.mult).then_inc(S["o_used"], 1)
                        dve.wait_ge(S["o_used"], 1 + it + 1)
                        v.tensor_tensor(och[:, :, h * DS:(h + 1) * DS], ot[:, 0], ot[:, 1], ALU.add
                                        ).then_inc(S["och_ready"], 1)
                        v.memset(credit[:, 14:15], 0.0).then_inc(S["o_link"], 1)
                    dve.wait_ge(S["yhi_ready"], m + 1)
                    v.tensor_tensor(ylo[:, ds(m * CH, CH)], ps[:, 5, :], yhi[:, ds(m * CH, CH)], ALU.subtract
                                    ).then_inc(S["ylo_ready"], 1)
                    dve.wait_ge(S["lg_ps"], m + 1)
                    v.tensor_tensor(gt[:, 2], ps[:, 4, 0:4 * E].rearrange("p (r e) -> p r e", e=E),
                                    row[:, R_GB:R_GB + E].unsqueeze(1).to_broadcast([P, 4, E]), ALU.add
                                    ).then_inc(S["lg_link"], 1)
                    dve.wait_ge(S["lg_link"], 5 * m + 1)
                    v.tensor_reduce(gl[:, 0], gt[:, 2], AX, ALU.max).then_inc(S["lg_link"], 1)
                    dve.wait_ge(S["lg_link"], 5 * m + 2)
                    v.tensor_tensor(gt[:, 0], gt[:, 2], gl[:, 0].unsqueeze(2).to_broadcast([P, 4, E]), ALU.subtract
                                    ).then_inc(S["lg_ready"], 1)
                    dve.wait_ge(S["eg_ready"], m + 1)
                    v.tensor_reduce(gl[:, 1], gt[:, 1], AX, ALU.add).then_inc(S["lg_link"], 1)
                    dve.wait_ge(S["lg_link"], 5 * m + 3)
                    v.reciprocal(gl[:, 2], gl[:, 1]).then_inc(S["lg_link"], 1)
                    dve.wait_ge(S["lg_link"], 5 * m + 4)
                    v.tensor_tensor(gt[:, 3], gt[:, 1], gl[:, 2].unsqueeze(2).to_broadcast([P, 4, E]), ALU.mult
                                    ).then_inc(S["gate_ready"], 1)
                    dve.wait_ge(S["gate_ready"], m + 1)
                    v.tensor_scalar(gs[:, ds(m, 1)].rearrange("p a r e -> p (a r) e"), gt[:, 3], 1.0 / WS, None, ALU.mult
                                    ).then_inc(S["lg_link"], 1)
                    dve.wait_ge(S["b2_ps"], m + 1)
                    hc = h_all[:, ds(8 * c + b, 4, step=2), :]
                    v.tensor_tensor(hc, ps[:, 5, :].rearrange("p (r d) -> p r d", r=4), hc, ALU.add
                                    ).then_inc(S["h2_ready"], 1)
                base += 4 * steps
                mbase += 4 * steps
            dve.wait_ge(S["h2_ready"], 1 + B * NQ)
            dve.wait_ge(S["lg_link"], 5 * B * NQ)

            def high_parts(n, f):
                s = n * FT + f
                dve.wait_ge(S["hid_ready"], s + 1 + CR)
                dve.wait_ge(S["w2_done"], s + 1)
                v.tensor_copy(hhi[:, f % 2], hid[:, f % 2]).then_inc(S["hhi_ready"], 1)

            def add_expert(n, par):
                dve.wait_ge(S["w2_done"], n * FT + FT + CR)
                dve.wait_ge(S["eo_used"], n * 4 + 8)
                m = n // E
                for r in range(4):
                    hr = h_all[:, ds((m // 2) * 8 + m % 2 + 2 * r, 1), :].rearrange("p a d -> p (a d)")
                    v.scalar_tensor_tensor(hr, ps[:, 2 + par, r * D:(r + 1) * D],
                                           gs[:, ds(m, 1), r, ds(n % E, 1)].rearrange("p a e -> p (a e)"), hr,
                                           ALU.mult, ALU.add).then_inc(S["eo_used"], 1)

            for u in range(2):
                for f in range(FT):
                    high_parts(u, f)
                    if u == 1 and f == 1:
                        add_expert(0, 0)
            with dve.Fori(2, NEXP - 1, 2) as n:
                for u in range(2):
                    for f in range(FT):
                        high_parts(n + u, f)
                        if f == 1:
                            add_expert(n + u - 1, 1 - u)
            add_expert(NEXP - 1, 1)

        @block.tensor
        def _(pe):
            t_ = nc.tensor

            def mm(o, l, r, start=True, stop=True):
                return t_.matmul(o, l, r, start=start, stop=stop, skip_group_check=True)

            def xn_T(c, par, first=False):
                pe.wait_ge(S["xn_ready"], c + 1)
                if not first:
                    pe.wait_ge(S["xnT_sb"], c)
                    pe.wait_ge(S["h1_ready"], c - 1)
                for b in range(B):
                    last = t_.transpose(ps[:, 0, b * P:(b + 1) * P], xn[par][:, b], ident)
                last.then_inc(S["xnT_ps"], 1)

            def project(c, par, first=False):
                pe.wait_ge(S["xnT_sb"], c + 1)
                pe.wait_ge(S["xsT_sb"], c + 1)
                if not first:
                    pe.wait_ge(S["qkT_sb"], c)
                mm(ps[:, 1, 0:B * P], wqkv[:, 0], xnT[par].rearrange("p b t -> p (b t)"))
                mm(ps[:, 1, B * P:], wqkv[:, 1], xsT[par].rearrange("p b t -> p (b t)")).then_inc(S["qkT_ps"], 1)
                if not first:
                    pe.wait_ge(S["var_ready"], c)
                for b in range(B):
                    if not (first and b == 0):
                        pe.wait_ge(S["qkv_sb"], 2 * c + b)
                    mm(ps[:, 2, 0:D], xnT[par][:, b], wqkv[:, 0])
                    mm(ps[:, 2, 2 * D:3 * D], xnT[par][:, b], wqkv[:, 2])
                    mm(ps[:, 2, D:2 * D], xsT[par][:, b], wqkv[:, 1]).then_inc(S["qkv_ps"], 1)

            def out_project(c):
                pe.wait_ge(S["ao_ready"], c + 1)
                for b in range(B):
                    last = t_.transpose(ps[:, 0, (B + b) * P:(B + b + 1) * P], ao[:, b], ident)
                last.then_inc(S["aoT_ps"], 1)
                pe.wait_ge(S["aoT_sb"], c + 1)
                for b in range(B):
                    last = mm(ps[:, 0, (B + b) * P:(B + b + 1) * P], aoT[:, b], wout[:])
                last.then_inc(S["pr_ps"], 1)

            def sums(c, par, b, first=False):
                kv = qkv[par][:, b, 1:3, :].rearrange("p a d -> p (a d)")
                pe.wait_ge(S["qkv_sb"], 2 * c + b + 1)
                if not first:
                    pe.wait_ge(S["ao_ready"], c)
                    pe.wait_ge(S["cum_sb"], c)
                mm(ps[:, 5 + b, 0:2 * D], upper, kv, stop=first)
                if not first:
                    mm(ps[:, 5 + b, 0:2 * D], last_row, cum[:, b].rearrange("p a d -> p (a d)"), start=False)
                    pe.wait_ge(S["sg_ready"], 2 * c)
                    mm(ps[:, 5 + b, 2 * D:], qkT[par][:, 0, b], sg[:, b].rearrange("p a d -> p (a d)"), start=False)
                mm(ps[:, 7, b * 2 * D:(b + 1) * 2 * D], qkv[par][:, b, 1, :], kv, start=(first and b == 0)
                   ).then_inc(S["state_ps"], 1)

            pe.wait_ge(S["load_w"], 80)
            pe.wait_ge(S["setup"], 6)
            xn_T(0, 0, first=True)
            project(0, 0, first=True)
            for b in range(B):
                pe.wait_ge(S["blk_ready"], b + 1)
                if b:
                    pe.wait_ge(S["dt_sb"], b)
                for z in range(2):
                    last = mm(ps[:, 3 + z, :], qkT[0][:, 0, b], blkbuf[:, b].rearrange("p (z h) j -> p z (h j)", z=2)[:, z])
                last.then_inc(S["dt_ps"], 1)
            for b in range(B):
                sums(0, 0, b, first=True)
            pe.wait_ge(S["dt_sb"], B)
            for b in range(B):
                pe.wait_ge(S["attn0"], b + 1)
                if b:
                    pe.wait_ge(S["attnT0_sb"], b)
                for h in range(HA):
                    last = t_.transpose(ps[:, 3 + h // 4, h % 4 * P:(h % 4 + 1) * P], sq[:, b, h], ident)
                last.then_inc(S["attnT0_ps"], 1)
                pe.wait_ge(S["attnT0_sb"], b + 1)
                for h in range(HA):
                    last = mm(ps[:, 5 + b, 3 * D + h * DA:3 * D + (h + 1) * DA], dtm[:, b, h],
                              qkv[0][:, b, 2, h * DA:(h + 1) * DA], start=False)
                last.then_inc(S["x_ps"], 1)
            out_project(0)
            xn_T(1, 1)
            project(1, 1)

            def core(c, par, nxt):
                cur = 1 - par
                for b in range(B):
                    pe.wait_ge(S["blk_ready"], 2 * c + b + 1)
                    pe.wait_ge(S["dt_sb"], 2 * c + b)
                    for z in range(2):
                        last = mm(ps[:, 3 + z, :], qkT[cur][:, 1, b],
                                  blkbuf[:, b].rearrange("p (z h) j -> p z (h j)", z=2)[:, z])
                    last.then_inc(S["dt_ps"], 1)
                    sums(c, cur, b)
                    if nxt and b == 0:
                        xn_T(c + 1, par)
                for b in range(B):
                    pe.wait_ge(S["dt_sb"], 2 * c + b + 1)
                    for h in range(HA):
                        mm(ps[:, 5 + b, 3 * D + h * DA:3 * D + (h + 1) * DA], dtm[:, b, h],
                           qkv[cur][:, b, 2, h * DA:(h + 1) * DA], start=False)
                    pe.wait_ge(S["sq_ready"], 2 * (c - 1) + b + 1)
                    for h in range(HA):
                        last = mm(ps[:, 2, 3 * D + b * HA + h:3 * D + b * HA + h + 1], sq[:, b, h], ones[:])
                    last.then_inc(S["x_ps"], 1)
                if nxt:
                    project(c + 1, par)
                out_project(c)

            with pe.Fori(1, NT - 2, 2) as c:
                for u in range(2):
                    core(c + u, u, True)
            core(NT - 1, 0, False)

            pe.wait_ge(S["load_s"], 80)

            def a2(c, par):
                pe.wait_ge(S["x2_ready"], c + 1)
                for b in range(B):
                    last = t_.transpose(ps[:, 0, (B * par + b) * P:(B * par + b + 1) * P], x2[par][:, b], ident)
                last.then_inc(S["x2T_ps"], 1)
                pe.wait_ge(S["hxT_sb"], c + 1)
                pe.wait_ge(S["qkn_ready"], 1 + 2 * c)
                for b in range(B):
                    last = mm(ps[:, 1 + b, 0:3 * D], hxT[par][:, b], wsm[:])
                last.then_inc(S["qkv2_ps"], 1)
                for b in range(B):
                    pe.wait_ge(S["qkn_ready"], 1 + 2 * c + b + 1)
                    pe.wait_ge(S["lo_ready"], 1 + 2 * c)
                    for i in range(4):
                        last = t_.transpose(ps[:, 3 + b, i * P:(i + 1) * P],
                                            qkn[:, b, i].rearrange("p z e -> p (z e)"), ident)
                    last.then_inc(S["qkd_ps"], 1)

            with pe.Fori(0, NT - 1, 2) as c:
                for u in range(2):
                    a2(c + u, u)

            pe.wait_ge(S["hi_ready"], T)
            pe.wait_ge(S["lo_ready"], 1 + T)
            pe.wait_ge(S["kh1_ready"], T)
            pe.wait_ge(S["vlo_ready"], NT)
            base, mbase = 0, 0
            for c in range(NQ):
                steps = 4 * c + 4
                with pe.Fori(0, B) as b:
                    m = 2 * c + b
                    q0 = b * N + c * CH
                    for h in range(HS):
                        for r in range(4):
                            for kb in range(c + 1):
                                j = r * (c + 1) + kb
                                k = mbase + (2 * b + h) * steps + j
                                w = CH if kb < c else (r + 1) * P
                                pe.wait_ge(S["sm_used"], k + 1)
                                last = mm(ps[:, 2 + j % 2, 0:w], qhh[:, h, ds(q0 + r * P, P)],
                                          khl[:, h, ds(b * N + kb * CH, w)], stop=kb < c)
                                if kb == c:
                                    last = mm(ps[:, 2 + j % 2, w - P:w], ident16, neg_qk, start=False)
                                last.then_inc(S["sm_ps"], 1)
                    for h in range(HS):
                        it = 4 * c + 2 * b + h
                        s0 = base + (2 * b + h) * steps
                        pe.wait_ge(S["mneg"], it + 1)
                        pe.wait_ge(S["mrow_sb"], 1 + it)
                        pe.wait_ge(S["gT_sb"], 1 + m)
                        for r in range(4):
                            last = mm(ps[0:DS + 1, 4, r * P:(r + 1) * P], mpad[:, h, r], ident16)
                        last.then_inc(S["mrow_ps"], 1)
                        pe.wait_ge(S["mrow_sb"], 1 + it + 1)

                        def scores(s, u, kt, lo=0, diag=False):
                            pe.wait_ge(S["p_ready"], s + 1)
                            at = ds(b * N + kt * P, P)
                            q = ds(q0 + lo, CH - lo)
                            mm(ps[:, u, lo:], khl[:, h, at], qhh[:, h, q], stop=False)
                            last = mm(ps[:, u, lo:], kh1[:, h, at], ql[:, h, q], start=False, stop=not diag)
                            if diag:
                                last = mm(ps[:, u, lo:lo + P], ident16, neg_kq, start=False)
                            last.then_inc(S["s_ps"], 1)

                        def values(s, u, kt, r0=0, first=False):
                            pe.wait_ge(S["plo_ready"], s + 1 + CR)
                            for r in range(r0, 4):
                                o = ps[:, 6 + r // 2, (r % 2) * VW:(r % 2 + 1) * VW]
                                vt = v16[:, ds(2 * kt + b, 1), h, :].rearrange("p a e -> p (a e)")
                                mm(o, phi[:, u, r * P:(r + 1) * P], vt, start=first and r % 2 == 0)
                                last = mm(o[:, 0:DS + 1], plo[:, u, r * P:(r + 1) * P], vt[:, 0:DS + 1], start=False)
                            last.then_inc(S["pv_done"], 1)

                        scores(s0, 0, 4 * c, 0, True)
                        pe.wait_ge(S["o_used"], 1 + it)
                        for d in range(4):
                            if d < 3:
                                scores(s0 + d + 1, (d + 1) % 2, 4 * c + d + 1, (d + 1) * P, True)
                            elif c:
                                scores(s0 + 4, 0, 0)
                            values(s0 + d, d % 2, 4 * c + d, d, d == 0)

                        def off_block(kb, last_one):
                            for i in range(4):
                                if not (last_one and i == 3):
                                    scores(s0 + 5 + 4 * kb + i, (i + 1) % 2, 4 * kb + i + 1)
                                values(s0 + 4 + 4 * kb + i, i % 2, 4 * kb + i)

                        if c > 1:
                            with pe.Fori(0, c - 1) as kb:
                                off_block(kb, False)
                        if c:
                            off_block(c - 1, True)
                    pe.wait_ge(S["och_ready"], 2 * m + 2)
                    for r in range(4):
                        last = t_.transpose(ps[:, 4, r * P:(r + 1) * P], och[:, r], ident)
                    last.then_inc(S["oT_ps"], 1)
                    pe.wait_ge(S["oT_sb"], m + 1)
                    pe.wait_ge(S["h2_ready"], 1 + m)
                    mm(ps[:, 5, :], wo[:], oT).then_inc(S["y_ps"], 1)
                    pe.wait_ge(S["yhi_ready"], m + 1)
                    for r in range(4):
                        last = mm(ps[:, 4, r * E:(r + 1) * E], y32[:, r * P:(r + 1) * P], wgate[:])
                    last.then_inc(S["lg_ps"], 1)
                    pe.wait_ge(S["gate_ready"], m + 1)
                    for r in range(4):
                        last = t_.transpose(ps[0:E, 4, r * P:(r + 1) * P], gt[:, 3, r], ident)
                    last.then_inc(S["gT_ps"], 1)
                    pe.wait_ge(S["gT_sb"], 1 + m + 1)
                    pe.wait_ge(S["ylo_ready"], m + 1)
                    for r in range(4):
                        last = mm(ps[:, 5, r * D:(r + 1) * D], gT[:, r * P:(r + 1) * P], b2s[:])
                    last.then_inc(S["b2_ps"], 1)
                base += 4 * steps
                mbase += 4 * steps

            pe.wait_ge(S["split_done"], 2 * NPIECE)
            pe.wait_ge(S["ylo_ready"], B * NQ)
            pe.wait_ge(S["p_ready"], base + CR)

            def up(n, f):
                pe.wait_ge(S["hid_ready"], n * FT + f + 1)
                w = ds((n % E) * FF + f * P, P)
                y = ds((n // E) * CH, CH)
                o = ps[:, f % 2, :]
                mm(o, w1hi[:, w], yhi[:, y], stop=False)
                mm(o, w1hi[:, w], ylo[:, y], start=False, stop=False)
                mm(o, w1lo[:, w], yhi[:, y], start=False).then_inc(S["hid_ps"], 1)

            def down(n, f, par):
                pe.wait_ge(S["hlo_ready"], n * FT + f + 1 + CR)
                if f == 0:
                    pe.wait_ge(S["eo_used"], 4 * n + 4)
                wi = (n % E) * FT + f
                for r in range(4):
                    o = ps[:, 2 + par, r * D:(r + 1) * D]
                    hi, lo = hhi[:, f % 2, r * P:(r + 1) * P], hlo[:, f % 2, r * P:(r + 1) * P]
                    whi, wlo = (w2hl[:, ds(wi, 1), z, :].rearrange("p a d -> p (a d)") for z in range(2))
                    mm(o, hi, whi, start=(f == 0 and r == 0), stop=False)
                    mm(o, hi, wlo, start=False, stop=False)
                    last = mm(o, lo, whi, start=False, stop=f == FT - 1)
                last.then_inc(S["w2_done"], 1)

            up(0, 0)
            with pe.Fori(0, NEXP - 3, 2) as n:
                for u in range(2):
                    for f in range(FT):
                        if f < FT - 1:
                            up(n + u, f + 1)
                        else:
                            up(n + u + 1, 0)
                        down(n + u, f, u)
            for u in range(2):
                for f in range(FT):
                    if f < FT - 1:
                        up(NEXP - 2 + u, f + 1)
                    elif u == 0:
                        up(NEXP - 1, 0)
                    down(NEXP - 2 + u, f, u)


def constants():
    c = np.zeros((P, C_END), np.float32)
    i = np.arange(P)
    c[:, C_ID:C_ID + P] = np.eye(P)
    c[:, C_U:C_U + P] = i[:, None] <= i[None, :]
    c[:, C_L:C_L + P] = i[:, None] >= i[None, :]
    c[P - 1, C_LAST:C_LAST + P] = 1.0
    c[:, C_BLK:C_BLK + P] = i[:, None] // DA == i[None, :] // DA
    c[:, C_HEAD:C_HEAD + HA] = i[:, None] // DA == np.arange(HA)[None, :]
    where = np.arange(NT)[None, :] * P + i[:, None] + 1
    c[:, C_INV:C_INV + NT] = 1.0 / where
    place = np.arange(1, N + 1, dtype=np.float32)[:, None]
    k = np.arange(D)
    exponent = (np.where(k % 2 == 0, k, k + 1).astype(np.float32) / np.float32(D)).astype(np.float32)
    angle = (place / np.power(np.float32(10000.0), exponent)).astype(np.float32)
    pe = np.where(k % 2 == 0, np.cos(angle), np.sin(angle)).astype(np.float32)
    c[:, C_POS:C_END] = pe.reshape(NT, P, D).transpose(1, 0, 2).reshape(P, NT * D)
    c16 = np.zeros((P, 3 * P), np.float16)
    c16[:, 0:P] = np.eye(P)
    c16[:, P:2 * P] = np.where(i[None, :] > i[:, None], NEG, 0.0)
    c16[:, 2 * P:] = np.where(i[:, None] > i[None, :], NEG, 0.0)
    return c, c16


def kernel(**inputs):
    import concourse.bacc as _bacc
    from concourse import mybir as _mybir
    from concourse.bass_utils import run_bass_kernel_spmd as _run

    a = {k: np.asarray(v) for k, v in inputs.items()}
    c, c16 = constants()
    rows = np.concatenate([a["L0_tok_b"], a["L0_attn_b_out"], a["L0_ffn_gate_b"],
                           a["L0_attn_norm_g"].reshape(-1), a["L0_attn_norm_b"].reshape(-1)])
    cols = np.concatenate([a["L0_ffn_ln_g"][:, None], a["L0_ffn_ln_b"][:, None],
                           np.tile(a["L0_ffn_qn_g"], 2)[:, None], np.tile(a["L0_ffn_kn_g"], 2)[:, None],
                           a["L0_ffn_b1"].reshape(E * FT, P).T], axis=1)
    arrays = {
        "ids": a["x"].reshape(B, NT, P).transpose(2, 1, 0).reshape(P, T),
        "emb_rows": a["L0_tok_W"].T,
        "consts": c, "consts16": c16,
        "rows": np.broadcast_to(rows[None, :], (P, R_END)),
        "cols": cols,
        "w_qkv": a["L0_attn_w_qkv"], "w_out": a["L0_attn_w_out"],
        "w_sm": np.concatenate([a["L0_ffn_Wq"], a["L0_ffn_Wk"], a["L0_ffn_Wv"]], axis=1),
        "w_o": a["L0_ffn_Wo"], "w_gate": a["L0_ffn_gate_W"],
        "w1": a["L0_ffn_W1"].transpose(1, 0, 2).reshape(D, E * FF),
        "w2": a["L0_ffn_W2"].reshape(E * FT, P, D).transpose(1, 0, 2).reshape(P, E * FT * D),
        "b2": a["L0_ffn_b2"],
    }
    arrays = {k: np.ascontiguousarray(v) for k, v in arrays.items()}
    nc = _bacc.Bacc("TRN2", target_bir_lowering=False, num_devices=1)
    args = [nc.dram_tensor(k, v.shape, _mybir.dt.from_np(v.dtype), kind="ExternalInput").ap()
            for k, v in arrays.items()]
    args.append(nc.dram_tensor("out", (B * N, D), F32, kind="ExternalOutput").ap())
    tower(nc, *args)
    r = _run(nc, [arrays], core_ids=[0])
    return r.results[0]["out"].reshape(B, N, D)
```

```python
from contextlib import ExitStack

import numpy as np

import concourse.bass as bass
from concourse import mybir

F32 = mybir.dt.float32
F16 = mybir.dt.float16
I32 = mybir.dt.int32
ALU = mybir.AluOpType
ACT = mybir.ActivationFunctionType
AX = mybir.AxisListType.X

P = 128
B, N, D = 2, 2048, 128
NT = N // P
T = B * NT
HA, DA = 8, 16
HS, DS = 2, 64
E, FF = 8, 512
FT = FF // P
NQ = N // 512
CH = 512
LN_EPS = 1e-5
DOT_EPS = 1e-8 * D
L2_EPS = 1e-12
NEG = -60000.0
WS = 64.0
VW = 2 * DS + 1

C_ID, C_U, C_L, C_LAST, C_BLK, C_HEAD, C_INV, C_POS = 0, 128, 256, 384, 512, 640, 648, 664
C_END = C_POS + NT * D
R_TB, R_BO, R_GB, R_NG, R_NB = 0, 128, 256, 264, 272
R_END = 280
K_LG, K_LB, K_QG, K_KG, K_B1 = 0, 1, 2, 3, 4
K_END = K_B1 + E * FT


def tower(nc, ids, emb_rows, consts, consts16, rows, cols, w_qkv, w_out, w_sm, w_o, w_gate, w1, w2, b2, out):
    with ExitStack() as ctx:
        def sb(name, shape, dt=F32):
            return ctx.enter_context(nc.sbuf_tensor(name, shape, dt))

        def sem(name):
            return ctx.enter_context(nc.semaphore(name))

        cst = sb("cst", [P, C_END])
        c16 = sb("c16", [P, 3 * P], F16)
        row = sb("row", [P, R_END])
        col = sb("col", [P, K_END])
        idx = sb("idx", [P, T], I32)
        wqkv = sb("wqkv", [P, 3, D])
        wout = sb("wout", [P, D])
        wsm = sb("wsm", [P, 3 * D])
        wo = sb("wo", [P, D])
        wgate = sb("wgate", [P, E])
        b2s = sb("b2s", [E, D])
        ones = sb("ones", [P, 1])
        mhalf = sb("mhalf", [P, 16])
        qkg8 = sb("qkg8", [P, 1])
        eps = sb("eps", [P, 10])
        ln_eps, l2_eps = eps[:, 0:2], eps[:, 2:10]
        credit = sb("credit", [P, 16])
        h_all = sb("h_all", [P, T, D])
        khl = sb("khl", [P, HS, B * N], F16)
        kh1 = sb("kh1", [DS + 1, HS, B * N], F16)
        qhh = sb("qhh", [P, HS, B * N], F16)
        ql = sb("ql", [DS + 1, HS, B * N], F16)
        v16 = sb("v16", [P, T, HS, VW], F16)
        y2 = sb("y2", [P, B * N])
        yhi = y2[:, 0:B * N // 2].bitcast(F16)
        ylo = y2[:, B * N // 2:].bitcast(F16)
        arena = sb("arena", [P, 2 * E * FF])
        w1hi = arena[:, 0:E * FF // 2].bitcast(F16)
        w1lo = arena[:, E * FF // 2:E * FF].bitcast(F16)
        w2hl = arena[:, E * FF:].bitcast(F16).rearrange("p (w z d) -> p w z d", z=2, d=D)

        ident = cst[:, C_ID:C_ID + P]
        upper = cst[:, C_U:C_U + P]
        lower = cst[:, C_L:C_L + P]
        last_row = cst[:, C_LAST:C_LAST + P]
        blk = cst[:, C_BLK:C_BLK + P]
        head = cst[:, C_HEAD:C_HEAD + HA]
        pos = cst[:, C_POS:C_END].rearrange("p (c d) -> p c d", d=D)
        ident16 = c16[:, 0:P]
        neg_qk = c16[:, P:2 * P]
        neg_kq = c16[:, 2 * P:3 * P]

        taken = [0]

        def early(*dims):
            n = int(np.prod(dims))
            piece = arena[:, taken[0]:taken[0] + n]
            taken[0] += n
            assert taken[0] <= 2 * E * FF
            names_ = "abcd"[:len(dims)]
            return piece if len(dims) == 1 else piece.rearrange(
                f"p ({' '.join(names_)}) -> p {' '.join(names_)}", **dict(zip(names_[1:], dims[1:])))

        xn = [early(B, D) for i in range(2)]
        xnT = [early(B, P) for i in range(2)]
        xsT = [early(B, P) for i in range(2)]
        qkT = [early(2, B, P) for i in range(2)]
        qkv = [early(B, 3, D) for i in range(2)]
        hb = [early(B, D) for i in range(2)]
        prod = early(B, 2, D)
        ao = early(B, D)
        ao2 = early(B, D)
        aoT = early(B, P)
        xall = [early(B, 4, D) for i in range(2)]
        st6 = sb("st6", [P, B, 6])
        mv = [sb(f"mv{i}", [P, B, 2]) for i in range(2)]
        rs = [sb(f"rs{i}", [P, B]) for i in range(2)]
        x0 = sb("x0", [P, B])
        sg = sb("sg", [P, B, 2, D])
        ab = sb("ab", [P, B, 2, HA])
        sm = sb("sm", [P, 8, B, HA])
        blkbuf = y2[:, 0:B * HA * P].rearrange("p (b h j) -> p b h j", b=B, h=HA)
        dtm = y2[:, B * HA * P:].rearrange("p (b h j) -> p b h j", b=B, h=HA)
        sq = sb("sq", [P, B, HA, P])
        st2 = sb("st2", [P, 2, B, 6])
        mv2 = [sb(f"mv2{i}", [P, B, 2]) for i in range(2)]
        rr = [sb(f"rr{i}", [P, 4, B]) for i in range(2)]
        x2 = [sb(f"x2{i}", [P, B, D]) for i in range(2)]
        hxT = [sb(f"hxT{i}", [P, B, P]) for i in range(2)]
        qk2 = sb("qk2", [P, B, 4 * DS])
        ss = sb("ss", [P, 2, 3, B * 4])
        qkn = sb("qkn", [P, B, 4, 2, DS])
        mx = sb("mx", [P, 4, NQ])
        mpad = sb("mpad", [P, HS, 4, DS + 1], F16)
        p32 = sb("p32", [P, 3, CH])
        phi = sb("phi", [P, 4, CH], F16)
        plo = sb("plo", [P, 4, CH], F16)
        mall = sb("mall", [P, 4])
        rl = sb("rl", [P, 4])
        ot = sb("ot", [P, 2, 4, DS])
        och = sb("och", [P, 4, D])
        gt = sb("gt", [P, 4, 4, E])
        gl = sb("gl", [P, 4, 4])
        gT = sb("gT", [E, CH])
        sqf = sq[:].rearrange("p b h j -> p (b h j)")
        stage, oT, y32 = sqf[:, 0:1024], sqf[:, 1024:1536], sqf[:, 1536:2048]
        hid = cst[:, C_POS:C_POS + 4 * CH].rearrange("p (u t) -> p u t", u=4)
        hhi = sqf[:, 0:2 * CH].bitcast(F16).rearrange("p (u t) -> p u t", u=4)
        hlo = sqf[:, 2 * CH:4 * CH].bitcast(F16).rearrange("p (u t) -> p u t", u=4)
        gs = sb("gs", [P, B * NQ, 4, E])

        ps = ctx.enter_context(nc.psum_tensor("ps", [P, 8, 512], F32))

        names = """load_c load_w load_s load_stage load_stage1 split_done gathered0 gathered1 gathered setup
            stats veps rstd hb_ready xn_ready xnT_ps xnT_sb x0_link xsT_sb qkT_ps qkT_sb qkv_ps qkv_sb
            blk_ready dt_ps dt_sb sq_ready state_ps sg_ready x_ps var_ready r_ready gr_ready grmu_ready
            coef ao_ready aoT_ps aoT_sb pr_ps h1_ready attn0 attnT0_ps attnT0_sb front_link core_link direct_link
            pos_ready stats2 st2_link rr_link rr_ready x2_ready x2T_ps hxT_sb qkv2_ps sqqk ss_ready rn_link rn_ready
            qkn_ready vhi_ready vlo_ready qkd_ps hi_ready lo_ready kh1_ready
            sm_ps sm_used max_link mneg mrow_ps mrow_sb s_ps p_ready plo_even plo_odd pv_done o_link o_used och_ready
            oT_ps oT_sb y_ps yhi_ready ylo_ready lg_ps lg_link lg_ready eg_ready gate_ready gT_ps gT_sb b2_ps h2_ready
            split_link hid_ps hid_ready hhi_ready hlo_even hlo_odd l2_link x_sb v_link ao_link w2_done eo_used stored"""
        S = {name: sem(name) for name in names.split()}
        NPIECE = (E * FF) // 512
        RING = 4
        QB = [1, 5]
        HBANK = [0, 1, 4, 5]
        NEXP = B * NQ * E
        ds = bass.ds

        block = ctx.enter_context(nc.Block())

        @block.sync
        def _(sp):
            sp.dma_start(idx[:], ids).then_inc(S["load_c"], 16)
            sp.dma_start(row[:], rows).then_inc(S["load_w"], 16)
            sp.dma_start(cst[:], consts).then_inc(S["load_w"], 16)
            sp.dma_start(wqkv[:].rearrange("p a d -> p (a d)"), w_qkv).then_inc(S["load_w"], 16)
            sp.dma_start(col[:], cols).then_inc(S["load_w"], 16)
            sp.dma_start(wout[:], w_out).then_inc(S["load_w"], 16)
            sp.dma_start(wsm[:], w_sm).then_inc(S["load_s"], 16)
            sp.dma_start(c16[:], consts16).then_inc(S["load_s"], 16)
            sp.dma_start(wo[:], w_o).then_inc(S["load_s"], 16)
            sp.dma_start(wgate[:], w_gate).then_inc(S["load_s"], 16)
            sp.dma_start(b2s[:], b2).then_inc(S["load_s"], 16)
            sp.wait_ge(S["h1_ready"], NT)
            for n in range(2 * NPIECE):
                if n >= 2:
                    sp.wait_ge(S["split_done"], n - 1)
                src = (w1 if n < NPIECE else w2)[:, (n % NPIECE) * 512:(n % NPIECE) * 512 + 512]
                sp.dma_start(stage[:, 512 * (n % 2):512 * (n % 2) + 512], src
                             ).then_inc(S["load_stage" if n % 2 == 0 else "load_stage1"], 16)
            for c in range(NQ):
                with sp.Fori(0, B) as b:
                    sp.wait_ge(S["eo_used"], (2 * c + b + 1) * E * 4 + 8)
                    for r in range(4):
                        sp.dma_start(out[ds(b * N + c * CH + r * P, P), :],
                                     h_all[:, ds(8 * c + 2 * r + b, 1), :].rearrange("p a d -> p (a d)")
                                     ).then_inc(S["stored"], 16)
            sp.wait_ge(S["stored"], 16 * 4 * B * NQ)

        @block.gpsimd
        def _(pool):
            g = nc.gpsimd
            pool.wait_ge(S["load_c"], 16)

            def gather(t0, t1):
                for t in range(t0, t1):
                    g.indirect_dma_start(out=h_all[:, t, :], out_offset=None, in_=emb_rows,
                                         in_offset=bass.IndirectOffsetOnAxis(ap=idx[:, t:t + 1], axis=0)
                                         ).then_inc(S["gathered0" if t < B else "gathered1" if t < 8 else "gathered"], 16)

            gather(0, B)
            g.memset(mhalf[:], -0.5).then_inc(S["setup"], 1)
            g.memset(ln_eps, LN_EPS).then_inc(S["setup"], 1)
            g.memset(l2_eps, L2_EPS).then_inc(S["setup"], 1)
            g.memset(v16[:, :, :, DS:DS + 1], 1.0).then_inc(S["setup"], 1)
            g.memset(mpad[:], 0.0).then_inc(S["setup"], 1)
            g.memset(ones[:], 1.0).then_inc(S["setup"], 1)
            gather(B, 9)
            pool.wait_ge(S["setup"], 6)
            pool.wait_ge(S["load_w"], 80)

            def front(c, par):
                pool.wait_ge(S["stats"], c + 1)
                g.tensor_tensor(rs[par][:], mv[par][:, :, 1], ln_eps, ALU.add).then_inc(S["veps"], 1)
                pool.wait_ge(S["veps"], c + 1)
                g.tensor_tensor(rs[par][:], rs[par][:], mhalf[:, 0:B], ALU.pow).then_inc(S["rstd"], 1)

            def out_bias(c, par, first=False):
                if not first:
                    pool.wait_ge(S["h1_ready"], c - 1)
                g.tensor_tensor(hb[par], h_all[:, ds(2 * c, 2), :],
                                row[:, R_BO:R_BO + D].unsqueeze(1).to_broadcast([P, B, D]),
                                ALU.add).then_inc(S["hb_ready"], 1)

            def shifted(c, par):
                pool.wait_ge(S["xnT_sb"], c + 1)
                g.tensor_tensor(xsT[par], xnT[par], x0[:].unsqueeze(2).to_broadcast([P, B, P]), ALU.subtract
                                ).then_inc(S["xsT_sb"], 1)

            def q_blocks(c, par, first=False):
                pool.wait_ge(S["qkT_sb"], c + 1)
                for b in range(B):
                    if not first:
                        pool.wait_ge(S["dt_ps"], 2 * c + b - 1)
                    g.tensor_tensor(blkbuf[:, b],
                                    qkT[par][:, 1 if first else 0, b, :].unsqueeze(1).to_broadcast([P, HA, P]),
                                    head.unsqueeze(2).to_broadcast([P, HA, P]), ALU.mult
                                    ).then_inc(S["blk_ready"], 1)

            def coefs(c):
                pool.wait_ge(S["var_ready"], c + 1)
                g.tensor_tensor(sm[:, 4], sm[:, 3], mhalf[:].rearrange("p (b h) -> p b h", b=B),
                                ALU.pow).then_inc(S["r_ready"], 1)
                pool.wait_ge(S["r_ready"], c + 1)
                g.tensor_tensor(sm[:, 5], sm[:, 4], row[:, R_NG:R_NG + HA].unsqueeze(1).to_broadcast([P, B, HA]),
                                ALU.mult).then_inc(S["gr_ready"], 1)
                pool.wait_ge(S["gr_ready"], c + 1)
                g.tensor_tensor(sm[:, 6], sm[:, 5], sm[:, 0], ALU.mult).then_inc(S["grmu_ready"], 1)
                pool.wait_ge(S["grmu_ready"], c + 1)
                g.tensor_tensor(sm[:, 7], row[:, R_NB:R_NB + HA].unsqueeze(1).to_broadcast([P, B, HA]), sm[:, 6],
                                ALU.subtract).then_inc(S["coef"], 1)

            front(0, 0)
            gather(9, 11)
            pool.wait_ge(S["x0_link"], 2)
            shifted(0, 0)
            gather(11, 13)
            front(1, 1)
            q_blocks(0, 0, first=True)
            shifted(1, 1)
            out_bias(0, 0, first=True)
            gather(13, 14)
            q_blocks(1, 1)
            out_bias(1, 1, first=True)
            gather(14, 22)
            coefs(0)
            gather(22, 24)
            front(2, 0)

            def step_a(c, nxt, more=2, tail=True):
                if more:
                    shifted(c + 1, nxt)
                if tail:
                    coefs(c - 1)
                else:
                    gather(24, 28)
                if more:
                    q_blocks(c + 1, nxt)
                if not tail:
                    gather(28, T)
                if more >= 2:
                    front(c + 2, 1 - nxt)
                if tail:
                    out_bias(c, 1 - nxt)

            step_a(1, 0, tail=False)
            with pool.Fori(2, NT - 3, 2) as c:
                for u in range(2):
                    step_a(c + u, 1 - u)
            step_a(NT - 2, 1, more=1)
            step_a(NT - 1, 0, more=0)
            coefs(NT - 1)

            def both_norms(c, par):
                pool.wait_ge(S["stats2"], c + 1)
                k = 5 * c
                var = mv2[par][:, :, 1]
                a, b_, c_ = rr[par][:, 0], rr[par][:, 1], rr[par][:, 2]
                g.tensor_tensor(a, var, ln_eps, ALU.add).then_inc(S["rr_link"], 1)
                pool.wait_ge(S["rr_link"], k + 1)
                g.tensor_tensor(b_, a, mhalf[:, 0:B], ALU.pow).then_inc(S["rr_link"], 1)
                pool.wait_ge(S["rr_link"], k + 2)
                g.tensor_tensor(a, var, b_, ALU.mult).then_inc(S["rr_link"], 1)
                pool.wait_ge(S["rr_link"], k + 3)
                g.tensor_tensor(c_, a, b_, ALU.mult).then_inc(S["rr_link"], 1)
                pool.wait_ge(S["rr_link"], k + 4)
                g.tensor_tensor(c_, c_, ln_eps, ALU.add).then_inc(S["rr_link"], 1)
                pool.wait_ge(S["rr_link"], k + 5)
                g.tensor_tensor(a, c_, mhalf[:, 0:B], ALU.pow).then_inc(S["rn_link"], 1)
                pool.wait_ge(S["rn_link"], c + 1)
                g.tensor_tensor(rr[par][:, 3], a, b_, ALU.mult).then_inc(S["rr_ready"], 1)

            def l2_factors(c, par):
                pool.wait_ge(S["ss_ready"], c + 1)
                g.tensor_tensor(ss[:, par, 1], ss[:, par, 0], l2_eps, ALU.add).then_inc(S["l2_link"], 1)
                pool.wait_ge(S["l2_link"], c + 1)
                g.tensor_tensor(ss[:, par, 2], ss[:, par, 1], mhalf[:, 0:8], ALU.pow).then_inc(S["rn_ready"], 1)

            for i in range(3):
                both_norms(i, i % 2)
            l2_factors(0, 0)

            def step_a2(c, par, left=3):
                if left >= 1:
                    l2_factors(c + 1, 1 - par)
                if left >= 3:
                    both_norms(c + 3, 1 - par)

            with pool.Fori(0, NT - 5, 2) as c:
                for u in range(2):
                    step_a2(c + u, u)
            for c in range(NT - 4, NT):
                step_a2(c, c % 2, NT - 1 - c)

            def split_op(n, op):
                o = (n % NPIECE) * 512
                st_ = stage[:, 512 * (n % 2):512 * (n % 2) + 512]
                if n < NPIECE:
                    hi, lo = w1hi[:, o:o + 512], w1lo[:, o:o + 512]
                else:
                    st_ = st_.rearrange("p (a d) -> p a d", d=D)
                    hi, lo = (w2hl[:, o // D:o // D + 4, part, :] for part in range(2))
                if op == 0:
                    pool.wait_ge(S["load_stage"] if n % 2 == 0 else S["load_stage1"], 16 * (n // 2 + 1))
                    g.tensor_scalar(st_, st_, WS, None, ALU.mult).then_inc(S["split_link"], 1)
                elif op == 1:
                    pool.wait_ge(S["split_link"], 2 * n + 1)
                    g.tensor_copy(hi, st_).then_inc(S["split_link"], 1)
                else:
                    pool.wait_ge(S["split_link"], 2 * n + 2)
                    g.tensor_tensor(lo, st_, hi, ALU.subtract).then_inc(S["split_done"], 1)

            ops = 0
            for k, (it, kt, r0, diag) in enumerate(STEPS):
                if k % 2 == 0:
                    lo = r0 * P
                    pool.wait_ge(S["p_ready"], k + 1)
                    if k >= 4:
                        pool.wait_ge(S["pv_done"], k - 3)
                    g.tensor_tensor(plo[:, k % 4, lo:], p32[:, k % 3, lo:], phi[:, k % 4, lo:], ALU.subtract
                                    ).then_inc(S["plo_even"], 1)
                    if ops < 6 * NPIECE:
                        split_op(ops // 3, ops % 3)
                        ops += 1
            assert ops == 6 * NPIECE

            with pool.Fori(0, NEXP) as n:
                for f in range(0, FT, 2):
                    pool.wait_ge(S["hhi_ready"], n * FT + f + 1)
                    pool.wait_ge(S["w2_done"], n * FT + f + 1)
                    g.tensor_tensor(hlo[:, f], hid[:, f], hhi[:, f], ALU.subtract).then_inc(S["hlo_even"], 1)

        @block.scalar
        def _(act):
            a = nc.scalar

            def front(c, par):
                act.wait_ge(S["xnT_ps"], c + 1)
                a.copy(xnT[par].rearrange("p b t -> p (b t)"), ps[:, 0, 0:B * P]).then_inc(S["xnT_sb"], 1)
                queries_keys(c, par)

            def queries_keys(c, par, read=False):
                act.wait_ge(S["qkT_ps"], c + 1)
                a.copy(qkT[par].rearrange("p a b t -> p (a b t)"), ps[:, 1, :]).then_inc(S["qkT_sb"], 1)
                if read:
                    act.wait_ge(S["var_ready"], c - 1)
                for b in range(B):
                    act.wait_ge(S["qkv_ps"], 2 * c + b + 1)
                    a.copy(qkv[par][:, b].rearrange("p a d -> p (a d)"), ps[:, 2, 0:3 * D]).then_inc(S["qkv_sb"], 1)

            def sums_out(c, cur, first=False):
                act.wait_ge(S["x_ps"], 2 * c + 2)
                if not first:
                    act.wait_ge(S["ao_ready"], c)
                if first:
                    a.copy(xall[cur][:, :, 0:2, :], ps[:, 5:7, 0:2 * D].rearrange("p b (a d) -> p b a d", d=D))
                    a.copy(xall[cur][:, :, 3, :], ps[:, 5:7, 3 * D:]).then_inc(S["x_sb"], 1)
                else:
                    a.copy(xall[cur].rearrange("p b a d -> p b (a d)"), ps[:, 5:7, :]).then_inc(S["x_sb"], 1)

            def ao_out(c):
                act.wait_ge(S["aoT_ps"], c + 1)
                a.copy(aoT.rearrange("p b t -> p (b t)"), ps[:, 0, B * P:]).then_inc(S["aoT_sb"], 1)

            a.preload_act_table(ACT.Exp)
            front(0, 0)
            front(1, 1)
            for b in range(B):
                act.wait_ge(S["attnT0_ps"], b + 1)
                act.wait_ge(S["sq_ready"], b + 1)
                a.copy(dtm[:, b].rearrange("p (z h) j -> p z (h j)", z=2), ps[:, 3:5, :]).then_inc(S["attnT0_sb"], 1)
            sums_out(0, 0, first=True)

            def step_a(c, nxt, more=True, first=False):
                if not first:
                    sums_out(c - 1, nxt)
                if more:
                    act.wait_ge(S["xnT_ps"], c + 2)
                    a.copy(xnT[nxt].rearrange("p b t -> p (b t)"), ps[:, 0, 0:B * P]).then_inc(S["xnT_sb"], 1)
                    queries_keys(c + 1, nxt, read=not first)
                ao_out(c - 1)

            step_a(1, 0, first=True)
            with act.Fori(2, NT - 3, 2) as c:
                for u in range(2):
                    step_a(c + u, 1 - u)
            step_a(NT - 2, 1)
            step_a(NT - 1, 0, more=False)
            sums_out(NT - 1, 1)
            ao_out(NT - 1)

            def normed_T(c, par):
                act.wait_ge(S["x2T_ps"], c + 1)
                a.activation(hxT[par][:].rearrange("p b t -> p (b t)"), ps[:, 0, 0:B * P],
                             ACT.Identity, bias=col[:, K_LB:K_LB + 1], scale=col[:, K_LG:K_LG + 1]
                             ).then_inc(S["hxT_sb"], 1)

            def squares(c, par, first=False):
                act.wait_ge(S["qkv2_ps"], c + 1)
                if not first:
                    act.wait_ge(S["ss_ready"], c)
                a.activation(qk2[:], ps[:, QB[par]:QB[par] + B, 0:2 * D], ACT.Square).then_inc(S["sqqk"], 1)
                a.copy(v16[:, ds(2 * c, B), :, 0:DS],
                       ps[:, QB[par]:QB[par] + B, 2 * D:3 * D].rearrange("p b (h d) -> p b h d", h=HS)).then_inc(S["vhi_ready"], 1)

            def high_qk(c):
                for b in range(B):
                    act.wait_ge(S["qkd_ps"], 2 * c + b + 1)
                    at = ds(b * N + c * P, P)
                    a.activation(qhh[:, :, at], ps[:, 3 + b, 0:2 * P].rearrange("p (h t) -> p h t", h=HS),
                                 ACT.Copy, scale=qkg8[:])
                    a.activation(kh1[0:DS, :, at], ps[0:DS, 3 + b, 2 * P:4 * P].rearrange("p (h t) -> p h t", h=HS),
                                 ACT.Copy, scale=col[0:DS, K_KG:K_KG + 1])
                    a.activation(khl[:, :, at], ps[:, 3 + b, 2 * P:4 * P].rearrange("p (h t) -> p h t", h=HS),
                                 ACT.Copy, scale=col[:, K_KG:K_KG + 1]).then_inc(S["hi_ready"], 1)

            normed_T(0, 0)
            normed_T(1, 1)
            squares(0, 0, first=True)

            def step_a2(c, par, left=3):
                if left >= 1:
                    squares(c + 1, 1 - par)
                high_qk(c)
                if left >= 2:
                    normed_T(c + 2, par)

            with act.Fori(0, NT - 5, 2) as c:
                for u in range(2):
                    step_a2(c + u, u)
            for c in range(NT - 4, NT):
                step_a2(c, c % 2, NT - 1 - c)

            def max_row(it):
                c, b, h = ITEMS[it]
                act.wait_ge(S["mrow_ps"], it + 1)
                a.copy(ql[DS:DS + 1, h, b * N + c * CH:b * N + (c + 1) * CH], ps[DS:DS + 1, 4, :]
                       ).then_inc(S["mrow_sb"], 1)

            max_row(0)
            for k in range(NSTEP + LAG + 5 * YGAP + 3):
                if k < NSTEP:
                    it, kt, r0, diag = STEPS[k]
                    lo = r0 * P
                    act.wait_ge(S["s_ps"], k + 1)
                    if k >= 3:
                        act.wait_ge(S["plo_even" if (k - 3) % 2 == 0 else "plo_odd"], (k - 3) // 2 + 1)
                    if k >= 4:
                        act.wait_ge(S["pv_done"], k - 3)
                    a.activation(p32[:, k % 3, lo:], ps[:, k % 2, lo:], ACT.Exp)
                    a.activation(phi[:, k % 4, lo:], ps[:, k % 2, lo:], ACT.Exp).then_inc(S["p_ready"], 1)
                    if k + 2 in FIRST:
                        max_row(FIRST.index(k + 2))
                for m in range(B * NQ):
                    j = (k - YAT[m]) / YGAP
                    if j == 1:
                        act.wait_ge(S["oT_ps"], m + 1)
                        a.copy(oT, ps[:, 4, :]).then_inc(S["oT_sb"], 1)
                    if j == 2:
                        act.wait_ge(S["y_ps"], m + 1)
                        a.copy(y32, ps[:, 5, :])
                        a.copy(yhi[:, m * CH:(m + 1) * CH], ps[:, 5, :]).then_inc(S["yhi_ready"], 1)
                    if j == 3:
                        act.wait_ge(S["lg_ready"], m + 1)
                        a.activation(gt[:, 1], gt[:, 0], ACT.Exp).then_inc(S["eg_ready"], 1)
                    if j == 4:
                        act.wait_ge(S["gT_ps"], m + 1)
                        a.copy(gT[:], ps[0:E, 4, :]).then_inc(S["gT_sb"], 1)

            a.preload_act_table(ACT.Gelu_apprx_tanh)
            with act.Fori(0, NEXP) as n:
                for f in range(FT):
                    act.wait_ge(S["hid_ps"], n * FT + f + 1)
                    act.wait_ge(S["hlo_even" if f % 2 == 0 else "hlo_odd"], 2 * n + f // 2 + 1)
                    a.activation(hid[:, f], ps[:, HBANK[f], :], ACT.Gelu_apprx_tanh,
                                 bias=col[:, ds(K_B1 + (n % E) * FT + f, 1)], scale=1.0 / WS
                                 ).then_inc(S["hid_ready"], 1)

        @block.vector
        def _(dve):
            v = nc.vector

            for i, (name, size) in enumerate([("hid_ready", RING), ("w2_done", RING), ("hlo_even", 2), ("hlo_odd", 2),
                                              ("eo_used", 8), ("qkn_ready", 1), ("lo_ready", 1), ("vlo_ready", 1)]):
                v.memset(credit[:, i:i + 1], 0.0).then_inc(S[name], size)
            v.memset(kh1[DS:DS + 1, :, :], 1.0).then_inc(S["pos_ready"], 1)
            dve.wait_ge(S["load_w"], 80)
            v.tensor_scalar(qkg8[:], col[:, K_QG:K_QG + 1], float(DS) ** 0.5, None, ALU.mult).then_inc(S["pos_ready"], 1)
            v.tensor_tensor(pos, pos, row[:, R_TB:R_TB + D].unsqueeze(1).to_broadcast([P, NT, D]),
                            ALU.add).then_inc(S["pos_ready"], 1)
            dve.wait_ge(S["pos_ready"], 3)

            def embed(c, par):
                h = h_all[:, ds(2 * c, 2), :]
                v.tensor_tensor(h, h, cst[:, ds(C_POS + c * D, D)].unsqueeze(1).to_broadcast([P, B, D]),
                                ALU.add).then_inc(S["front_link"], 1)
                dve.wait_ge(S["front_link"], 2 * c + 1)
                v.memset(credit[:, 13:14], 0.0)
                for b in range(B):
                    last = v.bn_stats(st6[:, b], h_all[:, ds(2 * c + b, 1), :].rearrange("p a d -> p (a d)"))
                last.then_inc(S["front_link"], 1)
                dve.wait_ge(S["front_link"], 2 * c + 2)
                v.memset(credit[:, 13:14], 0.0)
                for b in range(B):
                    last = v.bn_aggr(mv[par][:, b], st6[:, b])
                last.then_inc(S["stats"], 1)

            def normed(c, par):
                dve.wait_ge(S["rstd"], c + 1)
                dve.wait_ge(S["stats"], c + 1)
                for b in range(B):
                    last = v.tensor_scalar(xn[par][:, b], h_all[:, ds(2 * c + b, 1), :].rearrange("p a d -> p (a d)"),
                                           mv[par][:, b, 0:1], rs[par][:, b:b + 1], ALU.subtract, ALU.mult)
                last.then_inc(S["xn_ready"], 1)

            def state_out(c):
                dve.wait_ge(S["state_ps"], 2 * c + B)
                for b in range(B):
                    v.tensor_tensor(sg[:, b], ps[:, 7, b * 2 * D:(b + 1) * 2 * D].rearrange("p (a d) -> p a d", d=D),
                                    blk.unsqueeze(1).to_broadcast([P, 2, D]), ALU.mult).then_inc(S["sg_ready"], 1)

            def h1_out(c, par):
                dve.wait_ge(S["pr_ps"], c + 1)
                dve.wait_ge(S["hb_ready"], c + 1)
                v.tensor_tensor(h_all[:, ds(2 * c, 2), :], ps[:, 0, B * P:].rearrange("p (b d) -> p b d", b=B),
                                hb[par], ALU.add).then_inc(S["h1_ready"], 1)

            dve.wait_ge(S["gathered0"], 16 * B)
            embed(0, 0)
            normed(0, 0)
            dve.wait_ge(S["gathered1"], 16 * (8 - B))
            embed(1, 1)
            dve.wait_ge(S["xnT_sb"], 1)
            v.tensor_reduce(x0[:], xnT[0], AX, ALU.add
                            ).then_inc(S["x0_link"], 1)
            dve.wait_ge(S["x0_link"], 1)
            v.tensor_scalar(x0[:], x0[:], 1.0 / P, None, ALU.mult).then_inc(S["x0_link"], 1)
            normed(1, 1)
            links = 0

            def link(ins):
                nonlocal links
                links += 1
                ins.then_inc(S["direct_link"], 1)
                dve.wait_ge(S["direct_link"], links)

            low_h = lower.unsqueeze(1).to_broadcast([P, HA, P])
            inv0 = cst[:, C_INV:C_INV + 1]
            for b in range(B):
                dve.wait_ge(S["dt_ps"], b + 1)
                v.tensor_tensor(dtm[:, b], ps[:, 3:5, :].rearrange("p z (h j) -> p (z h) j", j=P), low_h,
                                ALU.mult).then_inc(S["dt_sb"], 1)
            for b in range(B):
                dve.wait_ge(S["dt_sb"], b + 1)
                link(v.tensor_reduce(sm[:, 1, b], dtm[:, b], AX, ALU.add))
                link(v.tensor_scalar(sm[:, 0, b], sm[:, 1, b], inv0, None, ALU.mult))
                link(v.tensor_tensor(sq[:, b], dtm[:, b], sm[:, 0, b].unsqueeze(2).to_broadcast([P, HA, P]), ALU.subtract))
                v.tensor_tensor(dtm[:, b], sq[:, b], low_h, ALU.mult).then_inc(S["attn0"], 1)
                dve.wait_ge(S["attn0"], b + 1)
                v.tensor_tensor(sq[:, b], dtm[:, b], dtm[:, b], ALU.mult).then_inc(S["sq_ready"], 1)
                dve.wait_ge(S["sq_ready"], b + 1)
                link(v.tensor_reduce(sm[:, 1, b], sq[:, b], AX, ALU.add))
            v.tensor_scalar(sm[:, 3], sm[:, 1], inv0, DOT_EPS, ALU.mult, ALU.add).then_inc(S["var_ready"], 1)
            state_out(0)

            def outputs(c, cur, first=False):
                dve.wait_ge(S["coef"], c + 1)
                if first:
                    dve.wait_ge(S["x_sb"], 1)
                shift = row[:, R_NB:R_NB + HA].unsqueeze(1).to_broadcast([P, B, HA]) if first else sm[:, 7]
                v.tensor_tensor(ao.rearrange("p b (h e) -> p b h e", e=DA),
                                xall[cur][:, :, 3, :].rearrange("p b (h e) -> p b h e", e=DA),
                                sm[:, 5].unsqueeze(3).to_broadcast([P, B, HA, DA]), ALU.mult)
                v.tensor_tensor(ao2.rearrange("p b (h e) -> p b h e", e=DA),
                                xall[cur][:, :, 1, :].rearrange("p b (h e) -> p b h e", e=DA),
                                shift.unsqueeze(3).to_broadcast([P, B, HA, DA]), ALU.mult
                                ).then_inc(S["ao_link"], 1)
                dve.wait_ge(S["ao_link"], c + 1)
                v.tensor_tensor(ao, ao, ao2, ALU.add).then_inc(S["ao_ready"], 1)

            def variances(c, cur):
                k = 4 * (c - 1)
                dve.wait_ge(S["x_sb"], c + 1)
                q = qkv[cur][:, :, 0, :]
                v.tensor_tensor(prod, xall[cur].rearrange("p b (a z) d -> p b a z d", z=2)[:, :, :, 0, :],
                                q.unsqueeze(2).to_broadcast([P, B, 2, D]), ALU.mult).then_inc(S["core_link"], 1)
                dve.wait_ge(S["core_link"], k + 1)
                v.tensor_reduce(ab[:].rearrange("p b a h -> p (b a h)"),
                                prod.rearrange("p b a (h e) -> p (b a h) e", e=DA), AX, ALU.add
                                ).then_inc(S["core_link"], 1)
                dve.wait_ge(S["core_link"], k + 2)
                inv = cst[:, ds(C_INV + c, 1)]
                v.tensor_scalar(sm[:, 0], ab[:, :, 0], inv, None, ALU.mult).then_inc(S["core_link"], 1)
                dve.wait_ge(S["core_link"], k + 3)
                v.tensor_tensor(sm[:, 2], sm[:, 0], sm[:, 0], ALU.mult).then_inc(S["core_link"], 1)
                dve.wait_ge(S["core_link"], k + 4)
                v.scalar_tensor_tensor(sm[:, 1], ab[:, :, 1], inv, sm[:, 2].rearrange("p b h -> p b h"), ALU.mult, ALU.subtract
                                       ).then_inc(S["v_link"], 1)
                dve.wait_ge(S["v_link"], c)
                v.tensor_scalar(sm[:, 3], sm[:, 1], 0.0, DOT_EPS, ALU.max, ALU.add).then_inc(S["var_ready"], 1)

            def step_a(c, nxt, more=2, first=False):
                cur = 1 - nxt
                for b in range(B):
                    if b:
                        if more:
                            normed(c + 1, nxt)
                        if not first:
                            variances(c - 1, nxt)
                        if more >= 2:
                            embed(c + 2, cur)
                    dve.wait_ge(S["dt_ps"], 2 * c + b + 1)
                    dve.wait_ge(S["x_ps"], 2 * c + b - 1)
                    v.tensor_tensor(dtm[:, b], ps[:, 3:5, :].rearrange("p z (h j) -> p (z h) j", j=P),
                                    upper.unsqueeze(1).to_broadcast([P, HA, P]), ALU.mult).then_inc(S["dt_sb"], 1)
                state_out(c)
                outputs(c - 1, nxt, first)
                h1_out(c - 1, nxt)

            embed(2, 0)
            step_a(1, 0, first=True)
            dve.wait_ge(S["gathered"], 16 * (T - 8))
            with dve.Fori(2, NT - 3, 2) as c:
                for u in range(2):
                    step_a(c + u, 1 - u)
            step_a(NT - 2, 1, more=1)
            step_a(NT - 1, 0, more=0)
            variances(NT - 1, 1)
            outputs(NT - 1, 1)
            h1_out(NT - 1, 1)

            def stats2(c, par):
                for b in range(B):
                    last = v.bn_stats(st2[:, par, b], h_all[:, ds(2 * c + b, 1), :].rearrange("p a d -> p (a d)"))
                last.then_inc(S["st2_link"], 1)
                dve.wait_ge(S["st2_link"], c + 1)
                v.memset(credit[:, 13:14], 0.0)
                for b in range(B):
                    last = v.bn_aggr(mv2[par][:, b], st2[:, par, b])
                last.then_inc(S["stats2"], 1)

            def normed2(c, par):
                dve.wait_ge(S["rr_ready"], c + 1)
                for b in range(B):
                    last = v.tensor_scalar(x2[par][:, b], h_all[:, ds(2 * c + b, 1), :].rearrange("p a d -> p (a d)"),
                                           mv2[par][:, b, 0:1], rr[par][:, 3, b:b + 1], ALU.subtract, ALU.mult)
                last.then_inc(S["x2_ready"], 1)

            def sum_squares(c, par):
                dve.wait_ge(S["sqqk"], c + 1)
                v.tensor_reduce(ss[:, par, 0], qk2[:].rearrange("p b (g e) -> p (b g) e", e=DS), AX, ALU.add
                                ).then_inc(S["ss_ready"], 1)

            def low_v(c, par):
                dve.wait_ge(S["vhi_ready"], c + 1)
                v.tensor_tensor(v16[:, ds(2 * c, B), :, DS + 1:],
                                ps[:, QB[par]:QB[par] + B, 2 * D:3 * D].rearrange("p b (h e) -> p b h e", h=HS),
                                v16[:, ds(2 * c, B), :, 0:DS], ALU.subtract).then_inc(S["vlo_ready"], 1)

            def unit_qk(c, par):
                dve.wait_ge(S["rn_ready"], c + 1)
                for b in range(B):
                    v.tensor_tensor(qkn[:, b], ps[:, QB[par] + b, 0:2 * D].rearrange("p (g e) -> p g e", e=DS)
                                    .unsqueeze(2).to_broadcast([P, 4, 2, DS]),
                                    ss[:, par, 2, 4 * b:4 * b + 4].unsqueeze(2).unsqueeze(3)
                                    .to_broadcast([P, 4, 2, DS]), ALU.mult).then_inc(S["qkn_ready"], 1)

            def low_qk(c):
                for b in range(B):
                    at = ds(b * N + c * P, P)
                    dve.wait_ge(S["hi_ready"], 2 * c + b + 1)
                    v.scalar_tensor_tensor(ql[0:DS, :, at], ps[0:DS, 3 + b, 0:2 * P].rearrange("p (h t) -> p h t", h=HS),
                                           qkg8[0:DS], qhh[0:DS, :, at], ALU.mult, ALU.subtract)
                    v.scalar_tensor_tensor(khl[DS:, :, at], ps[DS:, 3 + b, 2 * P:].rearrange("p (h t) -> p h t", h=HS),
                                           col[DS:, K_KG:K_KG + 1], khl[DS:, :, at], ALU.mult, ALU.subtract
                                           ).then_inc(S["lo_ready"], 1)

            dve.wait_ge(S["h1_ready"], NT)
            for i in range(2):
                stats2(i, i)
            normed2(0, 0)
            stats2(2, 0)
            normed2(1, 1)
            sum_squares(0, 0)
            low_v(0, 0)

            def step_a2(c, par, left=3):
                unit_qk(c, par)
                if left >= 2:
                    normed2(c + 2, par)
                if left >= 1:
                    sum_squares(c + 1, 1 - par)
                if left >= 3:
                    stats2(c + 3, 1 - par)
                low_qk(c)
                if left >= 1:
                    low_v(c + 1, 1 - par)

            with dve.Fori(0, NT - 5, 2) as c:
                for u in range(2):
                    step_a2(c + u, u)
            for c in range(NT - 4, NT):
                step_a2(c, c % 2, NT - 1 - c)

            def row_max(it, part):
                r, kb, w, k = part
                dve.wait_ge(S["sm_ps"], k + 1)
                v.tensor_reduce(mx[:, r, kb:kb + 1], ps[:, 2 + k % 2, 0:w], AX, ALU.max).then_inc(S["sm_used"], 1)
                c, _, h = ITEMS[it]
                if (r, kb) == (3, c):
                    dve.wait_ge(S["sm_used"], k + 1)
                    v.tensor_reduce(mall[:], mx[:, :, 0:c + 1], AX, ALU.max).then_inc(S["max_link"], 1)
                    dve.wait_ge(S["max_link"], it + 1)
                    if it >= HS:
                        dve.wait_ge(S["mrow_ps"], it - 1)
                    v.tensor_scalar(mpad[:, h, :, DS], mall[:], -1.0, None, ALU.mult).then_inc(S["mneg"], 1)

            def head_out(it):
                c, b, h = ITEMS[it]
                m = it // HS
                dve.wait_ge(S["pv_done"], (FIRST + [NSTEP])[it + 1])
                if h == 0 and m:
                    dve.wait_ge(S["oT_ps"], m)
                o = ps[:, 6:8, 0:2 * VW].rearrange("p a (z e) -> p a z e", e=VW)
                rlv = rl[:].rearrange("p (a z) -> p a z", a=2)
                v.reciprocal(rlv, o[:, :, :, DS]).then_inc(S["o_link"], 1)
                dve.wait_ge(S["o_link"], it + 1)
                rlb = rlv.unsqueeze(3).to_broadcast([P, 2, 2, DS])
                v.tensor_tensor(ot[:, 0].rearrange("p (a z) e -> p a z e", a=2), o[:, :, :, DS + 1:], rlb, ALU.mult)
                v.tensor_tensor(ot[:, 1].rearrange("p (a z) e -> p a z e", a=2), o[:, :, :, 0:DS], rlb,
                                ALU.mult).then_inc(S["o_used"], 1)
                dve.wait_ge(S["o_used"], it + 1)
                v.tensor_tensor(och[:, :, h * DS:(h + 1) * DS], ot[:, 0], ot[:, 1], ALU.add
                                ).then_inc(S["och_ready"], 1)

            for part in MPARTS[0]:
                row_max(0, part)
            for k in range(NSTEP + LAG + 5 * YGAP + 3):
                for it, part in MSLOT.get(k, ()):
                    row_max(it, part)
                if k < NSTEP and k % 2:
                    lo = STEPS[k][2] * P
                    dve.wait_ge(S["p_ready"], k + 1)
                    if k >= 4:
                        dve.wait_ge(S["pv_done"], k - 3)
                    v.tensor_tensor(plo[:, k % 4, lo:], p32[:, k % 3, lo:], phi[:, k % 4, lo:], ALU.subtract
                                    ).then_inc(S["plo_odd"], 1)
                for it in range(len(ITEMS)):
                    if k == OAT[it]:
                        head_out(it)
                for m in range(B * NQ):
                    j = (k - YAT[m]) / YGAP
                    if j == 2:
                        dve.wait_ge(S["yhi_ready"], m + 1)
                        v.tensor_tensor(ylo[:, m * CH:(m + 1) * CH], ps[:, 5, :], yhi[:, m * CH:(m + 1) * CH],
                                        ALU.subtract).then_inc(S["ylo_ready"], 1)
                    if j == 3:
                        dve.wait_ge(S["lg_ps"], m + 1)
                        v.tensor_tensor(gt[:, 2], ps[:, 4, 0:4 * E].rearrange("p (r e) -> p r e", e=E),
                                        row[:, R_GB:R_GB + E].unsqueeze(1).to_broadcast([P, 4, E]), ALU.add
                                        ).then_inc(S["lg_link"], 1)
                        dve.wait_ge(S["lg_link"], 5 * m + 1)
                        v.tensor_reduce(gl[:, 0], gt[:, 2], AX, ALU.max).then_inc(S["lg_link"], 1)
                        dve.wait_ge(S["lg_link"], 5 * m + 2)
                        v.tensor_tensor(gt[:, 0], gt[:, 2], gl[:, 0].unsqueeze(2).to_broadcast([P, 4, E]), ALU.subtract
                                        ).then_inc(S["lg_ready"], 1)
                    if j == 4:
                        dve.wait_ge(S["eg_ready"], m + 1)
                        v.tensor_reduce(gl[:, 1], gt[:, 1], AX, ALU.add).then_inc(S["lg_link"], 1)
                        dve.wait_ge(S["lg_link"], 5 * m + 3)
                        v.reciprocal(gl[:, 2], gl[:, 1]).then_inc(S["lg_link"], 1)
                        dve.wait_ge(S["lg_link"], 5 * m + 4)
                        if m:
                            dve.wait_ge(S["gT_ps"], m)
                        v.tensor_tensor(gt[:, 3], gt[:, 1], gl[:, 2].unsqueeze(2).to_broadcast([P, 4, E]), ALU.mult
                                        ).then_inc(S["gate_ready"], 1)
                        dve.wait_ge(S["gate_ready"], m + 1)
                        v.tensor_scalar(gs[:, m], gt[:, 3], 1.0 / WS, None, ALU.mult).then_inc(S["lg_link"], 1)
                    if j == 5:
                        dve.wait_ge(S["b2_ps"], m + 1)
                        hc = h_all[:, ds(8 * (m // 2) + m % 2, 4, step=2), :]
                        v.tensor_tensor(hc, ps[:, 5, :].rearrange("p (r d) -> p r d", r=4), hc, ALU.add
                                        ).then_inc(S["h2_ready"], 1)
            dve.wait_ge(S["h2_ready"], B * NQ)
            dve.wait_ge(S["lg_link"], 5 * B * NQ)
            dve.wait_ge(S["split_done"], 2 * NPIECE)

            def high_parts(n, f):
                s = n * FT + f
                dve.wait_ge(S["hid_ready"], s + 1 + RING)
                dve.wait_ge(S["w2_done"], s + 1)
                v.tensor_copy(hhi[:, f], hid[:, f]).then_inc(S["hhi_ready"], 1)
                if f % 2:
                    dve.wait_ge(S["hhi_ready"], s + 1)
                    v.tensor_tensor(hlo[:, f], hid[:, f], hhi[:, f], ALU.subtract).then_inc(S["hlo_odd"], 1)

            def add_expert(n, par):
                dve.wait_ge(S["w2_done"], n * FT + FT + RING)
                dve.wait_ge(S["eo_used"], n * 4 + 8)
                m = n // E
                for r in range(4):
                    hr = h_all[:, ds((m // 2) * 8 + m % 2 + 2 * r, 1), :].rearrange("p a d -> p (a d)")
                    v.scalar_tensor_tensor(hr, ps[:, 2 + par, r * D:(r + 1) * D],
                                           gs[:, ds(m, 1), r, ds(n % E, 1)].rearrange("p a e -> p (a e)"), hr,
                                           ALU.mult, ALU.add).then_inc(S["eo_used"], 1)

            for u in range(2):
                for f in range(FT):
                    high_parts(u, f)
            add_expert(0, 0)
            with dve.Fori(2, NEXP - 1, 2) as n:
                for u in range(2):
                    for f in range(FT):
                        high_parts(n + u, f)
                    add_expert(n + u - 1, 1 - u)
            add_expert(NEXP - 1, 1)

        @block.tensor
        def _(pe):
            t_ = nc.tensor

            def mm(o, l, r, start=True, stop=True):
                return t_.matmul(o, l, r, start=start, stop=stop, skip_group_check=True)

            def xn_T(c, par, first=False):
                pe.wait_ge(S["xn_ready"], c + 1)
                if not first:
                    pe.wait_ge(S["xnT_sb"], c)
                    pe.wait_ge(S["h1_ready"], c - 2)
                for b in range(B):
                    last = t_.transpose(ps[:, 0, b * P:(b + 1) * P], xn[par][:, b], ident)
                last.then_inc(S["xnT_ps"], 1)

            def project(c, par, first=False):
                pe.wait_ge(S["xnT_sb"], c + 1)
                pe.wait_ge(S["xsT_sb"], c + 1)
                if not first:
                    pe.wait_ge(S["qkT_sb"], c)
                mm(ps[:, 1, 0:B * P], wqkv[:, 0], xnT[par].rearrange("p b t -> p (b t)"))
                mm(ps[:, 1, B * P:], wqkv[:, 1], xsT[par].rearrange("p b t -> p (b t)")).then_inc(S["qkT_ps"], 1)

            def project_rows(c, par, b, first=False):
                if not (first and b == 0):
                    pe.wait_ge(S["qkv_sb"], 2 * c + b)
                mm(ps[:, 2, 0:D], xnT[par][:, b], wqkv[:, 0])
                mm(ps[:, 2, 2 * D:3 * D], xnT[par][:, b], wqkv[:, 2])
                mm(ps[:, 2, D:2 * D], xsT[par][:, b], wqkv[:, 1]).then_inc(S["qkv_ps"], 1)

            def out_T(c):
                pe.wait_ge(S["ao_ready"], c + 1)
                for b in range(B):
                    last = t_.transpose(ps[:, 0, (B + b) * P:(B + b + 1) * P], ao[:, b], ident)
                last.then_inc(S["aoT_ps"], 1)

            def out_project(c):
                pe.wait_ge(S["aoT_sb"], c + 1)
                for b in range(B):
                    last = mm(ps[:, 0, (B + b) * P:(B + b + 1) * P], aoT[:, b], wout[:])
                last.then_inc(S["pr_ps"], 1)

            def sums(c, par, b, first=False):
                kv = qkv[par][:, b, 1:3, :].rearrange("p a d -> p (a d)")
                pe.wait_ge(S["qkv_sb"], 2 * c + b + 1)
                if not first:
                    pe.wait_ge(S["x_sb"], c)
                mm(ps[:, 5 + b, 0:2 * D], upper, kv, stop=first)
                if not first:
                    mm(ps[:, 5 + b, 0:2 * D], last_row, xall[1 - par][:, b, 0:2, :].rearrange("p a d -> p (a d)"), start=False)
                    pe.wait_ge(S["sg_ready"], 2 * c)
                    mm(ps[:, 5 + b, 2 * D:], qkT[par][:, 0, b], sg[:, b].rearrange("p a d -> p (a d)"), start=False)
                mm(ps[:, 7, b * 2 * D:(b + 1) * 2 * D], qkv[par][:, b, 1, :], kv, start=(first and b == 0)
                   ).then_inc(S["state_ps"], 1)

            pe.wait_ge(S["load_w"], 80)
            pe.wait_ge(S["setup"], 6)
            xn_T(0, 0, first=True)
            project(0, 0, first=True)
            for b in range(B):
                project_rows(0, 0, b, first=True)
            for b in range(B):
                pe.wait_ge(S["blk_ready"], b + 1)
                if b:
                    pe.wait_ge(S["dt_sb"], b)
                for z in range(2):
                    last = mm(ps[:, 3 + z, :], qkT[0][:, 0, b], blkbuf[:, b].rearrange("p (z h) j -> p z (h j)", z=2)[:, z])
                last.then_inc(S["dt_ps"], 1)
            xn_T(1, 1, first=True)
            for b in range(B):
                sums(0, 0, b, first=True)
            project(1, 1)
            for b in range(B):
                project_rows(1, 1, b)
            pe.wait_ge(S["dt_sb"], B)
            for b in range(B):
                pe.wait_ge(S["attn0"], b + 1)
                if b:
                    pe.wait_ge(S["attnT0_sb"], b)
                for h in range(HA):
                    last = t_.transpose(ps[:, 3 + h // 4, h % 4 * P:(h % 4 + 1) * P], dtm[:, b, h], ident)
                last.then_inc(S["attnT0_ps"], 1)
                pe.wait_ge(S["attnT0_sb"], b + 1)
                for h in range(HA):
                    last = mm(ps[:, 5 + b, 3 * D + h * DA:3 * D + (h + 1) * DA], dtm[:, b, h],
                              qkv[0][:, b, 2, h * DA:(h + 1) * DA], start=False)
                last.then_inc(S["x_ps"], 1)

            def step_a(c, nxt, more=True, first=False):
                cur = 1 - nxt
                for b in range(B):
                    pe.wait_ge(S["blk_ready"], 2 * c + b + 1)
                    pe.wait_ge(S["dt_sb"], 2 * c + b)
                    for z in range(2):
                        last = mm(ps[:, 3 + z, :], qkT[cur][:, 1, b],
                                  blkbuf[:, b].rearrange("p (z h) j -> p z (h j)", z=2)[:, z])
                    last.then_inc(S["dt_ps"], 1)
                    sums(c, cur, b)
                    if more and b == 0:
                        xn_T(c + 1, nxt, first)
                if more:
                    project(c + 1, nxt)
                for b in range(B):
                    if more:
                        project_rows(c + 1, nxt, b)
                    if b:
                        if more:
                            pe.wait_ge(S["xnT_sb"], c + 2)
                        out_T(c - 1)
                    pe.wait_ge(S["dt_sb"], 2 * c + b + 1)
                    o = ps[:, 5 + b, 2 * D:].rearrange("p (a h e) -> p a h e", a=2, e=DA)
                    kv = qkv[cur][:, b, 1:3, :].rearrange("p a (h e) -> p a h e", e=DA)
                    for h in range(HA):
                        last = mm(o[:, :, h, :], dtm[:, b, h], kv[:, :, h, :], start=False)
                    last.then_inc(S["x_ps"], 1)
                out_project(c - 1)

            step_a(1, 0, first=True)
            with pe.Fori(2, NT - 3, 2) as c:
                for u in range(2):
                    step_a(c + u, 1 - u)
            step_a(NT - 2, 1)
            step_a(NT - 1, 0, more=False)
            out_T(NT - 1)
            out_project(NT - 1)

            pe.wait_ge(S["load_s"], 80)

            def normed_T(c, par, first=False):
                pe.wait_ge(S["x2_ready"], c + 1)
                if not first:
                    pe.wait_ge(S["hxT_sb"], c)
                for b in range(B):
                    last = t_.transpose(ps[:, 0, b * P:(b + 1) * P], x2[par][:, b], ident)
                last.then_inc(S["x2T_ps"], 1)

            def project2(c, par, first=False):
                pe.wait_ge(S["hxT_sb"], c + 1)
                if not first:
                    pe.wait_ge(S["qkn_ready"], 2 * c - 1)
                    pe.wait_ge(S["vlo_ready"], c)
                for b in range(B):
                    last = mm(ps[:, QB[par] + b, 0:3 * D], hxT[par][:, b], wsm[:])
                last.then_inc(S["qkv2_ps"], 1)

            def unit_T(c):
                for b in range(B):
                    pe.wait_ge(S["qkn_ready"], 1 + 2 * c + b + 1)
                    pe.wait_ge(S["lo_ready"], 1 + 2 * c)
                    for i in range(4):
                        last = t_.transpose(ps[:, 3 + b, i * P:(i + 1) * P],
                                            qkn[:, b, i].rearrange("p z e -> p (z e)"), ident)
                    last.then_inc(S["qkd_ps"], 1)

            pe.wait_ge(S["h1_ready"], NT)
            normed_T(0, 0, first=True)
            normed_T(1, 1)
            project2(0, 0, first=True)

            def step_a2(c, par, left=3):
                if left >= 1:
                    project2(c + 1, 1 - par)
                unit_T(c)
                if left >= 2:
                    normed_T(c + 2, par)

            with pe.Fori(0, NT - 5, 2) as c:
                for u in range(2):
                    step_a2(c + u, u)
            for c in range(NT - 4, NT):
                step_a2(c, c % 2, NT - 1 - c)

            pe.wait_ge(S["hi_ready"], T)
            pe.wait_ge(S["lo_ready"], 1 + T)
            pe.wait_ge(S["vlo_ready"], 1 + NT)
            bank4 = None

            def max_scores(it, part):
                c, b, h = ITEMS[it]
                r, kb, w, k = part
                q = b * N + c * CH + r * P
                if k >= 2:
                    pe.wait_ge(S["sm_used"], k - 1)
                last = mm(ps[:, 2 + k % 2, 0:w], qhh[:, h, q:q + P], khl[:, h, b * N + kb * CH:b * N + kb * CH + w],
                          stop=kb < c)
                if kb == c:
                    last = mm(ps[:, 2 + k % 2, w - P:w], ident16, neg_qk, start=False)
                last.then_inc(S["sm_ps"], 1)

            def max_row(it):
                nonlocal bank4
                h = ITEMS[it][2]
                if bank4:
                    pe.wait_ge(*bank4)
                pe.wait_ge(S["mneg"], it + 1)
                for r in range(4):
                    last = mm(ps[0:DS + 1, 4, r * P:(r + 1) * P], mpad[:, h, r], ident16)
                last.then_inc(S["mrow_ps"], 1)
                bank4 = S["mrow_sb"], it + 1

            def scores(k):
                it, kt, r0, diag = STEPS[k]
                c, b, h = ITEMS[it]
                if k in FIRST:
                    pe.wait_ge(S["mrow_sb"], it + 1)
                if k >= 2:
                    pe.wait_ge(S["p_ready"], k - 1)
                lo, at = r0 * P, b * N + kt * P
                q0 = b * N + c * CH
                mm(ps[:, k % 2, lo:], khl[:, h, at:at + P], qhh[:, h, q0 + lo:q0 + CH], stop=False)
                last = mm(ps[:, k % 2, lo:], kh1[:, h, at:at + P], ql[:, h, q0 + lo:q0 + CH], start=False, stop=not diag)
                if diag:
                    last = mm(ps[:, k % 2, lo:lo + P], ident16, neg_kq, start=False)
                last.then_inc(S["s_ps"], 1)

            def values(k):
                it, kt, r0, diag = STEPS[k]
                c, b, h = ITEMS[it]
                first = k in FIRST
                pe.wait_ge(S["plo_even" if k % 2 == 0 else "plo_odd"], k // 2 + 1)
                if first and it:
                    pe.wait_ge(S["o_used"], it)
                vt = v16[:, 2 * kt + b, h, :]
                for r in range(r0, 4):
                    o = ps[:, 6 + r // 2, (r % 2) * VW:(r % 2 + 1) * VW]
                    mm(o, phi[:, k % 4, r * P:(r + 1) * P], vt, start=first and r % 2 == 0)
                    last = mm(o[:, 0:DS + 1], plo[:, k % 4, r * P:(r + 1) * P], vt[:, 0:DS + 1], start=False)
                last.then_inc(S["pv_done"], 1)

            for part in MPARTS[0]:
                max_scores(0, part)
            max_row(0)
            for k in range(NSTEP + LAG + 5 * YGAP + 3):
                if k < NSTEP:
                    scores(k)
                    for it, part in MSLOT.get(k, ()):
                        max_scores(it, part)
                if LAG <= k < NSTEP + LAG:
                    values(k - LAG)
                if k + 2 in FIRST:
                    max_row(FIRST.index(k + 2))
                for m in range(B * NQ):
                    j = (k - YAT[m]) / YGAP
                    if j == 1:
                        pe.wait_ge(*bank4)
                        pe.wait_ge(S["och_ready"], 2 * m + 2)
                        for r in range(4):
                            last = t_.transpose(ps[:, 4, r * P:(r + 1) * P], och[:, r], ident)
                        last.then_inc(S["oT_ps"], 1)
                        bank4 = S["oT_sb"], m + 1
                    if j == 2:
                        pe.wait_ge(S["oT_sb"], m + 1)
                        if m:
                            pe.wait_ge(S["h2_ready"], m)
                        mm(ps[:, 5, :], wo[:], oT).then_inc(S["y_ps"], 1)
                    if j == 3:
                        pe.wait_ge(*bank4)
                        pe.wait_ge(S["yhi_ready"], m + 1)
                        for r in range(4):
                            last = mm(ps[:, 4, r * E:(r + 1) * E], y32[:, r * P:(r + 1) * P], wgate[:])
                        last.then_inc(S["lg_ps"], 1)
                        bank4 = S["lg_ready"], m + 1
                    if j == 4:
                        pe.wait_ge(*bank4)
                        pe.wait_ge(S["gate_ready"], m + 1)
                        for r in range(4):
                            last = t_.transpose(ps[0:E, 4, r * P:(r + 1) * P], gt[:, 3, r], ident)
                        last.then_inc(S["gT_ps"], 1)
                        bank4 = S["gT_sb"], m + 1
                    if j == 5:
                        pe.wait_ge(S["gT_sb"], m + 1)
                        pe.wait_ge(S["ylo_ready"], m + 1)
                        for r in range(4):
                            last = mm(ps[:, 5, r * D:(r + 1) * D], gT[:, r * P:(r + 1) * P], b2s[:])
                        last.then_inc(S["b2_ps"], 1)

            pe.wait_ge(S["split_done"], 2 * NPIECE)
            pe.wait_ge(S["ylo_ready"], B * NQ)
            pe.wait_ge(S["h2_ready"], B * NQ)
            pe.wait_ge(S["p_ready"], NSTEP)

            def up(n, f):
                pe.wait_ge(S["hid_ready"], n * FT + f + 1)
                w = ds((n % E) * FF + f * P, P)
                y = ds((n // E) * CH, CH)
                o = ps[:, HBANK[f], :]
                mm(o, w1hi[:, w], yhi[:, y], stop=False)
                mm(o, w1hi[:, w], ylo[:, y], start=False, stop=False)
                mm(o, w1lo[:, w], yhi[:, y], start=False).then_inc(S["hid_ps"], 1)

            def down(n, f, par):
                pe.wait_ge(S["hlo_even" if f % 2 == 0 else "hlo_odd"], 2 * n + f // 2 + 1 + 2)
                if f == 0:
                    pe.wait_ge(S["eo_used"], 4 * n + 4)
                wi = (n % E) * FT + f
                for r in range(4):
                    o = ps[:, 2 + par, r * D:(r + 1) * D]
                    hi, lo = hhi[:, f, r * P:(r + 1) * P], hlo[:, f, r * P:(r + 1) * P]
                    whi, wlo = (w2hl[:, ds(wi, 1), z, :].rearrange("p a d -> p (a d)") for z in range(2))
                    mm(o, hi, whi, start=(f == 0 and r == 0), stop=False)
                    mm(o, hi, wlo, start=False, stop=False)
                    last = mm(o, lo, whi, start=False, stop=f == FT - 1)
                last.then_inc(S["w2_done"], 1)

            def expert(n, par, more=True):
                for f in range(FT):
                    if f == 0:
                        up(n, FT - 1)
                    elif more:
                        up(n + 1, f - 1)
                    down(n, f, par)

            for f in range(FT - 1):
                up(0, f)
            with pe.Fori(0, NEXP - 3, 2) as n:
                for u in range(2):
                    expert(n + u, u)
            expert(NEXP - 2, 0)
            expert(NEXP - 1, 1, more=False)


def plan():
    items = [(c, b, h) for c in range(NQ) for b in range(B) for h in range(HS)]
    steps, first, mparts, mslot = [], [], [], {}
    k = 0
    for c, b, h in items:
        blocks = [(r, kb, CH if kb < c else (r + 1) * P) for kb in range(c + 1) for r in range(4)]
        mparts.append([(r, kb, w, k + i) for i, (r, kb, w) in enumerate(blocks)])
        k += len(blocks)
    for it, (c, b, h) in enumerate(items):
        first.append(len(steps))
        steps += [(it, 4 * c + d, d, True) for d in range(4)] + [(it, kt, 0, False) for kt in range(4 * c)]
        if it + 1 < len(items):
            span = 4 * c + 4 - 2
            for i, part in enumerate(mparts[it + 1]):
                mslot.setdefault(first[it] + i * span // len(mparts[it + 1]), []).append((it + 1, part))
    ends = first[1:] + [len(steps)]
    o_at = [e - 1 + LAG for e in ends]
    y_at = [o_at[it] for it in range(1, len(items), 2)]
    return items, steps, first, mparts, mslot, o_at, y_at


LAG = 3
YGAP = 2
ITEMS, STEPS, FIRST, MPARTS, MSLOT, OAT, YAT = plan()
NSTEP = len(STEPS)


def constants():
    c = np.zeros((P, C_END), np.float32)
    i = np.arange(P)
    c[:, C_ID:C_ID + P] = np.eye(P)
    c[:, C_U:C_U + P] = i[:, None] <= i[None, :]
    c[:, C_L:C_L + P] = i[:, None] >= i[None, :]
    c[P - 1, C_LAST:C_LAST + P] = 1.0
    c[:, C_BLK:C_BLK + P] = i[:, None] // DA == i[None, :] // DA
    c[:, C_HEAD:C_HEAD + HA] = i[:, None] // DA == np.arange(HA)[None, :]
    where = np.arange(NT)[None, :] * P + i[:, None] + 1
    c[:, C_INV:C_INV + NT] = 1.0 / where
    place = np.arange(1, N + 1, dtype=np.float32)[:, None]
    k = np.arange(D)
    exponent = (np.where(k % 2 == 0, k, k + 1).astype(np.float32) / np.float32(D)).astype(np.float32)
    angle = (place / np.power(np.float32(10000.0), exponent)).astype(np.float32)
    pe = np.where(k % 2 == 0, np.cos(angle), np.sin(angle)).astype(np.float32)
    c[:, C_POS:C_END] = pe.reshape(NT, P, D).transpose(1, 0, 2).reshape(P, NT * D)
    c16 = np.zeros((P, 3 * P), np.float16)
    c16[:, 0:P] = np.eye(P)
    c16[:, P:2 * P] = np.where(i[None, :] > i[:, None], NEG, 0.0)
    c16[:, 2 * P:] = np.where(i[:, None] > i[None, :], NEG, 0.0)
    return c, c16


def kernel(**inputs):
    import concourse.bacc as _bacc
    from concourse import mybir as _mybir
    from concourse.bass_utils import run_bass_kernel_spmd as _run

    a = {k: np.asarray(v) for k, v in inputs.items()}
    c, c16 = constants()
    rows = np.concatenate([a["L0_tok_b"], a["L0_attn_b_out"], a["L0_ffn_gate_b"],
                           a["L0_attn_norm_g"].reshape(-1), a["L0_attn_norm_b"].reshape(-1)])
    cols = np.concatenate([a["L0_ffn_ln_g"][:, None], a["L0_ffn_ln_b"][:, None],
                           np.tile(a["L0_ffn_qn_g"], 2)[:, None], np.tile(a["L0_ffn_kn_g"], 2)[:, None],
                           a["L0_ffn_b1"].reshape(E * FT, P).T], axis=1)
    arrays = {
        "ids": a["x"].reshape(B, NT, P).transpose(2, 1, 0).reshape(P, T),
        "emb_rows": a["L0_tok_W"].T,
        "consts": c, "consts16": c16,
        "rows": np.broadcast_to(rows[None, :], (P, R_END)),
        "cols": cols,
        "w_qkv": a["L0_attn_w_qkv"], "w_out": a["L0_attn_w_out"],
        "w_sm": np.concatenate([a["L0_ffn_Wq"], a["L0_ffn_Wk"], a["L0_ffn_Wv"]], axis=1),
        "w_o": a["L0_ffn_Wo"], "w_gate": a["L0_ffn_gate_W"],
        "w1": a["L0_ffn_W1"].transpose(1, 0, 2).reshape(D, E * FF),
        "w2": a["L0_ffn_W2"].reshape(E * FT, P, D).transpose(1, 0, 2).reshape(P, E * FT * D),
        "b2": a["L0_ffn_b2"],
    }
    arrays = {k: np.ascontiguousarray(v) for k, v in arrays.items()}
    nc = _bacc.Bacc("TRN2", target_bir_lowering=False, num_devices=1)
    args = [nc.dram_tensor(k, v.shape, _mybir.dt.from_np(v.dtype), kind="ExternalInput").ap()
            for k, v in arrays.items()]
    args.append(nc.dram_tensor("out", (B * N, D), F32, kind="ExternalOutput").ap())
    tower(nc, *args)
    r = _run(nc, [arrays], core_ids=[0])
    return r.results[0]["out"].reshape(B, N, D)
```

```python
from contextlib import ExitStack

import numpy as np

import concourse.bass as bass
from concourse import mybir

F32 = mybir.dt.float32
F16 = mybir.dt.float16
I32 = mybir.dt.int32
ALU = mybir.AluOpType
ACT = mybir.ActivationFunctionType
AX = mybir.AxisListType.X

P = 128
B, N, D = 2, 2048, 128
NT = N // P
T = B * NT
HA, DA = 8, 16
HS, DS = 2, 64
E, FF = 8, 512
FT = FF // P
NQ = N // 512
CH = 512
LN_EPS = 1e-5
DOT_EPS = 1e-8 * D
L2_EPS = 1e-12
NEG = -60000.0
WS = 64.0
VW = 2 * DS + 1

C_ID, C_U, C_L, C_LAST, C_BLK, C_HEAD, C_INV, C_POS = 0, 128, 256, 384, 512, 640, 648, 664
C_END = C_POS + NT * D
R_TB, R_BO, R_GB, R_NG, R_NB = 0, 128, 256, 264, 272
R_END = 280
K_LG, K_LB, K_QG, K_KG, K_B1 = 0, 1, 2, 3, 4
K_END = K_B1 + E * FT


def tower(nc, ids, emb_rows, consts, consts16, rows, cols, w_qkv, w_out, w_sm, w_o, w_gate, w12_rows, b2, out):
    with ExitStack() as ctx:
        def sb(name, shape, dt=F32):
            return ctx.enter_context(nc.sbuf_tensor(name, shape, dt))

        def sem(name):
            return ctx.enter_context(nc.semaphore(name))

        cst = sb("cst", [P, C_END])
        c16 = sb("c16", [P, 3 * P], F16)
        row = sb("row", [P, R_END])
        col = sb("col", [P, K_END])
        idx = sb("idx", [P, T], I32)
        wqkv = sb("wqkv", [P, 3, D])
        wout = sb("wout", [P, D])
        wsm = sb("wsm", [P, 3 * D])
        wo = sb("wo", [P, D])
        wgate = sb("wgate", [P, E])
        b2s = sb("b2s", [E, D])
        mhalf = sb("mhalf", [P, 16])
        qkg8 = sb("qkg8", [P, 1])
        eps = sb("eps", [P, 10])
        ln_eps, l2_eps = eps[:, 0:2], eps[:, 2:10]
        credit = sb("credit", [P, 16])
        h_all = sb("h_all", [P, T, D])
        khl = sb("khl", [P, HS, B * N], F16)
        kh1 = sb("kh1", [DS + 1, HS, B * N], F16)
        qhh = sb("qhh", [P, HS, B * N], F16)
        ql = sb("ql", [DS + 1, HS, B * N], F16)
        v16 = sb("v16", [P, T, HS, VW], F16)
        y2 = sb("y2", [P, B * N])
        yhi = y2[:, 0:B * N // 2].bitcast(F16)
        ylo = y2[:, B * N // 2:].bitcast(F16)
        arena = sb("arena", [P, 2 * E * FF])
        w12 = arena[:].bitcast(F16).rearrange("p (w z d) -> p w z d", z=2, d=D)

        ident = cst[:, C_ID:C_ID + P]
        upper = cst[:, C_U:C_U + P]
        lower = cst[:, C_L:C_L + P]
        last_row = cst[:, C_LAST:C_LAST + P]
        blk = cst[:, C_BLK:C_BLK + P]
        head = cst[:, C_HEAD:C_HEAD + HA]
        pos = cst[:, C_POS:C_END].rearrange("p (c d) -> p c d", d=D)
        ident16 = c16[:, 0:P]
        neg_qk = c16[:, P:2 * P]
        neg_kq = c16[:, 2 * P:3 * P]

        taken = [0]

        def early(*dims):
            n = int(np.prod(dims))
            piece = arena[:, taken[0]:taken[0] + n]
            taken[0] += n
            assert taken[0] <= 2 * E * FF
            names_ = "abcd"[:len(dims)]
            return piece if len(dims) == 1 else piece.rearrange(
                f"p ({' '.join(names_)}) -> p {' '.join(names_)}", **dict(zip(names_[1:], dims[1:])))

        xn = [early(B, D) for i in range(2)]
        xnT = [early(B, P) for i in range(2)]
        xsT = [early(B, P) for i in range(2)]
        qkT = [early(2, B, P) for i in range(2)]
        qkv = [early(B, 3, D) for i in range(2)]
        hb = [early(B, D) for i in range(2)]
        prod = early(B, 2, D)
        ao = early(B, D)
        ao2 = early(B, D)
        aoT = early(B, P)
        xall = [early(B, 4, D) for i in range(2)]
        st6 = sb("st6", [P, B, 6])
        mv = [sb(f"mv{i}", [P, B, 2]) for i in range(2)]
        rs = [sb(f"rs{i}", [P, B]) for i in range(2)]
        x0 = sb("x0", [P, B])
        sg = sb("sg", [P, B, 2, D])
        ab = sb("ab", [P, B, 2, HA])
        sm = sb("sm", [P, 8, B, HA])
        blkbuf = y2[:, 0:B * HA * P].rearrange("p (b h j) -> p b h j", b=B, h=HA)
        dtm = y2[:, B * HA * P:].rearrange("p (b h j) -> p b h j", b=B, h=HA)
        sq = sb("sq", [P, B, HA, P])
        st2 = sb("st2", [P, 2, B, 6])
        mv2 = [sb(f"mv2{i}", [P, B, 2]) for i in range(2)]
        rr = [sb(f"rr{i}", [P, 4, B]) for i in range(2)]
        x2 = [sb(f"x2{i}", [P, B, D]) for i in range(2)]
        hxT = [sb(f"hxT{i}", [P, B, P]) for i in range(2)]
        qk2 = sb("qk2", [P, B, 4 * DS])
        ss = sb("ss", [P, 2, 3, B * 4])
        qkn = sb("qkn", [P, B, 4, 2, DS])
        mx = sb("mx", [P, 4, NQ])
        mpad = sb("mpad", [P, HS, 4, DS + 1], F16)
        p32 = sb("p32", [P, QR, CH])
        phi = sb("phi", [P, PR, CH], F16)
        plo = sb("plo", [P, PR, CH], F16)
        mall = sb("mall", [P, 4])
        rl = sb("rl", [P, 4])
        och = sb("och", [P, 4, D])
        gt = sb("gt", [P, 4, 4, E])
        gl = sb("gl", [P, 4, 4])
        gT = sb("gT", [E, CH])
        sqf = sq[:].rearrange("p b h j -> p (b h j)")
        stage = [sqf[:, 0:512], sqf[:, 512:1024]]
        scaled = [sqf[:, 1024:1536], sqf[:, 1536:2048]]
        oT, y32 = scaled
        hid = cst[:, C_POS:C_POS + 4 * CH].rearrange("p (u t) -> p u t", u=4)
        hhi = sqf[:, 0:2 * CH].bitcast(F16).rearrange("p (u t) -> p u t", u=4)
        hlo = sqf[:, 2 * CH:4 * CH].bitcast(F16).rearrange("p (u t) -> p u t", u=4)
        gs = sb("gs", [P, B * NQ, 4, E])

        ps = ctx.enter_context(nc.psum_tensor("ps", [P, 8, 512], F32))

        names = """load_c load_w load_s load_stage load_stage1 split_done gathered0 gathered1 gathered setup stats veps
            rstd hb_ready xn_ready xnT_ps xnT_sb x0_link xsT_sb qkT_ps qkT_sb qkv_ps qkv_sb blk_ready dt_ps
            dt_sb sq_ready state_ps sg_ready x_ps var_ready r_ready gr_ready grmu_ready coef ao_ready aoT_ps
            aoT_sb pr_ps h1_ready attn0 attnT0_ps attnT0_sb front_link core_link direct_link pos_ready stats2
            st2_link rr_link rr_ready x2_ready x2T_ps hxT_sb qkv2_ps sqqk ss_ready rn_link rn_ready qkn_ready
            vhi_ready vlo_ready qkd_ps hi_ready lo_ready sm_ps sm_used max_link mneg mrow_ps mrow_sb s_ps
            p_ready plo_pool plo_dve scaled_ready pv_done o_link o_used oT_ps oT_sb y_ps yhi_ready ylo_ready
            lg_ps lg_link lg_ready eg_ready gate_ready gT_ps gT_sb b2_ps h2_ready hid_ps hid_ready hhi_ready
            hlo_even hlo_odd l2_link x_sb v_link ao_link w2_done eo_used stored"""
        S = {name: sem(name) for name in names.split()}
        NPIECE = 2 * E * FF // 512
        STAGED = ["load_stage", "load_stage1"]
        QB = [1, 5]
        MB = [2, 3, 5]
        RING = 4
        HBANK = [0, 1, 4, 5]
        NEXP = B * NQ * E
        ds = bass.ds

        block = ctx.enter_context(nc.Block())

        @block.sync
        def _(sp):
            sp.dma_start(idx[:], ids).then_inc(S["load_c"], 16)
            sp.dma_start(row[:], rows).then_inc(S["load_w"], 16)
            sp.dma_start(cst[:], consts).then_inc(S["load_w"], 16)
            sp.dma_start(wqkv[:].rearrange("p a d -> p (a d)"), w_qkv).then_inc(S["load_w"], 16)
            sp.dma_start(col[:], cols).then_inc(S["load_w"], 16)
            sp.dma_start(wout[:], w_out).then_inc(S["load_w"], 16)
            sp.dma_start(wsm[:], w_sm).then_inc(S["load_s"], 16)
            sp.dma_start(c16[:], consts16).then_inc(S["load_s"], 16)
            sp.dma_start(wo[:], w_o).then_inc(S["load_s"], 16)
            sp.dma_start(wgate[:], w_gate).then_inc(S["load_s"], 16)
            sp.dma_start(b2s[:], b2).then_inc(S["load_s"], 16)
            sp.wait_ge(S["var_ready"], 1)
            for n in range(2):
                sp.dma_start(stage[n], w12_rows[:, n * 512:(n + 1) * 512]).then_inc(S[STAGED[n]], 16)
            with sp.Fori(2, NT - 1, 2) as n:
                for u in range(2):
                    sp.wait_ge(S["scaled_ready"], n + (u - 1))
                    sp.dma_start(stage[u], w12_rows[:, ds(n * 512 + u * 512, 512)]).then_inc(S[STAGED[u]], 16)
            for c in range(NQ):
                with sp.Fori(0, B) as b:
                    sp.wait_ge(S["eo_used"], (2 * c + b + 1) * E * 4 + 8)
                    for r in range(4):
                        sp.dma_start(out[ds(b * N + c * CH + r * P, P), :],
                                     h_all[:, ds(8 * c + 2 * r + b, 1), :].rearrange("p a d -> p (a d)")
                                     ).then_inc(S["stored"], 16)
            sp.wait_ge(S["stored"], 16 * 4 * B * NQ)

        @block.gpsimd
        def _(pool):
            g = nc.gpsimd
            pool.wait_ge(S["load_c"], 16)

            def gather(t0, t1):
                for t in range(t0, t1):
                    g.indirect_dma_start(out=h_all[:, t, :], out_offset=None, in_=emb_rows,
                                         in_offset=bass.IndirectOffsetOnAxis(ap=idx[:, t:t + 1], axis=0)
                                         ).then_inc(S["gathered0" if t < B else "gathered1" if t < 8 else "gathered"], 16)

            gather(0, B)
            g.memset(mhalf[:], -0.5).then_inc(S["setup"], 1)
            g.memset(ln_eps, LN_EPS).then_inc(S["setup"], 1)
            g.memset(l2_eps, L2_EPS).then_inc(S["setup"], 1)
            g.memset(v16[:, :, :, DS:DS + 1], 1.0).then_inc(S["setup"], 1)
            g.memset(mpad[:], 0.0).then_inc(S["setup"], 1)
            gather(B, 9)
            pool.wait_ge(S["setup"], 5)
            pool.wait_ge(S["load_w"], 80)

            def front(c, par):
                pool.wait_ge(S["stats"], c + 1)
                g.tensor_tensor(rs[par][:], mv[par][:, :, 1], ln_eps, ALU.add).then_inc(S["veps"], 1)
                pool.wait_ge(S["veps"], c + 1)
                g.tensor_tensor(rs[par][:], rs[par][:], mhalf[:, 0:B], ALU.pow).then_inc(S["rstd"], 1)

            def out_bias(c, par, first=False):
                if not first:
                    pool.wait_ge(S["h1_ready"], c - 1)
                g.tensor_tensor(hb[par], h_all[:, ds(2 * c, 2), :],
                                row[:, R_BO:R_BO + D].unsqueeze(1).to_broadcast([P, B, D]),
                                ALU.add).then_inc(S["hb_ready"], 1)

            def shifted(c, par):
                pool.wait_ge(S["xnT_sb"], c + 1)
                g.tensor_tensor(xsT[par], xnT[par], x0[:].unsqueeze(2).to_broadcast([P, B, P]), ALU.subtract
                                ).then_inc(S["xsT_sb"], 1)

            def q_blocks(c, par, first=False):
                pool.wait_ge(S["qkT_sb"], c + 1)
                for b in range(B):
                    if not first:
                        pool.wait_ge(S["dt_ps"], 2 * c + b - 1)
                    g.tensor_tensor(blkbuf[:, b],
                                    qkT[par][:, 1 if first else 0, b, :].unsqueeze(1).to_broadcast([P, HA, P]),
                                    head.unsqueeze(2).to_broadcast([P, HA, P]), ALU.mult
                                    ).then_inc(S["blk_ready"], 1)

            def coefs(c):
                pool.wait_ge(S["var_ready"], c + 1)
                g.tensor_tensor(sm[:, 4], sm[:, 3], mhalf[:].rearrange("p (b h) -> p b h", b=B),
                                ALU.pow).then_inc(S["r_ready"], 1)
                pool.wait_ge(S["r_ready"], c + 1)
                g.tensor_tensor(sm[:, 5], sm[:, 4], row[:, R_NG:R_NG + HA].unsqueeze(1).to_broadcast([P, B, HA]),
                                ALU.mult).then_inc(S["gr_ready"], 1)
                pool.wait_ge(S["gr_ready"], c + 1)
                g.tensor_tensor(sm[:, 6], sm[:, 5], sm[:, 0], ALU.mult).then_inc(S["grmu_ready"], 1)
                pool.wait_ge(S["grmu_ready"], c + 1)
                g.tensor_tensor(sm[:, 7], row[:, R_NB:R_NB + HA].unsqueeze(1).to_broadcast([P, B, HA]), sm[:, 6],
                                ALU.subtract).then_inc(S["coef"], 1)

            front(0, 0)
            gather(9, 11)
            pool.wait_ge(S["x0_link"], 2)
            shifted(0, 0)
            gather(11, 13)
            front(1, 1)
            q_blocks(0, 0, first=True)
            shifted(1, 1)
            out_bias(0, 0, first=True)
            gather(13, 14)
            q_blocks(1, 1)
            out_bias(1, 1, first=True)
            gather(14, 22)
            coefs(0)
            gather(22, 24)
            front(2, 0)

            def step_a(c, nxt, more=2, tail=True):
                if more:
                    shifted(c + 1, nxt)
                if tail:
                    coefs(c - 1)
                else:
                    gather(24, 28)
                if more:
                    q_blocks(c + 1, nxt)
                if not tail:
                    gather(28, T)
                if more >= 2:
                    front(c + 2, 1 - nxt)
                if tail:
                    out_bias(c, 1 - nxt)

            step_a(1, 0, tail=False)
            with pool.Fori(2, NT - 3, 2) as c:
                for u in range(2):
                    step_a(c + u, 1 - u)
            step_a(NT - 2, 1, more=1)
            step_a(NT - 1, 0, more=0)

            def both_norms(c, par):
                pool.wait_ge(S["stats2"], c + 1)
                k = 5 * c
                var = mv2[par][:, :, 1]
                a, b_, c_ = rr[par][:, 0], rr[par][:, 1], rr[par][:, 2]
                g.tensor_tensor(a, var, ln_eps, ALU.add).then_inc(S["rr_link"], 1)
                pool.wait_ge(S["rr_link"], k + 1)
                g.tensor_tensor(b_, a, mhalf[:, 0:B], ALU.pow).then_inc(S["rr_link"], 1)
                pool.wait_ge(S["rr_link"], k + 2)
                g.tensor_tensor(a, var, b_, ALU.mult).then_inc(S["rr_link"], 1)
                pool.wait_ge(S["rr_link"], k + 3)
                g.tensor_tensor(c_, a, b_, ALU.mult).then_inc(S["rr_link"], 1)
                pool.wait_ge(S["rr_link"], k + 4)
                g.tensor_tensor(c_, c_, ln_eps, ALU.add).then_inc(S["rr_link"], 1)
                pool.wait_ge(S["rr_link"], k + 5)
                g.tensor_tensor(a, c_, mhalf[:, 0:B], ALU.pow).then_inc(S["rn_link"], 1)
                pool.wait_ge(S["rn_link"], c + 1)
                g.tensor_tensor(rr[par][:, 3], a, b_, ALU.mult).then_inc(S["rr_ready"], 1)

            def l2_factors(c, par):
                pool.wait_ge(S["ss_ready"], c + 1)
                g.tensor_tensor(ss[:, par, 1], ss[:, par, 0], l2_eps, ALU.add).then_inc(S["l2_link"], 1)
                pool.wait_ge(S["l2_link"], c + 1)
                g.tensor_tensor(ss[:, par, 2], ss[:, par, 1], mhalf[:, 0:8], ALU.pow).then_inc(S["rn_ready"], 1)

            both_norms(0, 0)
            coefs(NT - 1)
            both_norms(1, 1)
            l2_factors(0, 0)
            both_norms(2, 0)

            def weights_low(c, par):
                pool.wait_ge(S["scaled_ready"], c + 1)
                piece = w12[:, ds(c * 4, 4), :, :]
                g.tensor_tensor(piece[:, :, 1, :], scaled[par].rearrange("p (w d) -> p w d", d=D), piece[:, :, 0, :],
                                ALU.subtract).then_inc(S["split_done"], 1)

            def step_a2(c, par, left=3):
                if left >= 1:
                    l2_factors(c + 1, 1 - par)
                if left >= 3:
                    both_norms(c + 3, 1 - par)
                weights_low(c, par)

            with pool.Fori(0, NT - 5, 2) as c:
                for u in range(2):
                    step_a2(c + u, u)
            for c in range(NT - 4, NT):
                step_a2(c, c % 2, NT - 1 - c)

            for k in range(NSTEP + LAG + 5 * YGAP + 3):
                if k < NSTEP and on_pool(k):
                    lo = STEPS[k][2] * P
                    pool.wait_ge(S["p_ready"], k + 1)
                    if k >= PR:
                        pool.wait_ge(S["pv_done"], k - PR + 1)
                    g.tensor_tensor(plo[:, k % PR, lo:], p32[:, k % QR, lo:], phi[:, k % PR, lo:], ALU.subtract
                                    ).then_inc(S["plo_pool"], 1)
                for m in range(B * NQ):
                    if k == YAT[m] + 2 * YGAP:
                        pool.wait_ge(S["yhi_ready"], m + 1)
                        g.tensor_tensor(ylo[:, m * CH:(m + 1) * CH], y32, yhi[:, m * CH:(m + 1) * CH],
                                        ALU.subtract).then_inc(S["ylo_ready"], 1)

            with pool.Fori(0, NEXP) as n:
                for f in range(0, FT, 2):
                    pool.wait_ge(S["hhi_ready"], n * FT + f + 1)
                    pool.wait_ge(S["w2_done"], n * FT + f + 1)
                    g.tensor_tensor(hlo[:, f], hid[:, f], hhi[:, f], ALU.subtract).then_inc(S["hlo_even"], 1)

        @block.scalar
        def _(act):
            a = nc.scalar

            def front(c, par):
                act.wait_ge(S["xnT_ps"], c + 1)
                a.copy(xnT[par].rearrange("p b t -> p (b t)"), ps[:, 0, 0:B * P]).then_inc(S["xnT_sb"], 1)
                queries_keys(c, par)

            def queries_keys(c, par, read=False):
                act.wait_ge(S["qkT_ps"], c + 1)
                a.copy(qkT[par].rearrange("p a b t -> p (a b t)"), ps[:, 1, :]).then_inc(S["qkT_sb"], 1)
                if read:
                    act.wait_ge(S["var_ready"], c - 1)
                for b in range(B):
                    act.wait_ge(S["qkv_ps"], 2 * c + b + 1)
                    a.copy(qkv[par][:, b].rearrange("p a d -> p (a d)"), ps[:, 2, 0:3 * D]).then_inc(S["qkv_sb"], 1)

            def sums_out(c, cur, first=False):
                act.wait_ge(S["x_ps"], 2 * c + 2)
                if not first:
                    act.wait_ge(S["ao_ready"], c)
                if first:
                    a.copy(xall[cur][:, :, 0:2, :], ps[:, 5:7, 0:2 * D].rearrange("p b (a d) -> p b a d", d=D))
                    a.copy(xall[cur][:, :, 3, :], ps[:, 5:7, 3 * D:]).then_inc(S["x_sb"], 1)
                else:
                    a.copy(xall[cur].rearrange("p b a d -> p b (a d)"), ps[:, 5:7, :]).then_inc(S["x_sb"], 1)

            def ao_out(c):
                act.wait_ge(S["aoT_ps"], c + 1)
                a.copy(aoT.rearrange("p b t -> p (b t)"), ps[:, 0, B * P:]).then_inc(S["aoT_sb"], 1)

            a.preload_act_table(ACT.Exp)
            front(0, 0)
            front(1, 1)
            for b in range(B):
                act.wait_ge(S["attnT0_ps"], b + 1)
                act.wait_ge(S["sq_ready"], b + 1)
                a.copy(dtm[:, b].rearrange("p (z h) j -> p z (h j)", z=2), ps[:, 3:5, :]).then_inc(S["attnT0_sb"], 1)
            sums_out(0, 0, first=True)

            def step_a(c, nxt, more=True, first=False):
                if not first:
                    sums_out(c - 1, nxt)
                if more:
                    act.wait_ge(S["xnT_ps"], c + 2)
                    a.copy(xnT[nxt].rearrange("p b t -> p (b t)"), ps[:, 0, 0:B * P]).then_inc(S["xnT_sb"], 1)
                    queries_keys(c + 1, nxt, read=not first)
                ao_out(c - 1)

            step_a(1, 0, first=True)
            with act.Fori(2, NT - 3, 2) as c:
                for u in range(2):
                    step_a(c + u, 1 - u)
            step_a(NT - 2, 1)
            step_a(NT - 1, 0, more=False)
            sums_out(NT - 1, 1)

            def normed_T(c, par):
                act.wait_ge(S["x2T_ps"], c + 1)
                a.activation(hxT[par][:].rearrange("p b t -> p (b t)"), ps[:, 0, 0:B * P],
                             ACT.Identity, bias=col[:, K_LB:K_LB + 1], scale=col[:, K_LG:K_LG + 1]
                             ).then_inc(S["hxT_sb"], 1)

            def squares(c, par, first=False):
                act.wait_ge(S["qkv2_ps"], c + 1)
                if not first:
                    act.wait_ge(S["ss_ready"], c)
                a.activation(qk2[:], ps[:, QB[par]:QB[par] + B, 0:2 * D], ACT.Square).then_inc(S["sqqk"], 1)
                a.copy(v16[:, ds(2 * c, B), :, 0:DS],
                       ps[:, QB[par]:QB[par] + B, 2 * D:3 * D].rearrange("p b (h d) -> p b h d", h=HS)).then_inc(S["vhi_ready"], 1)

            def high_qk(c):
                for b in range(B):
                    act.wait_ge(S["qkd_ps"], 2 * c + b + 1)
                    at = ds(b * N + c * P, P)
                    a.activation(qhh[:, :, at], ps[:, 3 + b, 0:2 * P].rearrange("p (h t) -> p h t", h=HS),
                                 ACT.Copy, scale=qkg8[:])
                    a.activation(kh1[0:DS, :, at], ps[0:DS, 3 + b, 2 * P:4 * P].rearrange("p (h t) -> p h t", h=HS),
                                 ACT.Copy, scale=col[0:DS, K_KG:K_KG + 1])
                    a.activation(khl[:, :, at], ps[:, 3 + b, 2 * P:4 * P].rearrange("p (h t) -> p h t", h=HS),
                                 ACT.Copy, scale=col[:, K_KG:K_KG + 1]).then_inc(S["hi_ready"], 1)

            def weights_high(c, par):
                act.wait_ge(S[STAGED[par]], 8 * (c - par) + 16)
                act.wait_ge(S["split_done"], c + 1)
                st = stage[par].rearrange("p (w d) -> p w d", d=D)
                a.activation(w12[:, ds(c * 4, 4), 0, :], st, ACT.Copy, scale=WS)
                a.activation(scaled[par], stage[par], ACT.Copy, scale=WS).then_inc(S["scaled_ready"], 1)

            normed_T(0, 0)
            ao_out(NT - 1)
            normed_T(1, 1)
            act.wait_ge(S["h1_ready"], NT)
            squares(0, 0, first=True)

            def step_a2(c, par, left=3):
                if left >= 1:
                    squares(c + 1, 1 - par)
                high_qk(c)
                if left >= 2:
                    normed_T(c + 2, par)
                weights_high(c, par)

            with act.Fori(0, NT - 5, 2) as c:
                for u in range(2):
                    step_a2(c + u, u)
            for c in range(NT - 4, NT):
                step_a2(c, c % 2, NT - 1 - c)

            def max_row(it):
                c, b, h = ITEMS[it]
                act.wait_ge(S["mrow_ps"], it + 1)
                a.copy(ql[DS:DS + 1, h, b * N + c * CH:b * N + (c + 1) * CH], ps[DS:DS + 1, 4, :]
                       ).then_inc(S["mrow_sb"], 1)

            max_row(0)
            for k in range(NSTEP + LAG + 5 * YGAP + 3):
                if k < NSTEP:
                    it, kt, r0, diag = STEPS[k]
                    lo = r0 * P
                    act.wait_ge(S["s_ps"], k + 1)
                    if k >= QR:
                        act.wait_ge(S[low_sem(k - QR)], low_count(k - QR))
                    if k >= PR:
                        act.wait_ge(S["pv_done"], k - PR + 1)
                    a.activation(p32[:, k % QR, lo:], ps[:, k % 2, lo:], ACT.Exp)
                    a.activation(phi[:, k % PR, lo:], ps[:, k % 2, lo:], ACT.Exp).then_inc(S["p_ready"], 1)
                    if k + 2 in FIRST:
                        max_row(FIRST.index(k + 2))
                for m in range(B * NQ):
                    j = (k - YAT[m]) / YGAP
                    if j == 1:
                        act.wait_ge(S["oT_ps"], m + 1)
                        a.copy(oT, ps[:, 4, :]).then_inc(S["oT_sb"], 1)
                    if j == 2:
                        act.wait_ge(S["y_ps"], m + 1)
                        if m:
                            act.wait_ge(S["ylo_ready"], m)
                        a.copy(y32, ps[:, 4, :])
                        a.copy(yhi[:, m * CH:(m + 1) * CH], ps[:, 4, :]).then_inc(S["yhi_ready"], 1)
                    if j == 3:
                        act.wait_ge(S["lg_ready"], m + 1)
                        a.activation(gt[:, 1], gt[:, 0], ACT.Exp).then_inc(S["eg_ready"], 1)
                    if j == 4:
                        act.wait_ge(S["gT_ps"], m + 1)
                        a.copy(gT[:], ps[0:E, 4, :]).then_inc(S["gT_sb"], 1)

            a.preload_act_table(ACT.Gelu_apprx_tanh)
            with act.Fori(0, NEXP) as n:
                for f in range(FT):
                    act.wait_ge(S["hid_ps"], n * FT + f + 1)
                    act.wait_ge(S["hlo_even" if f % 2 == 0 else "hlo_odd"], 2 * n + f // 2 + 1)
                    a.activation(hid[:, f], ps[:, HBANK[f], :], ACT.Gelu_apprx_tanh,
                                 bias=col[:, ds(K_B1 + (n % E) * FT + f, 1)], scale=1.0 / WS
                                 ).then_inc(S["hid_ready"], 1)

        @block.vector
        def _(dve):
            v = nc.vector

            for i, (name, size) in enumerate([("hid_ready", RING), ("w2_done", RING), ("hlo_even", 2), ("hlo_odd", 2),
                                              ("eo_used", 8), ("qkn_ready", 1), ("lo_ready", 1), ("vlo_ready", 1),
                                              ("split_done", 2)]):
                v.memset(credit[:, i:i + 1], 0.0).then_inc(S[name], size)
            v.memset(kh1[DS:DS + 1, :, :], 1.0).then_inc(S["pos_ready"], 1)
            dve.wait_ge(S["load_w"], 80)
            v.tensor_scalar(qkg8[:], col[:, K_QG:K_QG + 1], float(DS) ** 0.5, None, ALU.mult).then_inc(S["pos_ready"], 1)
            v.tensor_tensor(pos, pos, row[:, R_TB:R_TB + D].unsqueeze(1).to_broadcast([P, NT, D]),
                            ALU.add).then_inc(S["pos_ready"], 1)
            dve.wait_ge(S["pos_ready"], 3)

            def embed(c, par):
                h = h_all[:, ds(2 * c, 2), :]
                v.tensor_tensor(h, h, cst[:, ds(C_POS + c * D, D)].unsqueeze(1).to_broadcast([P, B, D]),
                                ALU.add).then_inc(S["front_link"], 1)
                dve.wait_ge(S["front_link"], 2 * c + 1)
                v.memset(credit[:, 13:14], 0.0)
                for b in range(B):
                    last = v.bn_stats(st6[:, b], h_all[:, ds(2 * c + b, 1), :].rearrange("p a d -> p (a d)"))
                last.then_inc(S["front_link"], 1)
                dve.wait_ge(S["front_link"], 2 * c + 2)
                v.memset(credit[:, 13:14], 0.0)
                for b in range(B):
                    last = v.bn_aggr(mv[par][:, b], st6[:, b])
                last.then_inc(S["stats"], 1)

            def normed(c, par):
                dve.wait_ge(S["rstd"], c + 1)
                dve.wait_ge(S["stats"], c + 1)
                for b in range(B):
                    last = v.tensor_scalar(xn[par][:, b], h_all[:, ds(2 * c + b, 1), :].rearrange("p a d -> p (a d)"),
                                           mv[par][:, b, 0:1], rs[par][:, b:b + 1], ALU.subtract, ALU.mult)
                last.then_inc(S["xn_ready"], 1)

            def state_out(c):
                dve.wait_ge(S["state_ps"], 2 * c + B)
                for b in range(B):
                    v.tensor_tensor(sg[:, b], ps[:, 7, b * 2 * D:(b + 1) * 2 * D].rearrange("p (a d) -> p a d", d=D),
                                    blk.unsqueeze(1).to_broadcast([P, 2, D]), ALU.mult).then_inc(S["sg_ready"], 1)

            def h1_out(c, par):
                dve.wait_ge(S["pr_ps"], c + 1)
                dve.wait_ge(S["hb_ready"], c + 1)
                v.tensor_tensor(h_all[:, ds(2 * c, 2), :], ps[:, 0, B * P:].rearrange("p (b d) -> p b d", b=B),
                                hb[par], ALU.add).then_inc(S["h1_ready"], 1)

            dve.wait_ge(S["gathered0"], 16 * B)
            embed(0, 0)
            normed(0, 0)
            dve.wait_ge(S["gathered1"], 16 * (8 - B))
            embed(1, 1)
            dve.wait_ge(S["xnT_sb"], 1)
            v.tensor_reduce(x0[:], xnT[0], AX, ALU.add
                            ).then_inc(S["x0_link"], 1)
            dve.wait_ge(S["x0_link"], 1)
            v.tensor_scalar(x0[:], x0[:], 1.0 / P, None, ALU.mult).then_inc(S["x0_link"], 1)
            normed(1, 1)
            links = 0

            def link(ins):
                nonlocal links
                links += 1
                ins.then_inc(S["direct_link"], 1)
                dve.wait_ge(S["direct_link"], links)

            low_h = lower.unsqueeze(1).to_broadcast([P, HA, P])
            inv0 = cst[:, C_INV:C_INV + 1]
            for b in range(B):
                dve.wait_ge(S["dt_ps"], b + 1)
                v.tensor_tensor(dtm[:, b], ps[:, 3:5, :].rearrange("p z (h j) -> p (z h) j", j=P), low_h,
                                ALU.mult).then_inc(S["dt_sb"], 1)
            for b in range(B):
                dve.wait_ge(S["dt_sb"], b + 1)
                link(v.tensor_reduce(sm[:, 1, b], dtm[:, b], AX, ALU.add))
                link(v.tensor_scalar(sm[:, 0, b], sm[:, 1, b], inv0, None, ALU.mult))
                link(v.tensor_tensor(sq[:, b], dtm[:, b], sm[:, 0, b].unsqueeze(2).to_broadcast([P, HA, P]), ALU.subtract))
                v.tensor_tensor(dtm[:, b], sq[:, b], low_h, ALU.mult).then_inc(S["attn0"], 1)
                dve.wait_ge(S["attn0"], b + 1)
                v.tensor_tensor(sq[:, b], dtm[:, b], dtm[:, b], ALU.mult).then_inc(S["sq_ready"], 1)
                dve.wait_ge(S["sq_ready"], b + 1)
                link(v.tensor_reduce(sm[:, 1, b], sq[:, b], AX, ALU.add))
            v.tensor_scalar(sm[:, 3], sm[:, 1], inv0, DOT_EPS, ALU.mult, ALU.add).then_inc(S["var_ready"], 1)
            state_out(0)

            def outputs(c, cur, first=False):
                dve.wait_ge(S["coef"], c + 1)
                if first:
                    dve.wait_ge(S["x_sb"], 1)
                shift = row[:, R_NB:R_NB + HA].unsqueeze(1).to_broadcast([P, B, HA]) if first else sm[:, 7]
                v.tensor_tensor(ao.rearrange("p b (h e) -> p b h e", e=DA),
                                xall[cur][:, :, 3, :].rearrange("p b (h e) -> p b h e", e=DA),
                                sm[:, 5].unsqueeze(3).to_broadcast([P, B, HA, DA]), ALU.mult)
                v.tensor_tensor(ao2.rearrange("p b (h e) -> p b h e", e=DA),
                                xall[cur][:, :, 1, :].rearrange("p b (h e) -> p b h e", e=DA),
                                shift.unsqueeze(3).to_broadcast([P, B, HA, DA]), ALU.mult
                                ).then_inc(S["ao_link"], 1)
                dve.wait_ge(S["ao_link"], c + 1)
                v.tensor_tensor(ao, ao, ao2, ALU.add).then_inc(S["ao_ready"], 1)

            def variances(c, cur):
                k = 4 * (c - 1)
                dve.wait_ge(S["x_sb"], c + 1)
                q = qkv[cur][:, :, 0, :]
                v.tensor_tensor(prod, xall[cur].rearrange("p b (a z) d -> p b a z d", z=2)[:, :, :, 0, :],
                                q.unsqueeze(2).to_broadcast([P, B, 2, D]), ALU.mult).then_inc(S["core_link"], 1)
                dve.wait_ge(S["core_link"], k + 1)
                v.tensor_reduce(ab[:].rearrange("p b a h -> p (b a h)"),
                                prod.rearrange("p b a (h e) -> p (b a h) e", e=DA), AX, ALU.add
                                ).then_inc(S["core_link"], 1)
                dve.wait_ge(S["core_link"], k + 2)
                inv = cst[:, ds(C_INV + c, 1)]
                v.tensor_scalar(sm[:, 0], ab[:, :, 0], inv, None, ALU.mult).then_inc(S["core_link"], 1)
                dve.wait_ge(S["core_link"], k + 3)
                v.tensor_tensor(sm[:, 2], sm[:, 0], sm[:, 0], ALU.mult).then_inc(S["core_link"], 1)
                dve.wait_ge(S["core_link"], k + 4)
                v.scalar_tensor_tensor(sm[:, 1], ab[:, :, 1], inv, sm[:, 2], ALU.mult, ALU.subtract
                                       ).then_inc(S["v_link"], 1)
                dve.wait_ge(S["v_link"], c)
                v.tensor_scalar(sm[:, 3], sm[:, 1], 0.0, DOT_EPS, ALU.max, ALU.add).then_inc(S["var_ready"], 1)

            def step_a(c, nxt, more=2, first=False):
                cur = 1 - nxt
                for b in range(B):
                    if b:
                        if more:
                            normed(c + 1, nxt)
                        if not first:
                            variances(c - 1, nxt)
                        if more >= 2:
                            embed(c + 2, cur)
                    dve.wait_ge(S["dt_ps"], 2 * c + b + 1)
                    dve.wait_ge(S["x_ps"], 2 * c + b - 1)
                    v.tensor_tensor(dtm[:, b], ps[:, 3:5, :].rearrange("p z (h j) -> p (z h) j", j=P),
                                    upper.unsqueeze(1).to_broadcast([P, HA, P]), ALU.mult).then_inc(S["dt_sb"], 1)
                state_out(c)
                outputs(c - 1, nxt, first)
                h1_out(c - 1, nxt)

            embed(2, 0)
            step_a(1, 0, first=True)
            dve.wait_ge(S["gathered"], 16 * (T - 8))
            with dve.Fori(2, NT - 3, 2) as c:
                for u in range(2):
                    step_a(c + u, 1 - u)
            step_a(NT - 2, 1, more=1)
            step_a(NT - 1, 0, more=0)

            def stats2(c, par):
                for b in range(B):
                    last = v.bn_stats(st2[:, par, b], h_all[:, ds(2 * c + b, 1), :].rearrange("p a d -> p (a d)"))
                last.then_inc(S["st2_link"], 1)
                dve.wait_ge(S["st2_link"], c + 1)
                v.memset(credit[:, 13:14], 0.0)
                for b in range(B):
                    last = v.bn_aggr(mv2[par][:, b], st2[:, par, b])
                last.then_inc(S["stats2"], 1)

            def normed2(c, par):
                dve.wait_ge(S["rr_ready"], c + 1)
                for b in range(B):
                    last = v.tensor_scalar(x2[par][:, b], h_all[:, ds(2 * c + b, 1), :].rearrange("p a d -> p (a d)"),
                                           mv2[par][:, b, 0:1], rr[par][:, 3, b:b + 1], ALU.subtract, ALU.mult)
                last.then_inc(S["x2_ready"], 1)

            def sum_squares(c, par):
                dve.wait_ge(S["sqqk"], c + 1)
                v.tensor_reduce(ss[:, par, 0], qk2[:].rearrange("p b (g e) -> p (b g) e", e=DS), AX, ALU.add
                                ).then_inc(S["ss_ready"], 1)

            def low_v(c, par):
                dve.wait_ge(S["vhi_ready"], c + 1)
                v.tensor_tensor(v16[:, ds(2 * c, B), :, DS + 1:],
                                ps[:, QB[par]:QB[par] + B, 2 * D:3 * D].rearrange("p b (h e) -> p b h e", h=HS),
                                v16[:, ds(2 * c, B), :, 0:DS], ALU.subtract).then_inc(S["vlo_ready"], 1)

            def unit_qk(c, par):
                dve.wait_ge(S["rn_ready"], c + 1)
                for b in range(B):
                    v.tensor_tensor(qkn[:, b], ps[:, QB[par] + b, 0:2 * D].rearrange("p (g e) -> p g e", e=DS)
                                    .unsqueeze(2).to_broadcast([P, 4, 2, DS]),
                                    ss[:, par, 2, 4 * b:4 * b + 4].unsqueeze(2).unsqueeze(3)
                                    .to_broadcast([P, 4, 2, DS]), ALU.mult).then_inc(S["qkn_ready"], 1)

            def low_qk(c):
                for b in range(B):
                    at = ds(b * N + c * P, P)
                    dve.wait_ge(S["hi_ready"], 2 * c + b + 1)
                    v.scalar_tensor_tensor(ql[0:DS, :, at], ps[0:DS, 3 + b, 0:2 * P].rearrange("p (h t) -> p h t", h=HS),
                                           qkg8[0:DS], qhh[0:DS, :, at], ALU.mult, ALU.subtract)
                    v.scalar_tensor_tensor(khl[DS:, :, at], ps[DS:, 3 + b, 2 * P:].rearrange("p (h t) -> p h t", h=HS),
                                           col[DS:, K_KG:K_KG + 1], khl[DS:, :, at], ALU.mult, ALU.subtract
                                           ).then_inc(S["lo_ready"], 1)

            dve.wait_ge(S["h1_ready"], NT - 1)
            stats2(0, 0)
            variances(NT - 1, 1)
            stats2(1, 1)
            normed2(0, 0)
            outputs(NT - 1, 1)
            h1_out(NT - 1, 1)
            dve.wait_ge(S["h1_ready"], NT)
            stats2(2, 0)
            normed2(1, 1)
            sum_squares(0, 0)
            low_v(0, 0)

            def step_a2(c, par, left=3):
                unit_qk(c, par)
                if left >= 2:
                    normed2(c + 2, par)
                if left >= 1:
                    sum_squares(c + 1, 1 - par)
                if left >= 3:
                    stats2(c + 3, 1 - par)
                low_qk(c)
                if left >= 1:
                    low_v(c + 1, 1 - par)

            with dve.Fori(0, NT - 5, 2) as c:
                for u in range(2):
                    step_a2(c + u, u)
            for c in range(NT - 4, NT):
                step_a2(c, c % 2, NT - 1 - c)

            def row_max(it, part):
                r, kb, w, k = part
                dve.wait_ge(S["sm_ps"], k + 1)
                v.tensor_reduce(mx[:, r, kb:kb + 1], ps[:, MB[k % 3], 0:w], AX, ALU.max).then_inc(S["sm_used"], 1)
                c, _, h = ITEMS[it]
                if (r, kb) == (3, c):
                    dve.wait_ge(S["sm_used"], k + 1)
                    v.tensor_reduce(mall[:], mx[:, :, 0:c + 1], AX, ALU.max).then_inc(S["max_link"], 1)
                    dve.wait_ge(S["max_link"], it + 1)
                    if it >= HS:
                        dve.wait_ge(S["mrow_ps"], it - 1)
                    v.tensor_scalar(mpad[:, h, :, DS], mall[:], -1.0, None, ALU.mult).then_inc(S["mneg"], 1)

            def head_out(it):
                c, b, h = ITEMS[it]
                m = it // HS
                dve.wait_ge(S["pv_done"], (FIRST + [NSTEP])[it + 1])
                if h == 0 and m:
                    dve.wait_ge(S["oT_ps"], m)
                o = ps[:, 6 + it % 2, 0:4 * (DS + 1)].rearrange("p (r e) -> p r e", r=4)
                v.reciprocal(rl[:], o[:, :, DS]).then_inc(S["o_link"], 1)
                dve.wait_ge(S["o_link"], it + 1)
                v.tensor_tensor(och[:, :, h * DS:(h + 1) * DS], o[:, :, 0:DS],
                                rl[:].unsqueeze(2).to_broadcast([P, 4, DS]), ALU.mult).then_inc(S["o_used"], 1)

            for part in MPARTS[0]:
                row_max(0, part)
            for k in range(NSTEP + LAG + 5 * YGAP + 3):
                for it, part in MSLOT.get(k, ()):
                    row_max(it, part)
                if k < NSTEP and not on_pool(k):
                    lo = STEPS[k][2] * P
                    dve.wait_ge(S["p_ready"], k + 1)
                    if k >= PR:
                        dve.wait_ge(S["pv_done"], k - PR + 1)
                    v.tensor_tensor(plo[:, k % PR, lo:], p32[:, k % QR, lo:], phi[:, k % PR, lo:], ALU.subtract
                                    ).then_inc(S["plo_dve"], 1)
                for it in range(len(ITEMS)):
                    if k == OAT[it]:
                        head_out(it)
                for m in range(B * NQ):
                    j = (k - YAT[m]) / YGAP
                    if j == 3:
                        dve.wait_ge(S["lg_ps"], m + 1)
                        v.tensor_tensor(gt[:, 2], ps[:, 4, 0:4 * E].rearrange("p (r e) -> p r e", e=E),
                                        row[:, R_GB:R_GB + E].unsqueeze(1).to_broadcast([P, 4, E]), ALU.add
                                        ).then_inc(S["lg_link"], 1)
                        dve.wait_ge(S["lg_link"], 5 * m + 1)
                        v.tensor_reduce(gl[:, 0], gt[:, 2], AX, ALU.max).then_inc(S["lg_link"], 1)
                        dve.wait_ge(S["lg_link"], 5 * m + 2)
                        v.tensor_tensor(gt[:, 0], gt[:, 2], gl[:, 0].unsqueeze(2).to_broadcast([P, 4, E]), ALU.subtract
                                        ).then_inc(S["lg_ready"], 1)
                    if j == 4:
                        dve.wait_ge(S["eg_ready"], m + 1)
                        v.tensor_reduce(gl[:, 1], gt[:, 1], AX, ALU.add).then_inc(S["lg_link"], 1)
                        dve.wait_ge(S["lg_link"], 5 * m + 3)
                        v.reciprocal(gl[:, 2], gl[:, 1]).then_inc(S["lg_link"], 1)
                        dve.wait_ge(S["lg_link"], 5 * m + 4)
                        if m:
                            dve.wait_ge(S["gT_ps"], m)
                        v.tensor_tensor(gt[:, 3], gt[:, 1], gl[:, 2].unsqueeze(2).to_broadcast([P, 4, E]), ALU.mult
                                        ).then_inc(S["gate_ready"], 1)
                        dve.wait_ge(S["gate_ready"], m + 1)
                        v.tensor_scalar(gs[:, m], gt[:, 3], 1.0 / WS, None, ALU.mult).then_inc(S["lg_link"], 1)
                    if j == 5:
                        dve.wait_ge(S["b2_ps"], m + 1)
                        hc = h_all[:, ds(8 * (m // 2) + m % 2, 4, step=2), :]
                        v.tensor_tensor(hc, ps[:, 4, :].rearrange("p (r d) -> p r d", r=4), hc, ALU.add
                                        ).then_inc(S["h2_ready"], 1)
            dve.wait_ge(S["h2_ready"], B * NQ)
            dve.wait_ge(S["lg_link"], 5 * B * NQ)
            dve.wait_ge(S["split_done"], 2 + NPIECE)

            def high_parts(n, f):
                s = n * FT + f
                dve.wait_ge(S["hid_ready"], s + 1 + RING)
                dve.wait_ge(S["w2_done"], s + 1)
                v.tensor_copy(hhi[:, f], hid[:, f]).then_inc(S["hhi_ready"], 1)
                if f % 2:
                    dve.wait_ge(S["hhi_ready"], s + 1)
                    v.tensor_tensor(hlo[:, f], hid[:, f], hhi[:, f], ALU.subtract).then_inc(S["hlo_odd"], 1)

            def add_expert(n, par):
                dve.wait_ge(S["w2_done"], n * FT + FT + RING)
                dve.wait_ge(S["eo_used"], n * 4 + 8)
                m = n // E
                for r in range(4):
                    hr = h_all[:, ds((m // 2) * 8 + m % 2 + 2 * r, 1), :].rearrange("p a d -> p (a d)")
                    v.scalar_tensor_tensor(hr, ps[:, 2 + par, r * D:(r + 1) * D],
                                           gs[:, ds(m, 1), r, ds(n % E, 1)].rearrange("p a e -> p (a e)"), hr,
                                           ALU.mult, ALU.add).then_inc(S["eo_used"], 1)

            for u in range(2):
                for f in range(FT):
                    high_parts(u, f)
            add_expert(0, 0)
            with dve.Fori(2, NEXP - 1, 2) as n:
                for u in range(2):
                    for f in range(FT):
                        high_parts(n + u, f)
                    add_expert(n + u - 1, 1 - u)
            add_expert(NEXP - 1, 1)

        @block.tensor
        def _(pe):
            t_ = nc.tensor

            def mm(o, l, r, start=True, stop=True):
                return t_.matmul(o, l, r, start=start, stop=stop, skip_group_check=True)

            def xn_T(c, par, first=False):
                pe.wait_ge(S["xn_ready"], c + 1)
                if not first:
                    pe.wait_ge(S["xnT_sb"], c)
                    pe.wait_ge(S["h1_ready"], c - 2)
                for b in range(B):
                    last = t_.transpose(ps[:, 0, b * P:(b + 1) * P], xn[par][:, b], ident)
                last.then_inc(S["xnT_ps"], 1)

            def project(c, par, first=False):
                pe.wait_ge(S["xnT_sb"], c + 1)
                pe.wait_ge(S["xsT_sb"], c + 1)
                if not first:
                    pe.wait_ge(S["qkT_sb"], c)
                mm(ps[:, 1, 0:B * P], wqkv[:, 0], xnT[par].rearrange("p b t -> p (b t)"))
                mm(ps[:, 1, B * P:], wqkv[:, 1], xsT[par].rearrange("p b t -> p (b t)")).then_inc(S["qkT_ps"], 1)

            def project_rows(c, par, b, first=False):
                if not (first and b == 0):
                    pe.wait_ge(S["qkv_sb"], 2 * c + b)
                mm(ps[:, 2, 0:D], xnT[par][:, b], wqkv[:, 0])
                mm(ps[:, 2, 2 * D:3 * D], xnT[par][:, b], wqkv[:, 2])
                mm(ps[:, 2, D:2 * D], xsT[par][:, b], wqkv[:, 1]).then_inc(S["qkv_ps"], 1)

            def out_T(c):
                pe.wait_ge(S["ao_ready"], c + 1)
                for b in range(B):
                    last = t_.transpose(ps[:, 0, (B + b) * P:(B + b + 1) * P], ao[:, b], ident)
                last.then_inc(S["aoT_ps"], 1)

            def out_project(c):
                pe.wait_ge(S["aoT_sb"], c + 1)
                for b in range(B):
                    last = mm(ps[:, 0, (B + b) * P:(B + b + 1) * P], aoT[:, b], wout[:])
                last.then_inc(S["pr_ps"], 1)

            def sums(c, par, b, first=False):
                kv = qkv[par][:, b, 1:3, :].rearrange("p a d -> p (a d)")
                pe.wait_ge(S["qkv_sb"], 2 * c + b + 1)
                if not first:
                    pe.wait_ge(S["x_sb"], c)
                mm(ps[:, 5 + b, 0:2 * D], upper, kv, stop=first)
                if not first:
                    mm(ps[:, 5 + b, 0:2 * D], last_row, xall[1 - par][:, b, 0:2, :].rearrange("p a d -> p (a d)"), start=False)
                    pe.wait_ge(S["sg_ready"], 2 * c)
                    mm(ps[:, 5 + b, 2 * D:], qkT[par][:, 0, b], sg[:, b].rearrange("p a d -> p (a d)"), start=False)
                mm(ps[:, 7, b * 2 * D:(b + 1) * 2 * D], qkv[par][:, b, 1, :], kv, start=(first and b == 0)
                   ).then_inc(S["state_ps"], 1)

            pe.wait_ge(S["load_w"], 80)
            pe.wait_ge(S["setup"], 5)
            xn_T(0, 0, first=True)
            project(0, 0, first=True)
            for b in range(B):
                project_rows(0, 0, b, first=True)
            for b in range(B):
                pe.wait_ge(S["blk_ready"], b + 1)
                if b:
                    pe.wait_ge(S["dt_sb"], b)
                for z in range(2):
                    last = mm(ps[:, 3 + z, :], qkT[0][:, 0, b], blkbuf[:, b].rearrange("p (z h) j -> p z (h j)", z=2)[:, z])
                last.then_inc(S["dt_ps"], 1)
            xn_T(1, 1, first=True)
            for b in range(B):
                sums(0, 0, b, first=True)
            project(1, 1)
            for b in range(B):
                project_rows(1, 1, b)
            pe.wait_ge(S["dt_sb"], B)
            for b in range(B):
                pe.wait_ge(S["attn0"], b + 1)
                if b:
                    pe.wait_ge(S["attnT0_sb"], b)
                for h in range(HA):
                    last = t_.transpose(ps[:, 3 + h // 4, h % 4 * P:(h % 4 + 1) * P], dtm[:, b, h], ident)
                last.then_inc(S["attnT0_ps"], 1)
                pe.wait_ge(S["attnT0_sb"], b + 1)
                for h in range(HA):
                    last = mm(ps[:, 5 + b, 3 * D + h * DA:3 * D + (h + 1) * DA], dtm[:, b, h],
                              qkv[0][:, b, 2, h * DA:(h + 1) * DA], start=False)
                last.then_inc(S["x_ps"], 1)

            def step_a(c, nxt, more=True, first=False):
                cur = 1 - nxt
                for b in range(B):
                    pe.wait_ge(S["blk_ready"], 2 * c + b + 1)
                    pe.wait_ge(S["dt_sb"], 2 * c + b)
                    for z in range(2):
                        last = mm(ps[:, 3 + z, :], qkT[cur][:, 1, b],
                                  blkbuf[:, b].rearrange("p (z h) j -> p z (h j)", z=2)[:, z])
                    last.then_inc(S["dt_ps"], 1)
                    sums(c, cur, b)
                    if more and b == 0:
                        xn_T(c + 1, nxt, first)
                if more:
                    project(c + 1, nxt)
                for b in range(B):
                    if more:
                        project_rows(c + 1, nxt, b)
                    if b:
                        if more:
                            pe.wait_ge(S["xnT_sb"], c + 2)
                        out_T(c - 1)
                    pe.wait_ge(S["dt_sb"], 2 * c + b + 1)
                    o = ps[:, 5 + b, 2 * D:].rearrange("p (a h e) -> p a h e", a=2, e=DA)
                    kv = qkv[cur][:, b, 1:3, :].rearrange("p a (h e) -> p a h e", e=DA)
                    for h in range(HA):
                        last = mm(o[:, :, h, :], dtm[:, b, h], kv[:, :, h, :], start=False)
                    last.then_inc(S["x_ps"], 1)
                out_project(c - 1)

            step_a(1, 0, first=True)
            with pe.Fori(2, NT - 3, 2) as c:
                for u in range(2):
                    step_a(c + u, 1 - u)
            step_a(NT - 2, 1)
            step_a(NT - 1, 0, more=False)

            pe.wait_ge(S["load_s"], 80)

            def normed_T(c, par, first=False):
                pe.wait_ge(S["x2_ready"], c + 1)
                if not first:
                    pe.wait_ge(S["hxT_sb"], c)
                for b in range(B):
                    last = t_.transpose(ps[:, 0, b * P:(b + 1) * P], x2[par][:, b], ident)
                last.then_inc(S["x2T_ps"], 1)

            def project2(c, par, first=False):
                pe.wait_ge(S["hxT_sb"], c + 1)
                if not first:
                    pe.wait_ge(S["qkn_ready"], 2 * c - 1)
                    pe.wait_ge(S["vlo_ready"], c)
                for b in range(B):
                    last = mm(ps[:, QB[par] + b, 0:3 * D], hxT[par][:, b], wsm[:])
                last.then_inc(S["qkv2_ps"], 1)

            def unit_T(c):
                for b in range(B):
                    pe.wait_ge(S["qkn_ready"], 1 + 2 * c + b + 1)
                    pe.wait_ge(S["lo_ready"], 1 + 2 * c)
                    for i in range(4):
                        last = t_.transpose(ps[:, 3 + b, i * P:(i + 1) * P],
                                            qkn[:, b, i].rearrange("p z e -> p (z e)"), ident)
                    last.then_inc(S["qkd_ps"], 1)

            pe.wait_ge(S["h1_ready"], NT - 1)
            normed_T(0, 0, first=True)
            project2(0, 0, first=True)
            out_T(NT - 1)
            out_project(NT - 1)
            pe.wait_ge(S["h1_ready"], NT)
            pe.wait_ge(S["x_sb"], NT)
            normed_T(1, 1)

            def step_a2(c, par, left=3):
                if left >= 1:
                    project2(c + 1, 1 - par)
                unit_T(c)
                if left >= 2:
                    normed_T(c + 2, par)

            with pe.Fori(0, NT - 5, 2) as c:
                for u in range(2):
                    step_a2(c + u, u)
            for c in range(NT - 4, NT):
                step_a2(c, c % 2, NT - 1 - c)

            pe.wait_ge(S["hi_ready"], T)
            pe.wait_ge(S["lo_ready"], 1 + T)
            pe.wait_ge(S["vlo_ready"], 1 + NT)
            bank4 = None

            def max_scores(it, part):
                c, b, h = ITEMS[it]
                r, kb, w, k = part
                q = b * N + c * CH + r * P
                if k >= 3:
                    pe.wait_ge(S["sm_used"], k - 2)
                last = mm(ps[:, MB[k % 3], 0:w], qhh[:, h, q:q + P], khl[:, h, b * N + kb * CH:b * N + kb * CH + w],
                          stop=kb < c)
                if kb == c:
                    last = mm(ps[:, MB[k % 3], w - P:w], ident16, neg_qk, start=False)
                last.then_inc(S["sm_ps"], 1)

            def max_row(it):
                nonlocal bank4
                h = ITEMS[it][2]
                if bank4:
                    pe.wait_ge(*bank4)
                pe.wait_ge(S["mneg"], it + 1)
                for r in range(4):
                    last = mm(ps[0:DS + 1, 4, r * P:(r + 1) * P], mpad[:, h, r], ident16)
                last.then_inc(S["mrow_ps"], 1)
                bank4 = S["mrow_sb"], it + 1

            def scores(k):
                it, kt, r0, diag = STEPS[k]
                c, b, h = ITEMS[it]
                if k in FIRST:
                    pe.wait_ge(S["mrow_sb"], it + 1)
                if k >= 2:
                    pe.wait_ge(S["p_ready"], k - 1)
                lo, at = r0 * P, b * N + kt * P
                q0 = b * N + c * CH
                mm(ps[:, k % 2, lo:], khl[:, h, at:at + P], qhh[:, h, q0 + lo:q0 + CH], stop=False)
                last = mm(ps[:, k % 2, lo:], kh1[:, h, at:at + P], ql[:, h, q0 + lo:q0 + CH], start=False, stop=not diag)
                if diag:
                    last = mm(ps[:, k % 2, lo:lo + P], ident16, neg_kq, start=False)
                last.then_inc(S["s_ps"], 1)

            def values(k):
                it, kt, r0, diag = STEPS[k]
                c, b, h = ITEMS[it]
                first = k in FIRST
                pe.wait_ge(S[low_sem(k)], low_count(k))
                if first and it >= 2:
                    pe.wait_ge(S["o_used"], it - 1)
                vt = v16[:, 2 * kt + b, h, :]
                for r in range(r0, 4):
                    o = ps[:, 6 + it % 2, r * (DS + 1):(r + 1) * (DS + 1)]
                    mm(o, phi[:, k % PR, r * P:(r + 1) * P], vt[:, 0:DS + 1], start=first and r == 0)
                    mm(o[:, 0:DS], phi[:, k % PR, r * P:(r + 1) * P], vt[:, DS + 1:], start=False)
                    last = mm(o, plo[:, k % PR, r * P:(r + 1) * P], vt[:, 0:DS + 1], start=False)
                last.then_inc(S["pv_done"], 1)

            for part in MPARTS[0]:
                max_scores(0, part)
            max_row(0)
            for k in range(NSTEP + LAG + 5 * YGAP + 3):
                if k < NSTEP:
                    scores(k)
                    for it, part in MSLOT.get(k, ()):
                        max_scores(it, part)
                if LAG <= k < NSTEP + LAG:
                    values(k - LAG)
                if k + 2 in FIRST:
                    max_row(FIRST.index(k + 2))
                for m in range(B * NQ):
                    j = (k - YAT[m]) / YGAP
                    if j == 1:
                        pe.wait_ge(*bank4)
                        pe.wait_ge(S["o_used"], 2 * m + 2)
                        for r in range(4):
                            last = t_.transpose(ps[:, 4, r * P:(r + 1) * P], och[:, r], ident)
                        last.then_inc(S["oT_ps"], 1)
                        bank4 = S["oT_sb"], m + 1
                    if j == 2:
                        pe.wait_ge(*bank4)
                        pe.wait_ge(S["oT_sb"], m + 1)
                        mm(ps[:, 4, :], wo[:], oT).then_inc(S["y_ps"], 1)
                        bank4 = S["yhi_ready"], m + 1
                    if j == 3:
                        pe.wait_ge(*bank4)
                        pe.wait_ge(S["yhi_ready"], m + 1)
                        for r in range(4):
                            last = mm(ps[:, 4, r * E:(r + 1) * E], y32[:, r * P:(r + 1) * P], wgate[:])
                        last.then_inc(S["lg_ps"], 1)
                        bank4 = S["lg_ready"], m + 1
                    if j == 4:
                        pe.wait_ge(*bank4)
                        pe.wait_ge(S["gate_ready"], m + 1)
                        for r in range(4):
                            last = t_.transpose(ps[0:E, 4, r * P:(r + 1) * P], gt[:, 3, r], ident)
                        last.then_inc(S["gT_ps"], 1)
                        bank4 = S["gT_sb"], m + 1
                    if j == 5:
                        pe.wait_ge(*bank4)
                        pe.wait_ge(S["gT_sb"], m + 1)
                        for r in range(4):
                            last = mm(ps[:, 4, r * D:(r + 1) * D], gT[:, r * P:(r + 1) * P], b2s[:])
                        last.then_inc(S["b2_ps"], 1)
                        bank4 = S["h2_ready"], m + 1

            pe.wait_ge(S["split_done"], 2 + NPIECE)
            pe.wait_ge(S["ylo_ready"], B * NQ)
            pe.wait_ge(S["h2_ready"], B * NQ)
            pe.wait_ge(S["p_ready"], NSTEP)

            def up(n, f):
                pe.wait_ge(S["hid_ready"], n * FT + f + 1)
                whi, wlo = (w12[:, ds((n % E) * FT + f, 1), z, :].rearrange("p a d -> p (a d)") for z in range(2))
                y = ds((n // E) * CH, CH)
                o = ps[:, HBANK[f], :]
                mm(o, whi, yhi[:, y], stop=False)
                mm(o, whi, ylo[:, y], start=False, stop=False)
                mm(o, wlo, yhi[:, y], start=False).then_inc(S["hid_ps"], 1)

            def down(n, f, par):
                pe.wait_ge(S["hlo_even" if f % 2 == 0 else "hlo_odd"], 2 * n + f // 2 + 1 + 2)
                if f == 0:
                    pe.wait_ge(S["eo_used"], 4 * n + 4)
                wi = E * FT + (n % E) * FT + f
                for r in range(4):
                    o = ps[:, 2 + par, r * D:(r + 1) * D]
                    hi, lo = hhi[:, f, r * P:(r + 1) * P], hlo[:, f, r * P:(r + 1) * P]
                    whi, wlo = (w12[:, ds(wi, 1), z, :].rearrange("p a d -> p (a d)") for z in range(2))
                    mm(o, hi, whi, start=(f == 0 and r == 0), stop=False)
                    mm(o, hi, wlo, start=False, stop=False)
                    last = mm(o, lo, whi, start=False, stop=f == FT - 1)
                last.then_inc(S["w2_done"], 1)

            def expert(n, par, more=True):
                for f in range(FT):
                    if f == 0:
                        up(n, FT - 1)
                    elif more:
                        up(n + 1, f - 1)
                    down(n, f, par)

            for f in range(FT - 1):
                up(0, f)
            with pe.Fori(0, NEXP - 3, 2) as n:
                for u in range(2):
                    expert(n + u, u)
            expert(NEXP - 2, 0)
            expert(NEXP - 1, 1, more=False)


def plan():
    items = [(c, b, h) for c in range(NQ) for b in range(B) for h in range(HS)]
    steps, first, mparts, mslot = [], [], [], {}
    k = 0
    for c, b, h in items:
        blocks = [(r, kb, CH if kb < c else (r + 1) * P) for kb in range(c + 1) for r in range(4)]
        mparts.append([(r, kb, w, k + i) for i, (r, kb, w) in enumerate(blocks)])
        k += len(blocks)
    for it, (c, b, h) in enumerate(items):
        first.append(len(steps))
        steps += [(it, 4 * c + d, d, True) for d in range(4)] + [(it, kt, 0, False) for kt in range(4 * c)]
        if it + 1 < len(items):
            span = 4 * c + 4 - 2
            for i, part in enumerate(mparts[it + 1]):
                mslot.setdefault(first[it] + i * span // len(mparts[it + 1]), []).append((it + 1, part))
    ends = first[1:] + [len(steps)]
    o_at = [e - 1 + LAG for e in ends]
    y_at = [o_at[it] for it in range(1, len(items), 2)]
    return items, steps, first, mparts, mslot, o_at, y_at


PR, QR = 5, 4
LAG = 3
YGAP = 3
ITEMS, STEPS, FIRST, MPARTS, MSLOT, OAT, YAT = plan()
NSTEP = len(STEPS)


def on_pool(k):
    return k % 4 != 3


def low_sem(k):
    return "plo_pool" if on_pool(k) else "plo_dve"


def low_count(k):
    return sum(on_pool(i) == on_pool(k) for i in range(k + 1))


def constants():
    c = np.zeros((P, C_END), np.float32)
    i = np.arange(P)
    c[:, C_ID:C_ID + P] = np.eye(P)
    c[:, C_U:C_U + P] = i[:, None] <= i[None, :]
    c[:, C_L:C_L + P] = i[:, None] >= i[None, :]
    c[P - 1, C_LAST:C_LAST + P] = 1.0
    c[:, C_BLK:C_BLK + P] = i[:, None] // DA == i[None, :] // DA
    c[:, C_HEAD:C_HEAD + HA] = i[:, None] // DA == np.arange(HA)[None, :]
    where = np.arange(NT)[None, :] * P + i[:, None] + 1
    c[:, C_INV:C_INV + NT] = 1.0 / where
    place = np.arange(1, N + 1, dtype=np.float32)[:, None]
    k = np.arange(D)
    exponent = (np.where(k % 2 == 0, k, k + 1).astype(np.float32) / np.float32(D)).astype(np.float32)
    angle = (place / np.power(np.float32(10000.0), exponent)).astype(np.float32)
    pe = np.where(k % 2 == 0, np.cos(angle), np.sin(angle)).astype(np.float32)
    c[:, C_POS:C_END] = pe.reshape(NT, P, D).transpose(1, 0, 2).reshape(P, NT * D)
    c16 = np.zeros((P, 3 * P), np.float16)
    c16[:, 0:P] = np.eye(P)
    c16[:, P:2 * P] = np.where(i[None, :] > i[:, None], NEG, 0.0)
    c16[:, 2 * P:] = np.where(i[:, None] > i[None, :], NEG, 0.0)
    return c, c16


def kernel(**inputs):
    import concourse.bacc as _bacc
    from concourse import mybir as _mybir
    from concourse.bass_utils import run_bass_kernel_spmd as _run

    a = {k: np.asarray(v) for k, v in inputs.items()}
    c, c16 = constants()
    rows = np.concatenate([a["L0_tok_b"], a["L0_attn_b_out"], a["L0_ffn_gate_b"],
                           a["L0_attn_norm_g"].reshape(-1), a["L0_attn_norm_b"].reshape(-1)])
    cols = np.concatenate([a["L0_ffn_ln_g"][:, None], a["L0_ffn_ln_b"][:, None],
                           np.tile(a["L0_ffn_qn_g"], 2)[:, None], np.tile(a["L0_ffn_kn_g"], 2)[:, None],
                           a["L0_ffn_b1"].reshape(E * FT, P).T], axis=1)
    arrays = {
        "ids": a["x"].reshape(B, NT, P).transpose(2, 1, 0).reshape(P, T),
        "emb_rows": a["L0_tok_W"].T,
        "consts": c, "consts16": c16,
        "rows": np.broadcast_to(rows[None, :], (P, R_END)),
        "cols": cols,
        "w_qkv": a["L0_attn_w_qkv"], "w_out": a["L0_attn_w_out"],
        "w_sm": np.concatenate([a["L0_ffn_Wq"], a["L0_ffn_Wk"], a["L0_ffn_Wv"]], axis=1),
        "w_o": a["L0_ffn_Wo"], "w_gate": a["L0_ffn_gate_W"],
        "w12_rows": np.concatenate([a["L0_ffn_W1"].transpose(1, 0, 2).reshape(D, E * FF),
                                    a["L0_ffn_W2"].reshape(E * FT, P, D).transpose(1, 0, 2).reshape(P, E * FT * D)],
                                   axis=1),
        "b2": a["L0_ffn_b2"],
    }
    arrays = {k: np.ascontiguousarray(v) for k, v in arrays.items()}
    nc = _bacc.Bacc("TRN2", target_bir_lowering=False, num_devices=1)
    args = [nc.dram_tensor(k, v.shape, _mybir.dt.from_np(v.dtype), kind="ExternalInput").ap()
            for k, v in arrays.items()]
    args.append(nc.dram_tensor("out", (B * N, D), F32, kind="ExternalOutput").ap())
    tower(nc, *args)
    r = _run(nc, [arrays], core_ids=[0])
    return r.results[0]["out"].reshape(B, N, D)
```
